# Optimizing a Trainium2 kernel written in Bass

```python
import numpy as np
import jax
import jax.numpy as jnp

def _softmax(x, axis=-1):
    return jax.nn.softmax(x, axis=axis)

def _gelu(x):
    return jax.nn.gelu(x, approximate=True)

def _silu(x):
    return jax.nn.silu(x)

def _sigmoid(x):
    return jax.nn.sigmoid(x)

def _layernorm(x, axis=-1, eps=1e-05):
    m = jnp.mean(x, axis=axis, keepdims=True)
    v = jnp.var(x, axis=axis, keepdims=True)
    return (x - m) / jnp.sqrt(v + eps)

def _scatter_add(tgt, idx, src, axis=0):
    return tgt.at[idx].add(src)

def _segment_sum(src, seg, n):
    return jax.ops.segment_sum(src, seg, n)
kernel_name = 'mk_adaln_d1_jaxref_r4_ec6521'

def setup_inputs(seed: int=0):
    np.random.seed(seed)
    _w = jnp.asarray

    def _L0_attn_setup():
        import math
        import jax, jax.numpy as jnp
        import numpy as np
        H, G = (16, 4)

        def alibi_bias(S, n_heads, dtype):
            n = 2 ** int(math.floor(math.log2(n_heads)))
            m0 = 2.0 ** (-8.0 / n)
            slopes = m0 ** np.arange(1, n + 1)
            if n < n_heads:
                m1 = 2.0 ** (-4.0 / n)
                slopes = np.concatenate([slopes, m1 ** np.arange(1, 1 + 2 * (n_heads - n), 2)])
            i = jnp.arange(S)[:, None]
            j = jnp.arange(S)[None, :]
            dist = jnp.sqrt(jnp.maximum(i - j, 0).astype(dtype))
            bias = -jnp.asarray(slopes, dtype)[:, None, None] * dist[None]
            return jnp.where((j <= i)[None], bias, jnp.asarray(-jnp.inf, dtype))
        key = jax.random.key(seed)
        ks = jax.random.split(key, 5)
        B, S, Hd = (2, 512, 512)
        D = Hd // H
        return {'x': jax.random.normal(ks[0], (B, S, Hd), jnp.float32), 'Wq': jax.random.normal(ks[1], (Hd, Hd), jnp.float32) * 0.02, 'Wk': jax.random.normal(ks[2], (G * D, Hd), jnp.float32) * 0.02, 'Wv': jax.random.normal(ks[3], (G * D, Hd), jnp.float32) * 0.02, 'Wo': jax.random.normal(ks[4], (Hd, Hd), jnp.float32) * 0.02}
    _L0_attn_in = _L0_attn_setup()

    def _L0_ffn_setup():
        import jax, jax.numpy as jnp
        import numpy as np
        E, TOP_K, D, H = (8, 2, 512, 352)
        B, S = (2, 512)
        key = jax.random.key(seed)
        ks = jax.random.split(key, 8)
        x = jax.random.normal(ks[0], (B, S, D), dtype=jnp.float32)
        gate_w = jax.random.normal(ks[1], (E, D), dtype=jnp.float32) * (1.0 / np.sqrt(D))
        gate_b = jax.random.normal(ks[2], (E,), dtype=jnp.float32) * 0.01
        bias = jnp.zeros((E,), dtype=jnp.float32)
        w1 = jax.random.normal(ks[3], (E, H, D), dtype=jnp.float32) * (1.0 / np.sqrt(D))
        b1 = jax.random.normal(ks[4], (E, H), dtype=jnp.float32) * 0.01
        w2 = jax.random.normal(ks[5], (E, D, H), dtype=jnp.float32) * (1.0 / np.sqrt(H))
        b2 = jax.random.normal(ks[6], (E, D), dtype=jnp.float32) * 0.01
        return {'x': x, 'gate_w': gate_w, 'gate_b': gate_b, 'bias': bias, 'w1': w1, 'b1': b1, 'w2': w2, 'b2': b2}
    _L0_ffn_in = _L0_ffn_setup()
    _L0_c = _w((lambda *s: np.random.randn(*s).astype(np.float32) * 0.05)(2, 512))
    _L0_wmod = _w((lambda *s: np.random.randn(*s).astype(np.float32) * 0.05)(512, 6 * 512) * 512 ** (-0.5))
    _d = {'L0_attn_x': _L0_attn_in['x'], 'L0_attn_Wq': _L0_attn_in['Wq'], 'L0_attn_Wk': _L0_attn_in['Wk'], 'L0_attn_Wv': _L0_attn_in['Wv'], 'L0_attn_Wo': _L0_attn_in['Wo'], 'L0_ffn_gate_w': _L0_ffn_in['gate_w'], 'L0_ffn_gate_b': _L0_ffn_in['gate_b'], 'L0_ffn_bias': _L0_ffn_in['bias'], 'L0_ffn_w1': _L0_ffn_in['w1'], 'L0_ffn_b1': _L0_ffn_in['b1'], 'L0_ffn_w2': _L0_ffn_in['w2'], 'L0_ffn_b2': _L0_ffn_in['b2'], 'L0_c': _L0_c, 'L0_wmod': _L0_wmod}
    _x0 = _d['L0_attn_x']
    _d['L0_attn_x'] = jax.random.normal(jax.random.fold_in(jax.random.key(seed), 1), (2, 2048, 512), dtype=_x0.dtype)
    del _x0
    return _d

def reference(L0_attn_x, L0_attn_Wq, L0_attn_Wk, L0_attn_Wv, L0_attn_Wo, L0_ffn_gate_w, L0_ffn_gate_b, L0_ffn_bias, L0_ffn_w1, L0_ffn_b1, L0_ffn_w2, L0_ffn_b2, L0_c, L0_wmod):

    def _L0_attn_ref(x, Wq, Wk, Wv, Wo):
        import math
        import jax, jax.numpy as jnp
        import numpy as np
        H, G = (16, 4)

        def alibi_bias(S, n_heads, dtype):
            n = 2 ** int(math.floor(math.log2(n_heads)))
            m0 = 2.0 ** (-8.0 / n)
            slopes = m0 ** np.arange(1, n + 1)
            if n < n_heads:
                m1 = 2.0 ** (-4.0 / n)
                slopes = np.concatenate([slopes, m1 ** np.arange(1, 1 + 2 * (n_heads - n), 2)])
            i = jnp.arange(S)[:, None]
            j = jnp.arange(S)[None, :]
            dist = jnp.sqrt(jnp.maximum(i - j, 0).astype(dtype))
            bias = -jnp.asarray(slopes, dtype)[:, None, None] * dist[None]
            return jnp.where((j <= i)[None], bias, jnp.asarray(-jnp.inf, dtype))
        B, S, Hd = x.shape
        D = Hd // H
        rep = H // G
        q = (x @ Wq.T).reshape(B, S, G, rep, D)
        k = (x @ Wk.T).reshape(B, S, G, D)
        v = (x @ Wv.T).reshape(B, S, G, D)
        scale = 1.0 / math.sqrt(D)
        bias = alibi_bias(S, H, x.dtype).reshape(G, rep, S, S)
        scores = jnp.einsum('bqgrd,bkgd->bgrqk', q, k) * scale + bias
        attn = jax.nn.softmax(scores, axis=-1)
        o = jnp.einsum('bgrqk,bkgd->bqgrd', attn, v).reshape(B, S, Hd)
        return o @ Wo.T

    def _L0_ffn_ref(x, gate_w, gate_b, bias, w1, b1, w2, b2):
        import jax, jax.numpy as jnp
        import numpy as np
        E, TOP_K, D, H = (8, 2, 512, 352)
        B, S = (2, 512)
        b, s, d = x.shape
        xf = x.reshape(-1, d)
        scores = xf @ gate_w.T + gate_b + bias
        top_scores, top_idx = jax.lax.top_k(scores, TOP_K)
        gates = jax.nn.softmax(top_scores, axis=-1)
        comb = jnp.sum(jax.nn.one_hot(top_idx, E, dtype=gates.dtype) * gates[..., None], axis=1)
        h = jax.nn.silu(jnp.einsum('td,ehd->teh', xf, w1) + b1)
        y = jnp.einsum('teh,edh->ted', h, w2) + b2
        out = jnp.einsum('ted,te->td', y, comb)
        return out.reshape(b, s, d)
    x = L0_attn_x
    mod = (_silu(L0_c) @ L0_wmod).reshape(L0_c.shape[0], 6, 1, -1)
    sa, ca, ga, sb, cb, gb = (mod[:, 0], mod[:, 1], mod[:, 2], mod[:, 3], mod[:, 4], mod[:, 5])
    ga = (2 * (ga >= 0) - 1) * jnp.maximum(jnp.abs(ga), 0.25)
    gb = (2 * (gb >= 0) - 1) * jnp.maximum(jnp.abs(gb), 0.25)
    h = _layernorm(x, axis=-1) * (1 + ca) + sa
    x = x + ga * _L0_attn_ref(h, L0_attn_Wq, L0_attn_Wk, L0_attn_Wv, L0_attn_Wo)
    h = _layernorm(x, axis=-1) * (1 + cb) + sb
    x = x + gb * _L0_ffn_ref(h, L0_ffn_gate_w, L0_ffn_gate_b, L0_ffn_bias, L0_ffn_w1, L0_ffn_b1, L0_ffn_w2, L0_ffn_b2)
    return x

_drawn_inputs = setup_inputs


def setup_inputs(seed=0):
    import zlib

    import numpy as np

    out = dict(_drawn_inputs(seed))
    spreads = {'L0_ffn_bias': (0.0, 0.603)}
    factors = {'L0_attn_Wq': 8.0,
     'L0_attn_Wk': 8.0,
     'L0_attn_Wv': 7.313,
     'L0_attn_Wo': 7.091,
     'L0_ffn_gate_b': 55.0,
     'L0_ffn_b1': 64.0,
     'L0_ffn_b2': 64.0}
    for name, (base, spread) in spreads.items():
        noise = np.random.default_rng([zlib.crc32(name.encode()), seed]).standard_normal(out[name].shape)
        drawn = base * np.exp(spread * noise) if base else spread * noise
        out[name] = jnp.asarray(drawn.astype(out[name].dtype))
    for name, factor in factors.items():
        out[name] = (out[name] * factor).astype(out[name].dtype)
    return out
```

```python
from contextlib import ExitStack

import numpy as np

import concourse.bass as bass
from concourse import mybir

F32 = mybir.dt.float32
F32R = mybir.dt.float32r
I32 = mybir.dt.int32
U32 = mybir.dt.uint32
ALU = mybir.AluOpType
ACT = mybir.ActivationFunctionType
AX = mybir.AxisListType

P = 128
B, S, DM = 2, 2048, 512
H, G, D = 16, 4, 32
REP = H // G
C = DM // P
NB = S // P
NT = B * NB
SUP = 4
WIDE = SUP * P
UNITS = B * G
EPS = 1e-5
QSCALE = -1.0 / float(np.sqrt(D))
SA, CA, GA, SB, CB, GB = range(6)

E, HF = 8, 352
HC = [(0, 128), (128, 128), (256, 96)]
ROUTES = 2 * NT * P
ST = ROUTES // P + E
ROWS = ST * P


def apart(engine, sem):
    engine.sem_inc(sem, 1)


class Mem:

    def __init__(self, nc, ctx):
        self.nc, self.ctx, self.sems = nc, ctx, []
        ctx.callback(self.close)
        self.passed = self.sem(f"passed{nc.next_id()}")

    def sb(self, name, shape, dt=F32):
        return self.ctx.enter_context(self.nc.sbuf_tensor(name, shape, dt))

    def ps(self, name, shape):
        return self.ctx.enter_context(self.nc.psum_tensor(name, shape, F32))

    def sem(self, name):
        self.sems.append(self.nc.alloc_semaphore(name))
        return self.sems[-1]

    def close(self):
        self.nc.clear_and_free_semaphores(self.sems)
        self.nc.all_engine_barrier()


class LayerNorm:

    def __init__(self, m, name, size):
        self.size = size
        self.stats = m.sb(name + "_stats", [P, size, 6])
        self.mean = m.sb(name + "_mean", [P, size, 2])
        self.var = m.sb(name + "_var", [P, size])
        self.std = m.sb(name + "_std", [P, size])
        self.rstd = m.sb(name + "_rstd", [P, size])
        self.inv = m.sb(name + "_inv", [P, size])
        self.new = m.sb(name + "_new", [P, size])
        self.passed = m.passed
        self.bn_done = m.sem(name + "_bn_done")
        self.mean_done = m.sem(name + "_mean_done")
        self.var_done = m.sem(name + "_var_done")
        self.root_done = m.sem(name + "_root_done")
        self.newton = m.sem(name + "_newton")

    def statistics(self, nc, src, j):
        nc.vector.bn_stats(self.stats[:, j, :], src).then_inc(self.bn_done, 1)

    def deviation(self, nc, dve, t):
        size = self.size
        dve.wait_ge(self.bn_done, (t + 1) * size)
        apart(dve, self.passed)
        for j in range(size):
            nc.vector.bn_aggr(self.mean[:, j, :], self.stats[:, j, :]).then_inc(self.mean_done, 1)
        dve.wait_ge(self.mean_done, (t + 1) * size)
        nc.vector.tensor_scalar(self.var[:], self.mean[:, :, 1], EPS, None, ALU.add).then_inc(self.var_done, 1)
        dve.wait_ge(self.root_done, t + 1)
        steps = [
            lambda: nc.vector.reciprocal(self.inv[:], self.std[:]),
            lambda: nc.vector.tensor_tensor(self.new[:], self.inv[:], self.inv[:], ALU.mult),
            lambda: nc.vector.tensor_tensor(self.new[:], self.new[:], self.var[:], ALU.mult),
            lambda: nc.vector.tensor_scalar(self.new[:], self.new[:], -0.5, 1.5, ALU.mult, ALU.add),
            lambda: nc.vector.tensor_tensor(self.rstd[:, :], self.new[:], self.inv[:], ALU.mult),
        ]
        for k, step in enumerate(steps):
            step().then_inc(self.newton, 1)
            dve.wait_ge(self.newton, t * len(steps) + k + 1)

    def root(self, nc, act, t):
        act.wait_ge(self.var_done, t + 1)
        nc.scalar.activation(self.std[:], self.var[:], ACT.Sqrt).then_inc(self.root_done, 1)

    def apply(self, nc, out, src, j):
        return nc.vector.tensor_scalar(out, src, self.mean[:, j, 0:1], self.rstd[:, j:j + 1],
                                       ALU.subtract, ALU.mult)


def modulation(nc, c_t, wmod, mod_dram, rows_bc):
    with ExitStack() as ctx:
        m = Mem(nc, ctx)
        ct = m.sb("m_ct", [P, C, B])
        th = m.sb("m_th", [P, C, B])
        act_c = m.sb("m_act", [P, C, B])
        w = m.sb("m_w", [P, C, 6 * DM])
        row = m.sb("m_row", [P, 6, DM])
        mag = m.sb("m_mag", [P, 2, DM])
        sgn = m.sb("m_sgn", [P, 2, DM])
        pm = m.ps("m_pm", [P, 6, DM])
        c_in = m.sem("c_in")
        w_in = [m.sem(f"w_in{k}") for k in range(C)]
        tanh_done = m.sem("tanh_done")
        silu_step = m.sem("silu_step")
        mod_done = m.sem("mod_done")
        row_step = m.sem("row_step")
        rows_done = m.sem("rows_done")
        mod_out = m.sem("mod_out")
        bc_in = m.sem("bc_in")

        with nc.Block() as block:

            @block.sync
            def _(sp):
                sp.dma_start(ct[:], c_t.rearrange("(k p) b -> p k b", p=P)).then_inc(c_in, 16)
                for k in range(C):
                    sp.dma_start(w[:, k, :], wmod[k * P:(k + 1) * P, :]).then_inc(w_in[k], 16)
                sp.wait_ge(rows_done, 6)
                for v in range(6):
                    q = 32 * (v % 4)
                    sp.dma_start(mod_dram[v], row[q:q + B, v, :]).then_inc(mod_out, 16)
                sp.wait_ge(mod_out, 6 * 16)
                for v in range(6):
                    for b in range(B):
                        sp.dma_start(rows_bc[:, b, v, :], mod_dram[v, b, :].partition_broadcast(P)).then_inc(bc_in, 16)
                sp.wait_ge(bc_in, 6 * B * 16)

            @block.scalar
            def _(act):
                act.wait_ge(c_in, 16)
                nc.scalar.activation(th[:], ct[:], ACT.Tanh, scale=0.5).then_inc(tanh_done, 1)

            @block.vector
            def _(dve):
                dve.wait_ge(tanh_done, 1)
                nc.vector.scalar_tensor_tensor(out=act_c[:], in0=th[:], scalar=1.0, in1=ct[:],
                                               op0=ALU.add, op1=ALU.mult).then_inc(silu_step, 1)
                dve.wait_ge(silu_step, 1)
                nc.vector.tensor_scalar(act_c[:], act_c[:], 0.5, None, ALU.mult).then_inc(silu_step, 1)
                for v in range(6):
                    q = slice(32 * (v % 4), 32 * (v % 4) + B)
                    dve.wait_ge(mod_done, v + 1)
                    if v in (SA, SB):
                        nc.vector.tensor_copy(row[q, v, :], pm[q, v, :]).then_inc(rows_done, 1)
                    elif v in (CA, CB):
                        nc.vector.tensor_scalar(row[q, v, :], pm[q, v, :], 1.0, None, ALU.add).then_inc(rows_done, 1)
                    else:
                        k = v // 3
                        nc.vector.tensor_scalar(sgn[q, k, :], pm[q, v, :], 0.0, 2.0,
                                                ALU.is_ge, ALU.mult).then_inc(row_step, 1)
                        dve.wait_ge(row_step, 3 * k + 1)
                        nc.vector.scalar_tensor_tensor(out=mag[q, k, :], in0=sgn[q, k, :], scalar=-1.0,
                                                       in1=pm[q, v, :], op0=ALU.add, op1=ALU.mult).then_inc(row_step, 1)
                        dve.wait_ge(row_step, 3 * k + 2)
                        nc.vector.tensor_scalar(mag[q, k, :], mag[q, k, :], 0.25, None, ALU.max).then_inc(row_step, 1)
                        dve.wait_ge(row_step, 3 * k + 3)
                        nc.vector.scalar_tensor_tensor(out=row[q, v, :], in0=sgn[q, k, :], scalar=-1.0,
                                                       in1=mag[q, k, :], op0=ALU.add, op1=ALU.mult).then_inc(rows_done, 1)

            @block.tensor
            def _(pe):
                pe.wait_ge(silu_step, 2)
                for k in range(C):
                    pe.wait_ge(w_in[k], 16)
                for v in range(6):
                    q = 32 * (v % 4)
                    for k in range(C):
                        last = nc.tensor.matmul(pm[q:q + B, v, :], act_c[:, k, :], w[:, k, v * DM:(v + 1) * DM],
                                                start=(k == 0), stop=(k == C - 1), tile_position=(0, q))
                    last.then_inc(mod_done, 1)


def projections(nc, x, wq_t, wk_t, wv_t, ident, rows_bc, v_all, q_dram, k_dram):
    RX, RH, RT, RO, RS = 8, 4, 2, 4, 2
    BODY = 2 * SUP
    ITEMS = G + 2
    PAIRS = G + 1
    with ExitStack() as ctx:
        m = Mem(nc, ctx)
        wq = m.sb("p_wq", [P, C, DM])
        wk = m.sb("p_wk", [P, C, P])
        wv = m.sb("p_wv", [P, C, P])
        idn = m.sb("p_idn", [P, P])
        xt = m.sb("p_xt", [P, RX, DM])
        ln = LayerNorm(m, "p", SUP)
        hn = m.sb("p_hn", [P, RH, DM])
        ht = m.sb("p_ht", [P, 2, C, WIDE])
        hi = m.sb("p_hi", [P, RS, WIDE], F32R)
        lo = m.sb("p_lo", [P, RS, WIDE], F32R)
        tp = [m.ps(f"p_tp{k}", [P, C, P]) for k in range(RT)]
        po = [m.ps(f"p_po{k}", [P, WIDE]) for k in range(RO)]

        weights_in = m.sem("weights_in")
        x_in = [m.sem(f"x_in{k}") for k in range(RX)]
        norm_done = m.sem("norm_done")
        mul_done = m.sem("mul_done")
        h_done = m.sem("h_done")
        tp_done = m.sem("tp_done")
        ht_done = m.sem("ht_done")
        out_done = m.sem("out_done")
        hi_done = m.sem("hi_done")
        lo_done = m.sem("lo_done")
        v_done = m.sem("v_done")
        stage_out = [m.sem(f"stage_out{k}") for k in range(RS)]

        with nc.Block() as block:

            @block.sync
            def _(sp):
                sp.dma_start(idn[:], ident).then_inc(weights_in, 16)
                sp.dma_start(wq[:], wq_t.rearrange("(k p) n -> p k n", p=P)).then_inc(weights_in, 16)
                sp.dma_start(wk[:], wk_t.rearrange("(k p) n -> p k n", p=P)).then_inc(weights_in, 16)
                sp.dma_start(wv[:], wv_t.rearrange("(k p) n -> p k n", p=P)).then_inc(weights_in, 16)
                with sp.Fori(0, NT // BODY) as n:
                    for l in range(BODY):
                        sp.wait_ge(norm_done, n * BODY + l + 1)
                        sp.dma_start(xt[:, l % RX, :], x[bass.ds(n * (BODY * P) + l * P, P), :])\
                          .then_inc(x_in[l % RX], 16)

            @block.vector
            def _(dve):
                dve.sem_inc(norm_done, RX)
                dve.sem_inc(lo_done, PAIRS)

                def norm(n, l):
                    dve.wait_ge(tp_done, n * BODY + l + 1)
                    ln.apply(nc, hn[:, l % RH, :], xt[:, l % RX, :], l % SUP).then_inc(norm_done, 1)

                def statistics(n, u):
                    for j in range(SUP):
                        l = u * SUP + j
                        dve.wait_ge(x_in[l % RX], (n + 1) * 16)
                        ln.statistics(nc, xt[:, l % RX, :], j)
                    ln.deviation(nc, dve, n * 2 + u)

                def split(n, u, item):
                    slot = (u * PAIRS + item) % RS
                    bank = (u * ITEMS + item) % RO
                    dve.wait_ge(hi_done, n * (2 * PAIRS) + u * PAIRS + item + 1)
                    nc.vector.scalar_tensor_tensor(out=lo[:, slot, :], in0=po[bank][:],
                                                   scalar=QSCALE if item < G else 1.0,
                                                   in1=hi[:, slot, :].bitcast(F32), op0=ALU.mult,
                                                   op1=ALU.subtract).then_inc(lo_done, 1)

                def body(n, more):
                    for u in range(2):
                        ahead = u == 0 or more
                        after = (n, 1) if u == 0 else (n + 1, 0)
                        if ahead:
                            statistics(*after)
                        for item in range(PAIRS):
                            if ahead and item < SUP:
                                norm(after[0], after[1] * SUP + item)
                            split(n, u, item)

                statistics(0, 0)
                for j in range(SUP):
                    norm(0, j)
                with dve.Fori(0, NT // BODY - 1) as n:
                    body(n, True)
                body(NT // BODY - 1, False)

            @block.gpsimd
            def _(pool):
                for b in range(B):
                    with pool.Fori(b * (NB // BODY), (b + 1) * (NB // BODY)) as n:
                        for l in range(BODY):
                            k = n * BODY + l
                            r = l % RH
                            pool.wait_ge(norm_done, RX + k + 1)
                            nc.gpsimd.tensor_tensor(hn[:, r, :], hn[:, r, :], rows_bc[:, b, CA, :],
                                                    ALU.mult).then_inc(mul_done, 1)
                            pool.wait_ge(mul_done, k + 1)
                            nc.gpsimd.tensor_tensor(hn[:, r, :], hn[:, r, :], rows_bc[:, b, SA, :],
                                                    ALU.add).then_inc(h_done, 1)

            @block.scalar
            def _(act):
                act.sem_inc(ht_done, RT)
                act.sem_inc(v_done, 1)

                def transposed(n, l):
                    k = n * BODY + l
                    u, j = divmod(l, SUP)
                    act.wait_ge(tp_done, RH + k + 1)
                    if j == 0:
                        act.wait_ge(out_done, (n * 2 + u + 1) * ITEMS)
                    nc.scalar.activation(ht[:, u, :, j * P:(j + 1) * P], tp[l % RT][:], ACT.Copy).then_inc(ht_done, 1)

                def high(n, u, item):
                    slot = (u * PAIRS + item) % RS
                    bank = (u * ITEMS + item) % RO
                    act.wait_ge(out_done, 2 * ITEMS + (n * 2 + u) * ITEMS + item + 1)
                    act.wait_ge(stage_out[slot], n * (PAIRS * 32) + (u * PAIRS + item) // RS * 32)
                    nc.scalar.activation(hi[:, slot, :], po[bank][:], ACT.Copy,
                                         scale=QSCALE if item < G else 1.0).then_inc(hi_done, 1)
                    act.wait_ge(hi_done, n * (2 * PAIRS) + u * PAIRS + item + 1)
                    act.wait_ge(lo_done, PAIRS + n * (2 * PAIRS) + u * PAIRS + item + 1)
                    for half, src in ((0, hi), (1, lo)):
                        if item < G:
                            dst = q_dram[bass.ds(n // 2 * G + item, 1), half, :,
                                         bass.ds(n % 2 * (BODY * P) + u * WIDE, WIDE)]
                            act.dma_start(dst.rearrange("o p t -> (o p) t"), src[:, slot, :].bitcast(F32))\
                               .then_inc(stage_out[slot], 16)
                        else:
                            dst = k_dram[bass.ds(n // 2, 1), half, :,
                                         bass.ds(n % 2 * (BODY * P) + u * WIDE, WIDE)]
                            act.dma_start(dst.rearrange("o p t -> (o p) t"), src[:, slot, :].bitcast(F32))\
                               .then_inc(stage_out[slot], 16)

                def values(n, u):
                    bank = (u * ITEMS + G + 1) % RO
                    act.wait_ge(out_done, 2 * ITEMS + (n * 2 + u + 1) * ITEMS)
                    nc.scalar.activation(v_all[:, bass.ds(n * BODY + u * SUP, SUP), :],
                                         po[bank][:].rearrange("p (j c) -> p j c", c=P), ACT.Copy).then_inc(v_done, 1)

                def body(n, more):
                    for u in range(2):
                        ahead = u == 0 or more
                        after = (n, SUP) if u == 0 else (n + 1, 0)
                        if ahead:
                            ln.root(nc, act, n * 2 + u + 1)
                        for item in range(PAIRS):
                            high(n, u, item)
                            if ahead and item < SUP:
                                transposed(after[0], after[1] + item)
                        values(n, u)

                ln.root(nc, act, 0)
                for l in range(SUP):
                    transposed(0, l)
                with act.Fori(0, NT // BODY - 1) as n:
                    body(n, True)
                body(NT // BODY - 1, False)
                for slot in range(RS):
                    act.wait_ge(stage_out[slot], NT // BODY * PAIRS * 32)

            @block.tensor
            def _(pe):
                pe.sem_inc(tp_done, RH)
                pe.sem_inc(out_done, 2 * ITEMS)
                pe.wait_ge(weights_in, 4 * 16)

                def transposes(n, l):
                    pe.wait_ge(h_done, n * BODY + l + 1)
                    pe.wait_ge(ht_done, n * BODY + l + 1)
                    for c in range(C):
                        last = nc.tensor.transpose(tp[l % RT][:, c, :], hn[:, l % RH, c * P:(c + 1) * P], idn[:])
                    last.then_inc(tp_done, 1)

                def project(n, u, item):
                    s = n * 2 + u
                    bank = (u * ITEMS + item) % RO
                    if item < RO - 1:
                        pe.wait_ge(lo_done, s * PAIRS + item + 3)
                    elif item == RO - 1:
                        pe.wait_ge(v_done, s + 1)
                    else:
                        pe.wait_ge(lo_done, PAIRS + s * PAIRS + item - RO + 1)
                    if item <= G:
                        for c in range(C):
                            w = wq[:, c, item * P:(item + 1) * P] if item < G else wk[:, c, :]
                            last = nc.tensor.matmul(po[bank][:], w, ht[:, u, c, :], start=(c == 0), stop=(c == C - 1))
                    else:
                        for j in range(SUP):
                            for c in range(C):
                                last = nc.tensor.matmul(po[bank][:, j * P:(j + 1) * P],
                                                        ht[:, u, c, j * P:(j + 1) * P], wv[:, c, :],
                                                        start=(c == 0), stop=(c == C - 1))
                    last.then_inc(out_done, 1)

                def body(n, more):
                    for u in range(2):
                        ahead = u == 0 or more
                        after = (n, SUP) if u == 0 else (n + 1, 0)
                        pe.wait_ge(ht_done, RT + n * BODY + (u + 1) * SUP)
                        for item in range(ITEMS):
                            project(n, u, item)
                            if ahead and item < SUP:
                                transposes(after[0], after[1] + item)

                for l in range(SUP):
                    transposes(0, l)
                with pe.Fori(0, NT // BODY - 1) as n:
                    body(n, True)
                body(NT // BODY - 1, False)


class Task:

    def __init__(self, u, qb, r, first_half, first_group):
        self.u, self.qb, self.r = u, qb, r
        self.keys = (qb + 1) * P
        self.halves = -(-self.keys // HALF)
        self.groups = -(-self.keys // WIDE)
        self.half0, self.group0 = first_half, first_group
        self.qi = u * NB + qb

    def half_span(self, h):
        return h * HALF, min(self.keys, (h + 1) * HALF)

    def blocks(self, j):
        return range(4 * j, min(self.qb + 1, 4 * j + 4))


HALF = 2 * WIDE


def attention_tasks():
    tasks, half, group = [], 0, 0
    for u in range(2):
        for qb in range(NB):
            for r in range(REP):
                tasks.append(Task(u, qb, r, half, group))
                half += tasks[-1].halves
                group += tasks[-1].groups
    return tasks, half, group


def attention(nc, q_dram, k_dram, o_dram, dist, slopes, ident, v_all, slot_dram):
    tasks, HALVES, GROUPS = attention_tasks()
    UNIT_HALVES, UNIT_GROUPS = HALVES // 2, GROUPS // 2
    QIS = 2 * NB
    BODIES = UNITS // 2
    XR, TR, PR, AHEAD = 4, 2, 4, 3
    ZERO = ROWS * DM // P // (2 * UNITS)
    SBS = 2 * NB // SUP
    LAST_QI_HALF = [max(t.half0 + t.halves for t in tasks if t.qi == qi) for qi in range(QIS)]

    owner, rank = [], []
    for t in tasks:
        for j in range(t.groups):
            busy = j in [h * t.groups // t.halves for h in range(t.halves)]
            owner.append("A" if (busy and t.groups > 1) or (t.groups == 1 and t.r % 2) else "D")
            rank.append(owner[:-1].count(owner[-1]))
    COPIES = {k: owner.count(k) for k in "AD"}

    with ExitStack() as ctx:
        m = Mem(nc, ctx)
        idn = m.sb("a_idn", [P, P])
        dst = m.sb("a_dist", [P, S])
        slope_all = m.sb("a_slope_all", [P, (UNITS + 1) * REP])
        slope = m.sb("a_slope", [P, 2, REP])
        bias = m.sb("a_bias", [P, 2, REP, S])
        vcur = m.sb("a_vcur", [P, 2, NB, D])
        kp = m.sb("a_kp", [P, 2, S], F32R)
        qp = m.sb("a_qp", [P, 2, REP, WIDE], F32R)
        xs = m.sb("a_xs", [P, XR, S])
        zeros = m.sb("a_zeros", [P, ZERO])
        pt = m.sb("a_pt", [P, PR, WIDE])
        mn = m.sb("a_mn", [P, XR, 2])
        sums = m.sb("a_sums", [P, 2, REP, 2])
        total = m.sb("a_total", [P, 2, REP])
        rec = m.sb("a_rec", [P, 2, REP])
        recw = m.sb("a_recw", [P, 2, REP, D])
        rt = m.sb("a_rt", [P, 2, P])
        os = m.sb("a_os", [P, 2, P])
        sp_ps = [m.ps(f"a_s{k}", [P, HALF]) for k in range(2)]
        tp = [m.ps(f"a_t{k}", [P, WIDE]) for k in range(TR)]
        op = [m.ps(f"a_o{k}", [P, WIDE]) for k in range(2)]

        const_in = m.sem("const_in")
        zeros_set = m.sem("zeros_set")
        zeros_out = m.sem("zeros_out")
        k_in = [m.sem(f"k_in{k}") for k in range(2)]
        q_in = [m.sem(f"q_in{k}") for k in range(2)]
        slope_done = m.sem("slope_done")
        bias_done = m.sem("bias_done")
        vcur_done = m.sem("vcur_done")
        qk_done = m.sem("qk_done")
        min_done = m.sem("min_done")
        exp_done = m.sem("exp_done")
        tr_done = m.sem("tr_done")
        copied = {k: m.sem("copied_" + k) for k in "AD"}
        pv_done = m.sem("pv_done")
        total_done = m.sem("total_done")
        rec_done = m.sem("rec_done")
        recw_done = m.sem("recw_done")
        rtr_done = m.sem("rtr_done")
        rt_done = m.sem("rt_done")
        o_done = m.sem("o_done")
        o_out = [m.sem(f"o_out{k}") for k in range(2)]

        def at(i, count, event):
            return (i + 1) * count + event + 1

        slot_rows = slot_dram.rearrange("(p f) n -> p (f n)", p=P)

        with nc.Block() as block:

            @block.sync
            def _(sp):
                sp.dma_start(idn[:], ident).then_inc(const_in, 16)
                sp.dma_start(dst[:], dist).then_inc(const_in, 16)
                sp.dma_start(slope_all[:], slopes).then_inc(const_in, 16)
                sp.wait_ge(zeros_set, 1)
                with sp.Fori(0, BODIES) as i:
                    for u in range(2):
                        sp.wait_ge(qk_done, at(i, HALVES, (u + 1) * UNIT_HALVES - 1 - HALVES))
                        for s in range(4):
                            sp.dma_start(kp[s * D:(s + 1) * D, u, :].bitcast(F32),
                                         k_dram[bass.ds(i // 2, 1), s % 2, bass.ds(i % 2 * (2 * D) + u * D, D), :]
                                         .rearrange("o p t -> (o p) t")).then_inc(k_in[u], 16)
                        for c in range(NB // SUP):
                            q = u * (NB // SUP) + c
                            qi = (q - 2) * SUP + SUP - 1
                            last = LAST_QI_HALF[qi] if qi >= 0 else LAST_QI_HALF[qi + QIS] - HALVES
                            sp.wait_ge(qk_done, at(i, HALVES, last - 1))
                            for s in range(4):
                                sp.dma_start(qp[s * D:(s + 1) * D, q % 2, :, :].bitcast(F32),
                                             q_dram[bass.ds(i * 2 + u, 1), s // 2, :, c * WIDE:(c + 1) * WIDE]
                                             .rearrange("o (r d) t -> (o d) r t", d=D)).then_inc(q_in[q % 2], 16)
                            if c % 2:
                                sp.dma_start(slot_rows[:, bass.ds((i * 4 + u * 2 + c // 2) * ZERO, ZERO)],
                                             zeros[:]).then_inc(zeros_out, 16)
                sp.wait_ge(zeros_out, 2 * UNITS * 16)

            @block.gpsimd
            def _(pool):
                def tables(i, u, r):
                    unit = i * 2 + u
                    slot = u % 2
                    if r == 0:
                        pool.wait_ge(min_done, at(i, HALVES, (u + 1) * UNIT_HALVES - 1 - HALVES))
                        apart(pool, m.passed)
                        nc.gpsimd.tensor_copy(slope[:, slot, :], slope_all[:, bass.ds(unit * REP, REP)]).then_inc(slope_done, 1)
                        pool.wait_ge(slope_done, unit + 1)
                        apart(pool, m.passed)
                    nc.gpsimd.tensor_scalar(bias[:, slot, r, :], dst[:], slope[:, slot, r:r + 1], None,
                                            ALU.mult).then_inc(bias_done, 1)

                def values(i, u):
                    pool.wait_ge(pv_done, at(i, GROUPS, (u + 1) * UNIT_GROUPS - 1 - GROUPS))
                    apart(pool, m.passed)
                    nc.gpsimd.tensor_copy(vcur[:, u, :, :],
                                          v_all[:, bass.ds(i // 2 * NB, NB), bass.ds(i % 2 * (2 * D) + u * D, D)])\
                      .then_inc(vcur_done, 1)

                def widen(i, qi):
                    pool.wait_ge(rec_done, at(i, QIS, qi))
                    pool.wait_ge(rtr_done, at(i, QIS, qi - 2))
                    apart(pool, m.passed)
                    nc.gpsimd.tensor_copy(recw[:, qi % 2, :, :],
                                          rec[:, qi % 2, :].unsqueeze(2).broadcast_to([P, REP, D])).then_inc(recw_done, 1)

                def store(i, qi):
                    u, qb = divmod(qi, NB)
                    pool.wait_ge(o_done, at(i, QIS, qi))
                    pool.dma_start(o_dram[bass.ds(i * 2 + u, 1), qb, :, :].rearrange("o p t -> (o p) t"),
                                   os[:, qi % 2, :]).then_inc(o_out[qi % 2], 16)

                pool.wait_ge(const_in, 3 * 16)
                for r in range(REP):
                    tables(0, 0, r)
                with pool.Fori(0, BODIES) as i:
                    for qi in range(QIS):
                        u, qb = divmod(qi, NB)
                        if qb == 0:
                            values(i, u)
                        widen(i, qi)
                        if qb in (2, 5, 8, 11):
                            tables(i, u + 1, (qb - 2) // 3)
                        if qi:
                            store(i, qi - 1)
                    store(i, QIS - 1)
                for k in range(2):
                    pool.wait_ge(o_out[k], BODIES * QIS // 2 * 16)

            @block.vector
            def _(dve):
                dve.sem_inc(min_done, HALVES)
                dve.sem_inc(copied["D"], COPIES["D"])
                dve.sem_inc(rec_done, QIS)
                dve.sem_inc(o_done, QIS)
                nc.vector.memset(zeros[:], 0.0).then_inc(zeros_set, 1)

                def minimum(i, t, h):
                    task = tasks[t]
                    hs = task.half0 + h
                    a, b = task.half_span(h)
                    x = t % XR
                    off = (NB - 1 - task.qb) * P
                    if t % REP == 0 and task.qb == 0 and h == 0:
                        dve.wait_ge(bias_done, i * (2 * REP) + (task.u + 1) * REP)
                    dve.wait_ge(qk_done, at(i, HALVES, hs))
                    if h == 0:
                        old = tasks[t - XR]
                        dve.wait_ge(tr_done, at(i, GROUPS, old.group0 + old.groups - 1 - (GROUPS if t < XR else 0)))
                        start = 3e38
                    else:
                        dve.wait_ge(min_done, at(i, HALVES, hs - 1))
                        start = mn[:, x, 0:1]
                    apart(dve, m.passed)
                    nc.vector.tensor_tensor_reduce(out=xs[:, x, a:b], in0=sp_ps[hs % 2][:, 0:b - a],
                                                   in1=bias[:, task.u, task.r, off + a:off + b], scale=1.0, scalar=start,
                                                   op0=ALU.add, op1=ALU.min, accum_out=mn[:, x, h:h + 1])\
                      .then_inc(min_done, 1)

                def copy(i, g, cols):
                    dve.wait_ge(tr_done, at(i, GROUPS, g))
                    dve.wait_ge(pv_done, at(i, GROUPS, g - PR))
                    nc.vector.tensor_copy(pt[:, g % PR, 0:cols], tp[g % TR][:, 0:cols]).then_inc(copied["D"], 1)

                def reciprocal(i, qi):
                    task = tasks[qi * REP + REP - 1]
                    k = qi % 2
                    dve.wait_ge(exp_done, i * HALVES + task.half0 + task.halves)
                    dve.wait_ge(recw_done, i * QIS + max(qi - 1, 0))
                    src = sums[:, k, :, 0]
                    if task.halves > 1:
                        nc.vector.tensor_tensor(total[:, k, :], sums[:, k, :, 0], sums[:, k, :, 1], ALU.add)\
                          .then_inc(total_done, 1)
                        dve.wait_ge(total_done, i * NB + (qi // NB) * (NB // 2) + task.qb - NB // 2 + 1)
                        src = total[:, k, :]
                    nc.vector.reciprocal(rec[:, k, :], src).then_inc(rec_done, 1)

                def normalise(i, qi):
                    k = qi % 2
                    dve.wait_ge(rt_done, i * QIS + qi + 1)
                    dve.wait_ge(o_out[k], i * (QIS // 2 * 16) + qi // 2 * 16)
                    nc.vector.tensor_tensor(os[:, k, :], op[k][:, 0:P], rt[:, k, :], ALU.mult).then_inc(o_done, 1)

                with dve.Fori(0, BODIES) as i:
                    for t in range(2):
                        for h in range(tasks[t].halves):
                            minimum(i, t, h)
                    for t, task in enumerate(tasks):
                        for j in range(task.groups):
                            if t + 2 < len(tasks):
                                nxt = tasks[t + 2]
                                for h in range(nxt.halves):
                                    if min(h * nxt.groups // nxt.halves, task.groups - 1) == j:
                                        minimum(i, t + 2, h)
                            g = task.group0 + j
                            if owner[g] == "D":
                                copy(i, g, len(task.blocks(j)) * P)
                        if task.r == 0 and task.qi:
                            reciprocal(i, task.qi - 1)
                        if task.r == 2 and task.qi:
                            normalise(i, task.qi - 1)
                    reciprocal(i, QIS - 1)
                    normalise(i, QIS - 1)

            @block.scalar
            def _(act):
                act.sem_inc(copied["A"], COPIES["A"])

                def exponentials(i, t, h):
                    task = tasks[t]
                    a, b = task.half_span(h)
                    x = t % XR
                    act.wait_ge(min_done, at(i, HALVES, task.half0 + task.halves - 1))
                    if task.r == 0 and h == 0:
                        act.wait_ge(rec_done, at(i, QIS, task.qi - 2))
                    nc.scalar.activation(xs[:, x, a:b], xs[:, x, a:b], ACT.Exp, scale=-1.0,
                                         bias=mn[:, x, task.halves - 1:task.halves],
                                         accum_out=sums[:, task.qi % 2, task.r, h:h + 1]).then_inc(exp_done, 1)

                def copy(i, g, cols):
                    act.wait_ge(tr_done, at(i, GROUPS, g))
                    act.wait_ge(pv_done, at(i, GROUPS, g - PR))
                    nc.scalar.activation(pt[:, g % PR, 0:cols], tp[g % TR][:, 0:cols], ACT.Copy).then_inc(copied["A"], 1)

                def reciprocals(i, qi):
                    act.wait_ge(rtr_done, at(i, QIS, qi))
                    act.wait_ge(o_done, at(i, QIS, qi - 2))
                    nc.scalar.activation(rt[:, qi % 2, :], op[qi % 2][:, P:2 * P], ACT.Copy).then_inc(rt_done, 1)

                with act.Fori(0, BODIES) as i:
                    for h in range(tasks[0].halves):
                        exponentials(i, 0, h)
                    for t, task in enumerate(tasks):
                        for j in range(task.groups):
                            g = task.group0 + j
                            if owner[g] == "A":
                                copy(i, g, len(task.blocks(j)) * P)
                            if t + 1 < len(tasks):
                                nxt = tasks[t + 1]
                                for h in range(nxt.halves):
                                    if min(h * nxt.groups // nxt.halves, task.groups - 1) == j:
                                        exponentials(i, t + 1, h)
                        if task.r == 1 and task.qi:
                            reciprocals(i, task.qi - 1)
                    reciprocals(i, QIS - 1)

            @block.tensor
            def _(pe):
                pe.sem_inc(qk_done, HALVES)
                pe.sem_inc(tr_done, GROUPS)
                pe.sem_inc(pv_done, GROUPS)
                pe.sem_inc(rtr_done, QIS)
                pe.wait_ge(const_in, 3 * 16)

                def scores(i, t, h):
                    task = tasks[t]
                    hs = task.half0 + h
                    a, b = task.half_span(h)
                    q = task.qi // SUP
                    if task.qb == 0 and task.r == 0:
                        pe.wait_ge(k_in[task.u], (i + 1) * 64)
                    if task.qb % SUP == 0 and task.r == 0 and h == 0:
                        pe.wait_ge(q_in[q % 2], i * (SBS // 2 * 64) + (q // 2 + 1) * 64)
                    pe.wait_ge(min_done, at(i, HALVES, hs - 2))
                    for c in range(a, b, WIDE):
                        e = min(b, c + WIDE)
                        last = nc.tensor.matmul(sp_ps[hs % 2][:, c - a:e - a],
                                                qp[:, q % 2, task.r, task.qb % SUP * P:(task.qb % SUP + 1) * P],
                                                kp[:, task.u, c:e], start=True, stop=True)
                    last.then_inc(qk_done, 1)

                def transposes(i, t, j):
                    task = tasks[t]
                    g = task.group0 + j
                    pe.wait_ge(exp_done, i * HALVES + task.half0 + j // 2 + 1)
                    wait_copy(i, g - TR)
                    for k, c in enumerate(task.blocks(j)):
                        last = nc.tensor.transpose(tp[g % TR][:, k * P:(k + 1) * P], xs[:, t % XR, c * P:(c + 1) * P], idn[:])
                    last.then_inc(tr_done, 1)

                def wait_copy(i, g):
                    who = owner[g]
                    pe.wait_ge(copied[who], at(i, COPIES[who], rank[g] - (COPIES[who] if g < 0 else 0)))

                def products(i, t, j):
                    task = tasks[t]
                    g = task.group0 + j
                    wait_copy(i, g)
                    if j == 0 and task.r == 0:
                        pe.wait_ge(o_done, at(i, QIS, task.qi - 2))
                        if task.qb == 0:
                            pe.wait_ge(vcur_done, i * 2 + task.u + 1)
                    o = op[task.qi % 2][task.r * D:(task.r + 1) * D, 0:P]
                    for k, c in enumerate(task.blocks(j)):
                        last = nc.tensor.matmul(o, vcur[:, task.u, c, :], pt[:, g % PR, k * P:(k + 1) * P],
                                                start=(c == 0), stop=(c == task.qb), tile_position=(0, task.r * D))
                    last.then_inc(pv_done, 1)

                def reciprocals(i, qi):
                    pe.wait_ge(recw_done, i * QIS + qi + 1)
                    nc.tensor.transpose(op[qi % 2][:, P:2 * P], recw[:, qi % 2, :, :].rearrange("p r d -> p (r d)"),
                                        idn[:]).then_inc(rtr_done, 1)

                with pe.Fori(0, BODIES) as i:
                    for t in range(AHEAD):
                        for h in range(tasks[t].halves):
                            scores(i, t, h)
                    waiting = []
                    for t, task in enumerate(tasks):
                        for j in range(task.groups):
                            transposes(i, t, j)
                            waiting.append((t, j))
                            if len(waiting) > TR:
                                products(i, *waiting.pop(0))
                            if t + AHEAD < len(tasks):
                                nxt = tasks[t + AHEAD]
                                for h in range(nxt.halves):
                                    if min((h + 1) * nxt.groups // nxt.halves, task.groups) - 1 == j:
                                        scores(i, t + AHEAD, h)
                        if task.r == 1 and task.qi and not [w for w in waiting if tasks[w[0]].qi < task.qi]:
                            reciprocals(i, task.qi - 1)
                        elif task.r == 1 and task.qi:
                            raise AssertionError("products late")
                    for w in waiting:
                        products(i, *w)
                    reciprocals(i, QIS - 1)


def mix_and_gate(nc, x, o_dram, wo_t, gate_w_t, gate_b, gate_bias, ident, rows_bc, top_v, top_i, x1_dram, h2_dram,
                 fetch):
    RX, RH, RT = 8, 4, 2
    BODY = 2 * SUP
    with ExitStack() as ctx:
        m = Mem(nc, ctx)
        idn = m.sb("g_idn", [P, P])
        wo = m.sb("g_wo", [P, B * G, DM])
        gw = m.sb("g_gw", [P, C, E])
        gb = m.sb("g_gb", [P, 2, E])
        gbs = m.sb("g_gbs", [P, E])
        ot = m.sb("g_ot", [P, SUP, G, P])
        xt = m.sb("g_xt", [P, RX, DM])
        hn = m.sb("g_hn", [P, RH, DM])
        ht = m.sb("g_ht", [P, RT, C, P])
        score = m.sb("g_score", [P, 2, E])
        best = m.sb("g_best", [P, 2, 8])
        index = m.sb("g_index", [P, 2, 8], U32)
        ln = LayerNorm(m, "g", SUP)
        pp = [m.ps(f"g_pp{k}", [P, DM]) for k in range(2)]
        tp = [m.ps(f"g_tp{k}", [P, C, P]) for k in range(RT)]
        pg = [m.ps(f"g_pg{k}", [P, DM]) for k in range(2)]

        wo_in = m.sem("wo_in")
        const_in = m.sem("g_const_in")
        wo_scaled = m.sem("wo_scaled")
        gbs_done = m.sem("gbs_done")
        o_in = [m.sem(f"o_in{k}") for k in range(SUP)]
        x_in = [m.sem(f"gx_in{k}") for k in range(RX)]
        proj_done = m.sem("proj_done")
        x1_done = m.sem("x1_done")
        x1_out = [m.sem(f"x1_out{k}") for k in range(RX)]
        norm_done = m.sem("g_norm_done")
        mul_done = m.sem("g_mul_done")
        h_done = m.sem("g_h_done")
        h_out = [m.sem(f"h_out{k}") for k in range(RH)]
        tp_done = m.sem("g_tp_done")
        ht_done = m.sem("g_ht_done")
        gate_done = m.sem("gate_done")
        score_done = m.sem("score_done")
        best_done = m.sem("best_done")
        index_done = m.sem("index_done")
        kept_v = m.sem("kept_v")
        kept_i = m.sem("kept_i")

        with nc.Block() as block:

            @block.sync
            def _(sp):
                sp.dma_start(wo[:, 0:G, :], wo_t.rearrange("(g p) n -> p g n", p=P)).then_inc(wo_in, 16)
                sp.dma_start(wo[:, G:2 * G, :], wo_t.rearrange("(g p) n -> p g n", p=P)).then_inc(wo_in, 16)
                sp.dma_start(idn[:], ident).then_inc(const_in, 16)
                sp.dma_start(gw[:], gate_w_t.rearrange("(c p) e -> p c e", p=P)).then_inc(const_in, 16)
                sp.dma_start(gb[:, 0, :], gate_b.partition_broadcast(P)).then_inc(const_in, 16)
                sp.dma_start(gb[:, 1, :], gate_bias.partition_broadcast(P)).then_inc(const_in, 16)

                def load(n, l):
                    k = n * BODY + l
                    sp.wait_ge(proj_done, k + 1)
                    sp.dma_start(ot[:, l % SUP, :, :],
                                 o_dram[bass.ds(n // 2 * G, G), bass.ds(n % 2 * BODY + l, 1), :, :]
                                 .rearrange("g o p t -> p (g o) t")).then_inc(o_in[l % SUP], 16)
                    sp.wait_ge(x1_out[l % RX], n * 16)
                    sp.wait_ge(norm_done, k + 1)
                    sp.dma_start(xt[:, l % RX, :], x[bass.ds(k * P, P), :]).then_inc(x_in[l % RX], 16)

                with sp.Fori(0, NT // BODY) as n:
                    for l in range(BODY):
                        load(n, l)
                fetch(sp)

            @block.tensor
            def _(pe):
                pe.sem_inc(proj_done, SUP)
                pe.sem_inc(tp_done, RH)
                pe.sem_inc(gate_done, RT)
                pe.wait_ge(const_in, 4 * 16)
                pe.wait_ge(wo_scaled, B * G)

                def project(n, l):
                    k = n * BODY + l
                    pe.wait_ge(o_in[l % SUP], n * (BODY // SUP * 16) + (l // SUP + 1) * 16)
                    pe.wait_ge(x1_done, k + 1)
                    for g in range(G):
                        w = wo[:, bass.ds(n // 2 * G + g, 1), :].rearrange("p o n -> p (o n)")
                        last = nc.tensor.matmul(pp[l % 2][:], ot[:, l % SUP, g, :], w, start=(g == 0), stop=(g == G - 1))
                    last.then_inc(proj_done, 1)

                def transposes(n, l):
                    k = n * BODY + l
                    pe.wait_ge(h_done, k + 1)
                    pe.wait_ge(ht_done, k + 1)
                    for c in range(C):
                        last = nc.tensor.transpose(tp[l % RT][:, c, :], hn[:, l % RH, c * P:(c + 1) * P], idn[:])
                    last.then_inc(tp_done, 1)

                def gate(n, l):
                    k = n * BODY + l
                    pe.wait_ge(ht_done, RT + k + 1)
                    pe.wait_ge(score_done, k + 1)
                    for c in range(C):
                        last = nc.tensor.matmul(pg[l % 2][:, 0:E], ht[:, l % RT, c, :], gw[:, c, :],
                                                start=(c == 0), stop=(c == C - 1))
                    last.then_inc(gate_done, 1)

                def body(n, more):
                    for u in range(2):
                        ahead = u == 0 or more
                        after = (n, SUP) if u == 0 else (n + 1, 0)
                        for j in range(SUP):
                            transposes(n, u * SUP + j)
                            if ahead:
                                project(after[0], after[1] + j)
                            gate(n, u * SUP + j)

                for l in range(SUP):
                    project(0, l)
                with pe.Fori(0, NT // BODY - 1) as n:
                    body(n, True)
                body(NT // BODY - 1, False)

            @block.vector
            def _(dve):
                dve.sem_inc(x1_done, 2)
                dve.sem_inc(norm_done, RX)
                dve.sem_inc(score_done, 2)
                dve.wait_ge(wo_in, 2 * 16)
                for b in range(B):
                    for g in range(G):
                        nc.vector.tensor_tensor(wo[:, b * G + g, :], wo[:, b * G + g, :], rows_bc[:, b, GA, :],
                                                ALU.mult).then_inc(wo_scaled, 1)
                dve.wait_ge(const_in, 4 * 16)
                nc.vector.tensor_tensor(gbs[:], gb[:, 0, :], gb[:, 1, :], ALU.add).then_inc(gbs_done, 1)
                dve.wait_ge(gbs_done, 1)

                def residual(n, l):
                    k = n * BODY + l
                    dve.wait_ge(x_in[l % RX], (n + 1) * 16)
                    dve.wait_ge(proj_done, SUP + k + 1)
                    nc.vector.tensor_tensor(xt[:, l % RX, :], pp[l % 2][:], xt[:, l % RX, :], ALU.add).then_inc(x1_done, 1)
                    dve.wait_ge(x1_done, 2 + k + 1)
                    ln.statistics(nc, xt[:, l % RX, :], l % SUP)

                def norm(n, l):
                    k = n * BODY + l
                    dve.wait_ge(tp_done, k + 1)
                    dve.wait_ge(h_out[l % RH], n * (BODY // RH * 16) + l // RH * 16)
                    ln.apply(nc, hn[:, l % RH, :], xt[:, l % RX, :], l % SUP).then_inc(norm_done, 1)

                def choose(n, l):
                    k = n * BODY + l
                    s = l % 2
                    dve.wait_ge(gate_done, RT + k + 1)
                    nc.vector.tensor_tensor(score[:, s, :], pg[s][:, 0:E], gbs[:], ALU.add).then_inc(score_done, 1)
                    dve.wait_ge(score_done, 2 + k + 1)
                    apart(dve, m.passed)
                    nc.vector.max(best[:, s, :], score[:, s, :]).then_inc(best_done, 1)
                    dve.wait_ge(best_done, k + 1)
                    apart(dve, m.passed)
                    nc.vector.max_index(index[:, s, :], best[:, s, :], score[:, s, :]).then_inc(index_done, 1)
                    dve.wait_ge(index_done, k + 1)
                    nc.vector.tensor_copy(top_v[:, bass.ds(k, 1), :], best[:, s:s + 1, 0:2]).then_inc(kept_v, 1)
                    nc.vector.tensor_copy(top_i[:, bass.ds(k, 1), :], index[:, s:s + 1, 0:2]).then_inc(kept_i, 1)

                def body(n, more):
                    for u in range(2):
                        ahead = u == 0 or more
                        after = (n, SUP) if u == 0 else (n + 1, 0)
                        for j in range(SUP):
                            if ahead:
                                residual(after[0], after[1] + j)
                            choose(n, u * SUP + j)
                        if ahead:
                            ln.deviation(nc, dve, n * 2 + u + 1)
                            for j in range(SUP):
                                norm(after[0], after[1] + j)

                for l in range(SUP):
                    residual(0, l)
                ln.deviation(nc, dve, 0)
                for l in range(SUP):
                    norm(0, l)
                with dve.Fori(0, NT // BODY - 1) as n:
                    body(n, True)
                body(NT // BODY - 1, False)
                dve.wait_ge(kept_v, NT)
                dve.wait_ge(kept_i, NT)

            @block.gpsimd
            def _(pool):
                for b in range(B):
                    with pool.Fori(b * (NB // BODY), (b + 1) * (NB // BODY)) as n:
                        for l in range(BODY):
                            k = n * BODY + l
                            r = l % RH
                            pool.wait_ge(norm_done, RX + k + 1)
                            nc.gpsimd.tensor_tensor(hn[:, r, :], hn[:, r, :], rows_bc[:, b, CB, :],
                                                    ALU.mult).then_inc(mul_done, 1)
                            pool.wait_ge(mul_done, k + 1)
                            nc.gpsimd.tensor_tensor(hn[:, r, :], hn[:, r, :], rows_bc[:, b, SB, :],
                                                    ALU.add).then_inc(h_done, 1)

            @block.scalar
            def _(act):
                act.sem_inc(ht_done, RT)

                def transposed(n, l):
                    k = n * BODY + l
                    act.wait_ge(tp_done, RH + k + 1)
                    act.wait_ge(gate_done, k + 1)
                    nc.scalar.activation(ht[:, l % RT, :, :], tp[l % RT][:], ACT.Copy).then_inc(ht_done, 1)
                    act.wait_ge(x1_done, 2 + k + 1)
                    act.dma_start(x1_dram[bass.ds(k * P, P), :], xt[:, l % RX, :]).then_inc(x1_out[l % RX], 16)
                    act.wait_ge(h_done, k + 1)
                    act.dma_start(h2_dram[bass.ds(k * P, P), :], hn[:, l % RH, :]).then_inc(h_out[l % RH], 16)

                def body(n, more):
                    for u in range(2):
                        for j in range(SUP):
                            transposed(n, u * SUP + j)
                        if u == 0 or more:
                            ln.root(nc, act, n * 2 + u + 1)

                ln.root(nc, act, 0)
                with act.Fori(0, NT // BODY - 1) as n:
                    body(n, True)
                body(NT // BODY - 1, False)
                for k in range(RX):
                    act.wait_ge(x1_out[k], NT // RX * 16)
                for k in range(RH):
                    act.wait_ge(h_out[k], NT // RH * 16)


def route(nc, top_v, top_i, before, experts, tile_start, gates, slots, tile_expert, h2_dram, slot_dram):
    RL = 4
    N = NT * E
    with ExitStack() as ctx:
        m = Mem(nc, ctx)
        tri = m.sb("r_tri", [P, P])
        ones = m.sb("r_ones", [P, P])
        iota = m.sb("r_iota", [P, NT, E])
        starts = m.sb("r_starts", [P, ST])
        mask = [m.sb(f"r_mask{k}", [P, NT, E]) for k in range(2)]
        both = m.sb("r_both", [P, NT, E])
        count = m.sb("r_count", [P, NT, E])
        upto = m.sb("r_upto", [P, NT, E])
        place = m.sb("r_place", [P, NT, E])
        hit = m.sb("r_hit", [P, NT, E])
        padded = m.sb("r_padded", [P, E])
        padded_i = m.sb("r_padded_i", [P, E], I32)
        ends = m.sb("r_ends", [P, E])
        begins = m.sb("r_begins", [P, E])
        slot_f = m.sb("r_slot_f", [P, NT])
        expert_f = m.sb("r_expert_f", [P, ST])
        diff = m.sb("r_diff", [P, NT])
        ratio = m.sb("r_ratio", [P, NT])
        one_more = m.sb("r_one_more", [P, NT])
        rows = m.sb("r_rows", [P, RL, DM])
        where = m.sb("r_where", [P, RL, 2], U32)
        rank_ps = m.ps("r_rank", [P, NT, E])
        total_ps = m.ps("r_total", [P, NT, E])

        const_in = m.sem("r_const_in")
        ones_set = m.sem("ones_set")
        step = m.sem("route_step")
        both_done = m.sem("both_done")
        ranked = m.sem("ranked")
        totalled = m.sem("totalled")
        diff_done = m.sem("diff_done")
        ratio_done = m.sem("ratio_done")
        slots_done = m.sem("slots_done")
        rows_in = [m.sem(f"rows_in{k}") for k in range(RL)]
        where_done = m.sem("where_done")
        scattered = [m.sem(f"scattered{k}") for k in range(RL)]

        with nc.Block() as block:

            @block.sync
            def _(sp):
                sp.dma_start(tri[:], before).then_inc(const_in, 16)
                sp.dma_start(iota[:], experts).then_inc(const_in, 16)
                sp.dma_start(starts[:], tile_start).then_inc(const_in, 16)
                with sp.Fori(0, NT // RL) as n:
                    for l in range(RL):
                        sp.wait_ge(scattered[l], n * 32)
                        sp.dma_start(rows[:, l, :], h2_dram[bass.ds(n * (RL * P) + l * P, P), :]).then_inc(rows_in[l], 16)

            @block.tensor
            def _(pe):
                pe.wait_ge(const_in, 3 * 16)
                pe.wait_ge(ones_set, 1)
                pe.wait_ge(both_done, 1)
                flat = both[:].rearrange("p t e -> p (t e)")
                nc.tensor.matmul(rank_ps[:].rearrange("p t e -> p (t e)"), tri[:], flat, start=True, stop=True).then_inc(ranked, 1)
                nc.tensor.matmul(total_ps[:].rearrange("p t e -> p (t e)"), ones[:], flat, start=True, stop=True).then_inc(totalled, 1)

            @block.scalar
            def _(act):
                act.wait_ge(diff_done, 1)
                nc.scalar.activation(ratio[:], diff[:], ACT.Exp).then_inc(ratio_done, 1)

            @block.vector
            def _(dve):
                done = [0]

                def then(ins):
                    done[0] += 1
                    ins.then_inc(step, 1)
                    dve.wait_ge(step, done[0])

                nc.vector.memset(ones[:], 1.0).then_inc(ones_set, 1)
                nc.vector.tensor_tensor(diff[:], top_v[:, :, 1], top_v[:, :, 0], ALU.subtract).then_inc(diff_done, 1)
                dve.wait_ge(const_in, 3 * 16)
                for k in range(2):
                    then(nc.vector.tensor_tensor(mask[k][:], iota[:], top_i[:, :, k].unsqueeze(2).broadcast_to([P, NT, E]),
                                                 ALU.is_equal))
                nc.vector.tensor_tensor(both[:], mask[0][:], mask[1][:], ALU.add).then_inc(both_done, 1)
                dve.wait_ge(ones_set, 1)
                dve.wait_ge(totalled, 1)
                then(nc.vector.tensor_copy(count[:], total_ps[:]))
                for e in range(E):
                    last = nc.vector.tensor_tensor_scan(out=upto[:, :, e], data0=ones[:, 0:NT], data1=count[:, :, e],
                                                        initial=0.0, op0=ALU.mult, op1=ALU.add)
                    then(last)
                then(nc.vector.tensor_scalar(padded_i[:], upto[:, NT - 1, :], float(P - 1), None, ALU.add))
                then(nc.vector.tensor_scalar(padded_i[:], padded_i[:], 7, 7, ALU.arith_shift_right, ALU.arith_shift_left))
                then(nc.vector.tensor_copy(padded[:], padded_i[:]))
                then(nc.vector.tensor_tensor_scan(out=ends[:], data0=ones[:, 0:E], data1=padded[:], initial=0.0,
                                                  op0=ALU.mult, op1=ALU.add))
                then(nc.vector.tensor_tensor(begins[:], ends[:], padded[:], ALU.subtract))
                then(nc.vector.tensor_tensor(place[:], upto[:], count[:], ALU.subtract))
                then(nc.vector.tensor_tensor(place[:], place[:], begins[:].unsqueeze(1).broadcast_to([P, NT, E]), ALU.add))
                dve.wait_ge(ranked, 1)
                then(nc.vector.tensor_tensor(place[:], rank_ps[:], place[:], ALU.add))
                for k in range(2):
                    then(nc.vector.tensor_tensor(hit[:], mask[k][:], place[:], ALU.mult))
                    then(nc.vector.tensor_reduce(slot_f[:], hit[:], AX.X, ALU.add))
                    nc.vector.tensor_copy(slots[:, :, k], slot_f[:]).then_inc(slots_done, 1)
                    dve.wait_ge(slots_done, k + 1)
                then(nc.vector.tensor_scalar(expert_f[:], starts[:], ends[:, 0:1], None, ALU.is_ge))
                for e in range(1, E - 1):
                    then(nc.vector.scalar_tensor_tensor(out=expert_f[:], in0=starts[:], scalar=ends[:, e:e + 1],
                                                        in1=expert_f[:], op0=ALU.is_ge, op1=ALU.add))
                then(nc.vector.tensor_copy(tile_expert[:], expert_f[:]))
                dve.wait_ge(ratio_done, 1)
                then(nc.vector.tensor_scalar(one_more[:], ratio[:], 1.0, None, ALU.add))
                then(nc.vector.reciprocal(gates[:, 0, :], one_more[:]))
                then(nc.vector.tensor_tensor(gates[:, 1, :], ratio[:], gates[:, 0, :], ALU.mult))

            @block.gpsimd
            def _(pool):
                pool.wait_ge(slots_done, 2)
                with pool.Fori(0, NT // RL) as n:
                    for l in range(RL):
                        pool.wait_ge(scattered[l], n * 32)
                        apart(pool, m.passed)
                        nc.gpsimd.tensor_copy(where[:, l:l + 1, :], slots[:, bass.ds(n * RL + l, 1), :]).then_inc(where_done, 1)
                        pool.wait_ge(where_done, n * RL + l + 1)
                        pool.wait_ge(rows_in[l], (n + 1) * 16)
                        apart(pool, m.passed)
                        for k in range(2):
                            pool.indirect_dma_start(slot_dram, bass.IndirectOffsetOnAxis(ap=where[:, l, k:k + 1], axis=0),
                                                    rows[:, l, :], None, bounds_check=ROWS - 1,
                                                    oob_is_err=False).then_inc(scattered[l], 16)
                for l in range(RL):
                    pool.wait_ge(scattered[l], NT // RL * 32)


def run_experts(nc, ident, w1, w2, b1, b2, weights_in, tile_expert, slot_dram, y_dram):
    RX = 4
    PADH = len(HC) * P
    with ExitStack() as ctx:
        m = Mem(nc, ctx)
        idn = m.sb("e_idn", [P, P])
        xt = m.sb("e_xt", [P, RX, DM])
        xtt = m.sb("e_xtt", [P, 2, C, P])
        z = m.sb("e_z", [P, 2, HF])
        th = m.sb("e_th", [P, 2, HF])
        hz = m.sb("e_hz", [P, 2, PADH])
        hzt = m.sb("e_hzt", [P, 2, PADH])
        ys = m.sb("e_ys", [P, 2, DM])
        tx = [m.ps(f"e_tx{k}", [P, C, P]) for k in range(2)]
        thp = [m.ps(f"e_th{k}", [P, PADH]) for k in range(2)]
        pz = [m.ps(f"e_pz{k}", [P, DM]) for k in range(2)]
        py = [m.ps(f"e_py{k}", [P, DM]) for k in range(2)]

        idn_in = m.sem("e_idn_in")
        x_in = [m.sem(f"ex_in{k}") for k in range(RX)]
        tx_done = m.sem("tx_done")
        xtt_done = m.sem("xtt_done")
        up_done = m.sem("up_done")
        z_done = m.sem("z_done")
        tanh_done = m.sem("e_tanh_done")
        pad_set = m.sem("pad_set")
        hz_done = m.sem("hz_done")
        th_done = m.sem("th_done")
        hzt_done = m.sem("hzt_done")
        down_done = m.sem("down_done")
        y_done = m.sem("y_done")
        y_out = [m.sem(f"y_out{k}") for k in range(2)]

        with nc.Block() as block:

            @block.sync
            def _(sp):
                sp.dma_start(idn[:], ident).then_inc(idn_in, 16)
                with sp.Fori(0, ST // RX) as n:
                    for l in range(RX):
                        sp.wait_ge(tx_done, n * RX + l + 1)
                        sp.dma_start(xt[:, l, :], slot_dram[bass.ds(n * (RX * P) + l * P, P), :]).then_inc(x_in[l], 16)

            @block.tensor
            def _(pe):
                pe.sem_inc(tx_done, RX)
                pe.sem_inc(up_done, 2)
                pe.sem_inc(th_done, 2)
                pe.sem_inc(down_done, 2)
                pe.wait_ge(idn_in, 16)
                for s in weights_in:
                    pe.wait_ge(*s)

                def transposes(n, l):
                    k = n * RX + l
                    pe.wait_ge(x_in[l], (n + 1) * 16)
                    pe.wait_ge(xtt_done, k + 1)
                    for c in range(C):
                        last = nc.tensor.transpose(tx[l % 2][:, c, :], xt[:, l, c * P:(c + 1) * P], idn[:])
                    last.then_inc(tx_done, 1)

                def up(n, l):
                    k = n * RX + l
                    e = nc.tensor.value_load(tile_expert[0:1, bass.ds(k, 1)], min_val=0, max_val=E - 1)
                    pe.wait_ge(xtt_done, 2 + k + 1)
                    pe.wait_ge(z_done, k + 1)
                    for c in range(C):
                        last = nc.tensor.matmul(pz[l % 2][:, 0:HF], xtt[:, l % 2, c, :], w1[:, c, bass.ds(e * HF, HF)],
                                                start=(c == 0), stop=(c == C - 1))
                    last.then_inc(up_done, 1)

                def turn(n, l):
                    k = n * RX + l
                    pe.wait_ge(hz_done, k + 1)
                    pe.wait_ge(hzt_done, k + 1)
                    for c in range(len(HC)):
                        last = nc.tensor.transpose(thp[l % 2][:, c * P:(c + 1) * P], hz[:, l % 2, c * P:(c + 1) * P], idn[:])
                    last.then_inc(th_done, 1)

                def down(n, l):
                    k = n * RX + l
                    e = nc.tensor.value_load(tile_expert[0:1, bass.ds(k, 1)], min_val=0, max_val=E - 1)
                    pe.wait_ge(hzt_done, 2 + k + 1)
                    pe.wait_ge(y_done, k + 1)
                    for c in range(len(HC)):
                        last = nc.tensor.matmul(py[l % 2][:], hzt[:, l % 2, c * P:(c + 1) * P], w2[:, c, bass.ds(e * DM, DM)],
                                                start=(c == 0), stop=(c == len(HC) - 1))
                    last.then_inc(down_done, 1)

                def body(n, more):
                    for l in range(RX):
                        ahead = l < RX - 1 or more
                        after = (n, l + 1) if l < RX - 1 else (n + 1, 0)
                        if ahead:
                            transposes(*after)
                        turn(n, l)
                        if ahead:
                            up(*after)
                        down(n, l)

                transposes(0, 0)
                up(0, 0)
                with pe.Fori(0, ST // RX - 1) as n:
                    body(n, True)
                body(ST // RX - 1, False)

            @block.scalar
            def _(act):
                act.sem_inc(xtt_done, 2)
                act.sem_inc(hzt_done, 2)

                def input_copy(n, l):
                    k = n * RX + l
                    act.wait_ge(tx_done, RX + k + 1)
                    act.wait_ge(up_done, k + 1)
                    nc.scalar.activation(xtt[:, l % 2, :, :], tx[l % 2][:], ACT.Copy).then_inc(xtt_done, 1)

                def hidden_copy(n, l):
                    k = n * RX + l
                    act.wait_ge(th_done, 2 + k + 1)
                    act.wait_ge(down_done, k + 1)
                    nc.scalar.activation(hzt[:, l % 2, :], thp[l % 2][:], ACT.Copy).then_inc(hzt_done, 1)

                def tanh(n, l):
                    k = n * RX + l
                    act.wait_ge(z_done, 2 + k + 1)
                    act.wait_ge(hz_done, n * RX + max(l - 1, 0))
                    nc.scalar.activation(th[:, l % 2, :], z[:, l % 2, :], ACT.Tanh, scale=0.5).then_inc(tanh_done, 1)

                def body(n, more):
                    for l in range(RX):
                        ahead = l < RX - 1 or more
                        after = (n, l + 1) if l < RX - 1 else (n + 1, 0)
                        if ahead:
                            input_copy(*after)
                        hidden_copy(n, l)
                        if ahead:
                            tanh(*after)

                input_copy(0, 0)
                tanh(0, 0)
                with act.Fori(0, ST // RX - 1) as n:
                    body(n, True)
                body(ST // RX - 1, False)

            @block.vector
            def _(dve):
                dve.sem_inc(z_done, 2)
                dve.sem_inc(y_done, 2)
                nc.vector.memset(hz[:, :, HF:PADH], 0.0).then_inc(pad_set, 1)
                dve.wait_ge(pad_set, 1)
                for s in weights_in:
                    dve.wait_ge(*s)

                def hidden(n, l):
                    k = n * RX + l
                    e = nc.vector.value_load(tile_expert[0:1, bass.ds(k, 1)], min_val=0, max_val=E - 1)
                    dve.wait_ge(up_done, 2 + k + 1)
                    nc.vector.tensor_tensor(z[:, l % 2, :], pz[l % 2][:, 0:HF], b1[:, bass.ds(e * HF, HF)],
                                            ALU.add).then_inc(z_done, 1)
                    dve.wait_ge(tanh_done, k + 1)
                    dve.wait_ge(th_done, k + 1)
                    nc.vector.scalar_tensor_tensor(out=hz[:, l % 2, 0:HF], in0=th[:, l % 2, :], scalar=1.0,
                                                   in1=z[:, l % 2, :], op0=ALU.add, op1=ALU.mult).then_inc(hz_done, 1)

                def output(n, l):
                    k = n * RX + l
                    e = nc.vector.value_load(tile_expert[0:1, bass.ds(k, 1)], min_val=0, max_val=E - 1)
                    dve.wait_ge(down_done, 2 + k + 1)
                    dve.wait_ge(y_out[l % 2], n * (RX // 2 * 16) + l // 2 * 16)
                    nc.vector.scalar_tensor_tensor(out=ys[:, l % 2, :], in0=py[l % 2][:], scalar=0.5,
                                                   in1=b2[:, bass.ds(e * DM, DM)], op0=ALU.mult,
                                                   op1=ALU.add).then_inc(y_done, 1)

                def body(n, more):
                    for l in range(RX):
                        if l < RX - 1:
                            hidden(n, l + 1)
                        elif more:
                            hidden(n + 1, 0)
                        output(n, l)

                hidden(0, 0)
                with dve.Fori(0, ST // RX - 1) as n:
                    body(n, True)
                body(ST // RX - 1, False)

            @block.gpsimd
            def _(pool):
                with pool.Fori(0, ST // 2) as n:
                    for l in range(2):
                        pool.wait_ge(y_done, 2 + n * 2 + l + 1)
                        pool.dma_start(y_dram[bass.ds(n * (2 * P) + l * P, P), :], ys[:, l, :]).then_inc(y_out[l], 16)
                for l in range(2):
                    pool.wait_ge(y_out[l], ST // 2 * 16)


def combine(nc, rows_bc, gates, slots, x1_dram, y_dram, out):
    R = 4
    with ExitStack() as ctx:
        m = Mem(nc, ctx)
        xt = m.sb("c_xt", [P, R, DM])
        y = m.sb("c_y", [P, R, 2, DM])
        acc = m.sb("c_acc", [P, R, DM])
        where = m.sb("c_where", [P, R, 2], U32)
        weight = m.sb("c_weight", [P, R, 2])
        x_in = [m.sem(f"cx_in{k}") for k in range(R)]
        y_in = [m.sem(f"cy_in{k}") for k in range(R)]
        where_done = m.sem("c_where_done")
        weight_done = m.sem("weight_done")
        first_done = m.sem("first_done")
        both_done = m.sem("c_both_done")
        scaled = m.sem("scaled")
        sum_done = m.sem("sum_done")
        out_done = [m.sem(f"c_out{k}") for k in range(R)]

        with nc.Block() as block:

            @block.sync
            def _(sp):
                with sp.Fori(0, NT // R) as n:
                    for l in range(R):
                        sp.wait_ge(sum_done, n * R + l + 1)
                        sp.dma_start(xt[:, l, :], x1_dram[bass.ds(n * (R * P) + l * P, P), :]).then_inc(x_in[l], 16)

            @block.gpsimd
            def _(pool):
                with pool.Fori(0, NT // R) as n:
                    for l in range(R):
                        k = n * R + l
                        pool.wait_ge(both_done, k + 1)
                        apart(pool, m.passed)
                        nc.gpsimd.tensor_copy(where[:, l:l + 1, :], slots[:, bass.ds(k, 1), :]).then_inc(where_done, 1)
                        nc.gpsimd.tensor_copy(weight[:, l, :].unsqueeze(2), gates[:, :, bass.ds(k, 1)]).then_inc(weight_done, 1)
                        pool.wait_ge(where_done, k + 1)
                        apart(pool, m.passed)
                        for j in range(2):
                            pool.indirect_dma_start(y[:, l, j, :], None, y_dram,
                                                    bass.IndirectOffsetOnAxis(ap=where[:, l, j:j + 1], axis=0),
                                                    bounds_check=ROWS - 1, oob_is_err=False).then_inc(y_in[l], 16)

            @block.vector
            def _(dve):
                dve.sem_inc(both_done, R)
                dve.sem_inc(sum_done, R)
                for b in range(B):
                    with dve.Fori(b * (NB // R), (b + 1) * (NB // R)) as n:
                        for l in range(R):
                            k = n * R + l
                            dve.wait_ge(y_in[l], (n + 1) * 32)
                            dve.wait_ge(weight_done, k + 1)
                            dve.wait_ge(out_done[l], n * 16)
                            nc.vector.tensor_scalar(acc[:, l, :], y[:, l, 0, :], weight[:, l, 0:1], None,
                                                    ALU.mult).then_inc(first_done, 1)
                            dve.wait_ge(first_done, k + 1)
                            nc.vector.scalar_tensor_tensor(out=acc[:, l, :], in0=y[:, l, 1, :], scalar=weight[:, l, 1:2],
                                                           in1=acc[:, l, :], op0=ALU.mult, op1=ALU.add).then_inc(both_done, 1)
                            dve.wait_ge(both_done, R + k + 1)
                            nc.vector.tensor_tensor(acc[:, l, :], acc[:, l, :], rows_bc[:, b, GB, :],
                                                    ALU.mult).then_inc(scaled, 1)
                            dve.wait_ge(scaled, k + 1)
                            dve.wait_ge(x_in[l], (n + 1) * 16)
                            nc.vector.tensor_tensor(acc[:, l, :], acc[:, l, :], xt[:, l, :], ALU.add).then_inc(sum_done, 1)

            @block.scalar
            def _(act):
                with act.Fori(0, NT // R) as n:
                    for l in range(R):
                        act.wait_ge(sum_done, R + n * R + l + 1)
                        act.dma_start(out[bass.ds(n * (R * P) + l * P, P), :], acc[:, l, :]).then_inc(out_done[l], 16)
                for l in range(R):
                    act.wait_ge(out_done[l], NT // R * 16)


def build(nc, x, wq_t, wk_t, wv_t, wo_t, gate_w_t, gate_b, gate_bias, w1_t, b1, w2_t, b2, c_t, wmod,
          ident, before, experts, tile_start, dist, slopes, out):
    def scratch(name, shape):
        return nc.dram_tensor(name, shape, F32, kind="Internal").ap()

    mod_dram = scratch("mod_dram", (6, B, DM))
    q_dram = scratch("q_dram", (UNITS, 2, P, S))
    k_dram = scratch("k_dram", (B, 2, P, S))
    o_dram = scratch("o_dram", (UNITS, NB, P, P))
    x1_dram = scratch("x1_dram", (NT * P, DM))
    h2_dram = scratch("h2_dram", (NT * P, DM))
    slot_dram = scratch("slot_dram", (ROWS, DM))
    y_dram = scratch("y_dram", (ROWS, DM))

    with ExitStack() as ctx:
        m = Mem(nc, ctx)
        rows_bc = m.sb("rows_bc", [P, B, 6, DM])
        modulation(nc, c_t, wmod, mod_dram, rows_bc)
        with nc.sbuf_tensor("v_all", [P, NT, P], F32) as v_all:
            projections(nc, x, wq_t, wk_t, wv_t, ident, rows_bc, v_all, q_dram, k_dram)
            attention(nc, q_dram, k_dram, o_dram, dist, slopes, ident, v_all, slot_dram)
        top_v = m.sb("top_v", [P, NT, 2])
        top_i = m.sb("top_i", [P, NT, 2])
        gates = m.sb("gates", [P, 2, NT])
        slots = m.sb("slots", [P, NT, 2], U32)
        tile_expert = m.sb("tile_expert", [P, ST], I32)
        with ExitStack() as inner:
            w = Mem(nc, inner)
            w1 = w.sb("w1", [P, C, E * HF])
            w2 = w.sb("w2", [P, len(HC), E * DM])
            b1_bc = w.sb("b1_bc", [P, E * HF])
            b2_bc = w.sb("b2_bc", [P, E * DM])
            w_in = w.sem("experts_in")
            zero_set = w.sem("zero_set")

            def fetch(sp):
                for c in range(C):
                    sp.dma_start(w1[:, c, :], w1_t[c * P:(c + 1) * P, :]).then_inc(w_in, 16)
                for c, (a, size) in enumerate(HC):
                    sp.dma_start(w2[0:size, c, :], w2_t[a:a + size, :]).then_inc(w_in, 16)
                sp.dma_start(b1_bc[:], b1.partition_broadcast(P)).then_inc(w_in, 16)
                sp.dma_start(b2_bc[:], b2.partition_broadcast(P)).then_inc(w_in, 16)

            weights_in = [(w_in, (C + len(HC) + 2) * 16), (zero_set, 1)]
            with nc.Block() as block:

                @block.vector
                def _(dve):
                    nc.vector.memset(w2[HC[-1][1]:P, len(HC) - 1, :], 0.0).then_inc(zero_set, 1)

            mix_and_gate(nc, x, o_dram, wo_t, gate_w_t, gate_b, gate_bias, ident, rows_bc, top_v, top_i,
                         x1_dram, h2_dram, fetch)
            route(nc, top_v, top_i, before, experts, tile_start, gates, slots, tile_expert, h2_dram, slot_dram)
            run_experts(nc, ident, w1, w2, b1_bc, b2_bc, weights_in, tile_expert, slot_dram, y_dram)
        combine(nc, rows_bc, gates, slots, x1_dram, y_dram, out)


def kernel(L0_attn_x, L0_attn_Wq, L0_attn_Wk, L0_attn_Wv, L0_attn_Wo, L0_ffn_gate_w, L0_ffn_gate_b, L0_ffn_bias,
           L0_ffn_w1, L0_ffn_b1, L0_ffn_w2, L0_ffn_b2, L0_c, L0_wmod):
    import concourse.bacc as bacc
    from concourse.bass_utils import run_bass_kernel_spmd

    def t(a):
        return np.ascontiguousarray(np.asarray(a).T)

    p = np.arange(P)[:, None]
    y = np.arange(S)[None, :]
    d = p + (NB - 1) * P - y
    dist = np.where(d >= 0, np.sqrt(np.maximum(d, 0).astype(np.float32)), np.float32(1e32)).astype(np.float32)
    slope = ((2.0 ** (-8.0 / H)) ** np.arange(1, H + 1)).astype(np.float32)
    slopes = np.zeros((P, (UNITS + 1) * REP), np.float32)
    slopes[:, :UNITS * REP] = np.tile(slope, B)[None]
    ins = {
        "x": np.asarray(L0_attn_x).reshape(NT * P, DM),
        "wq_t": t(L0_attn_Wq), "wk_t": t(L0_attn_Wk), "wv_t": t(L0_attn_Wv), "wo_t": t(L0_attn_Wo),
        "gate_w_t": t(L0_ffn_gate_w), "gate_b": np.asarray(L0_ffn_gate_b), "gate_bias": np.asarray(L0_ffn_bias),
        "w1_t": t(np.asarray(L0_ffn_w1).reshape(E * HF, DM)),
        "b1": np.asarray(L0_ffn_b1).reshape(E * HF),
        "w2_t": np.ascontiguousarray(np.asarray(L0_ffn_w2).transpose(2, 0, 1)).reshape(HF, E * DM),
        "b2": np.asarray(L0_ffn_b2).reshape(E * DM),
        "c_t": t(L0_c), "wmod": np.asarray(L0_wmod),
        "ident": np.eye(P, dtype=np.float32),
        "before": np.triu(np.ones((P, P), np.float32), 1),
        "experts": np.broadcast_to(np.arange(E, dtype=np.float32), (P, NT, E)).copy(),
        "tile_start": np.broadcast_to(np.arange(ST, dtype=np.float32) * P, (P, ST)).copy(),
        "dist": dist, "slopes": slopes,
    }
    nc = bacc.Bacc("TRN2", target_bir_lowering=False, num_devices=1)
    args = {n: nc.dram_tensor(n, a.shape, mybir.dt.from_np(a.dtype), kind="ExternalInput").ap() for n, a in ins.items()}
    out = nc.dram_tensor("out", (NT * P, DM), F32, kind="ExternalOutput").ap()
    build(nc, out=out, **args)
    r = run_bass_kernel_spmd(nc, [ins], core_ids=[0])
    return r.results[0]["out"].reshape(B, S, DM)
```

```python
from contextlib import ExitStack

import numpy as np

import concourse.bass as bass
from concourse import mybir

F32 = mybir.dt.float32
F32R = mybir.dt.float32r
I32 = mybir.dt.int32
U32 = mybir.dt.uint32
ALU = mybir.AluOpType
ACT = mybir.ActivationFunctionType
AX = mybir.AxisListType

P = 128
B, S, DM = 2, 2048, 512
H, G, D = 16, 4, 32
REP = H // G
C = DM // P
NB = S // P
NT = B * NB
SUP = 4
WIDE = SUP * P
UNITS = B * G
EPS = 1e-5
QSCALE = -1.0 / float(np.sqrt(D))
SA, CA, GA, SB, CB, GB = range(6)

E, HF = 8, 352
HC = [(0, 128), (128, 128), (256, 96)]
ROUTES = 2 * NT * P
ST = ROUTES // P + E
ROWS = ST * P


def apart(engine, sem):
    engine.sem_inc(sem, 1)


class Mem:

    def __init__(self, nc, ctx):
        self.nc, self.ctx, self.sems = nc, ctx, []
        ctx.callback(self.close)
        self.passed = self.sem(f"passed{nc.next_id()}")

    def sb(self, name, shape, dt=F32):
        return self.ctx.enter_context(self.nc.sbuf_tensor(name, shape, dt))

    def ps(self, name, shape):
        return self.ctx.enter_context(self.nc.psum_tensor(name, shape, F32))

    def sem(self, name):
        self.sems.append(self.nc.alloc_semaphore(name))
        return self.sems[-1]

    def close(self):
        self.nc.clear_and_free_semaphores(self.sems)
        self.nc.all_engine_barrier()


class LayerNorm:

    def __init__(self, m, name, size):
        self.size = size
        self.stats = m.sb(name + "_stats", [P, size, 6])
        self.mean = m.sb(name + "_mean", [P, size, 2])
        self.var = m.sb(name + "_var", [P, size])
        self.std = m.sb(name + "_std", [P, size])
        self.rstd = m.sb(name + "_rstd", [P, size])
        self.inv = m.sb(name + "_inv", [P, size])
        self.new = m.sb(name + "_new", [P, size])
        self.passed = m.passed
        self.bn_done = m.sem(name + "_bn_done")
        self.mean_done = m.sem(name + "_mean_done")
        self.var_done = m.sem(name + "_var_done")
        self.root_done = m.sem(name + "_root_done")
        self.newton = m.sem(name + "_newton")

    def statistics(self, nc, src, j):
        nc.vector.bn_stats(self.stats[:, j, :], src).then_inc(self.bn_done, 1)

    def deviation(self, nc, dve, t):
        size = self.size
        dve.wait_ge(self.bn_done, (t + 1) * size)
        apart(dve, self.passed)
        for j in range(size):
            nc.vector.bn_aggr(self.mean[:, j, :], self.stats[:, j, :]).then_inc(self.mean_done, 1)
        dve.wait_ge(self.mean_done, (t + 1) * size)
        nc.vector.tensor_scalar(self.var[:], self.mean[:, :, 1], EPS, None, ALU.add).then_inc(self.var_done, 1)
        dve.wait_ge(self.root_done, t + 1)
        steps = [
            lambda: nc.vector.reciprocal(self.inv[:], self.std[:]),
            lambda: nc.vector.tensor_tensor(self.new[:], self.inv[:], self.inv[:], ALU.mult),
            lambda: nc.vector.tensor_tensor(self.new[:], self.new[:], self.var[:], ALU.mult),
            lambda: nc.vector.tensor_scalar(self.new[:], self.new[:], -0.5, 1.5, ALU.mult, ALU.add),
            lambda: nc.vector.tensor_tensor(self.rstd[:, :], self.new[:], self.inv[:], ALU.mult),
        ]
        for k, step in enumerate(steps):
            step().then_inc(self.newton, 1)
            dve.wait_ge(self.newton, t * len(steps) + k + 1)

    def root(self, nc, act, t):
        act.wait_ge(self.var_done, t + 1)
        nc.scalar.activation(self.std[:], self.var[:], ACT.Sqrt).then_inc(self.root_done, 1)

    def centre(self, nc, out, src, j, factor):
        return nc.vector.scalar_tensor_tensor(out=out, in0=src, scalar=self.mean[:, j, 0:1], in1=factor,
                                              op0=ALU.subtract, op1=ALU.mult)

    def shift(self, nc, out, j, term):
        return nc.vector.scalar_tensor_tensor(out=out, in0=out, scalar=self.rstd[:, j:j + 1], in1=term,
                                              op0=ALU.mult, op1=ALU.add)


def row_of(rows_bc, n, v):
    return rows_bc[:, bass.ds(n // 2, 1), v, :].rearrange("p o n -> p (o n)")


def modulation(nc, c_t, wmod, mod_dram, rows_bc):
    with ExitStack() as ctx:
        m = Mem(nc, ctx)
        ct = m.sb("m_ct", [P, C, B])
        th = m.sb("m_th", [P, C, B])
        act_c = m.sb("m_act", [P, C, B])
        w = m.sb("m_w", [P, C, 6 * DM])
        row = m.sb("m_row", [P, 6, DM])
        mag = m.sb("m_mag", [P, 2, DM])
        sgn = m.sb("m_sgn", [P, 2, DM])
        pm = m.ps("m_pm", [P, 6, DM])
        c_in = m.sem("c_in")
        w_in = [m.sem(f"w_in{k}") for k in range(C)]
        tanh_done = m.sem("tanh_done")
        silu_step = m.sem("silu_step")
        mod_done = m.sem("mod_done")
        row_step = m.sem("row_step")
        rows_done = m.sem("rows_done")
        mod_out = m.sem("mod_out")
        bc_in = m.sem("bc_in")

        with nc.Block() as block:

            @block.sync
            def _(sp):
                sp.dma_start(ct[:], c_t.rearrange("(k p) b -> p k b", p=P)).then_inc(c_in, 16)
                for k in range(C):
                    sp.dma_start(w[:, k, :], wmod[k * P:(k + 1) * P, :]).then_inc(w_in[k], 16)
                sp.wait_ge(rows_done, 6)
                for v in range(6):
                    q = 32 * (v % 4)
                    sp.dma_start(mod_dram[v], row[q:q + B, v, :]).then_inc(mod_out, 16)
                sp.wait_ge(mod_out, 6 * 16)
                for v in range(6):
                    for b in range(B):
                        sp.dma_start(rows_bc[:, b, v, :], mod_dram[v, b, :].partition_broadcast(P)).then_inc(bc_in, 16)
                sp.wait_ge(bc_in, 6 * B * 16)

            @block.scalar
            def _(act):
                act.wait_ge(c_in, 16)
                nc.scalar.activation(th[:], ct[:], ACT.Tanh, scale=0.5).then_inc(tanh_done, 1)

            @block.vector
            def _(dve):
                dve.wait_ge(tanh_done, 1)
                nc.vector.scalar_tensor_tensor(out=act_c[:], in0=th[:], scalar=1.0, in1=ct[:],
                                               op0=ALU.add, op1=ALU.mult).then_inc(silu_step, 1)
                dve.wait_ge(silu_step, 1)
                nc.vector.tensor_scalar(act_c[:], act_c[:], 0.5, None, ALU.mult).then_inc(silu_step, 1)
                for v in range(6):
                    q = slice(32 * (v % 4), 32 * (v % 4) + B)
                    dve.wait_ge(mod_done, v + 1)
                    if v in (SA, SB):
                        nc.vector.tensor_copy(row[q, v, :], pm[q, v, :]).then_inc(rows_done, 1)
                    elif v in (CA, CB):
                        nc.vector.tensor_scalar(row[q, v, :], pm[q, v, :], 1.0, None, ALU.add).then_inc(rows_done, 1)
                    else:
                        k = v // 3
                        nc.vector.tensor_scalar(sgn[q, k, :], pm[q, v, :], 0.0, 2.0,
                                                ALU.is_ge, ALU.mult).then_inc(row_step, 1)
                        dve.wait_ge(row_step, 3 * k + 1)
                        nc.vector.scalar_tensor_tensor(out=mag[q, k, :], in0=sgn[q, k, :], scalar=-1.0,
                                                       in1=pm[q, v, :], op0=ALU.add, op1=ALU.mult).then_inc(row_step, 1)
                        dve.wait_ge(row_step, 3 * k + 2)
                        nc.vector.tensor_scalar(mag[q, k, :], mag[q, k, :], 0.25, None, ALU.max).then_inc(row_step, 1)
                        dve.wait_ge(row_step, 3 * k + 3)
                        nc.vector.scalar_tensor_tensor(out=row[q, v, :], in0=sgn[q, k, :], scalar=-1.0,
                                                       in1=mag[q, k, :], op0=ALU.add, op1=ALU.mult).then_inc(rows_done, 1)

            @block.tensor
            def _(pe):
                pe.wait_ge(silu_step, 2)
                for k in range(C):
                    pe.wait_ge(w_in[k], 16)
                for v in range(6):
                    q = 32 * (v % 4)
                    for k in range(C):
                        last = nc.tensor.matmul(pm[q:q + B, v, :], act_c[:, k, :], w[:, k, v * DM:(v + 1) * DM],
                                                start=(k == 0), stop=(k == C - 1), tile_position=(0, q))
                    last.then_inc(mod_done, 1)


def projections(nc, x, wq_t, wk_t, wv_t, ident, rows_bc, v_all, q_dram, k_dram):
    RX, RH, RT, RO, RS = 8, 4, 2, 4, 2
    BODY = 2 * SUP
    ITEMS = G + 2
    PAIRS = G + 1
    with ExitStack() as ctx:
        m = Mem(nc, ctx)
        wq = m.sb("p_wq", [P, C, DM])
        wk = m.sb("p_wk", [P, C, P])
        wv = m.sb("p_wv", [P, C, P])
        idn = m.sb("p_idn", [P, P])
        xt = m.sb("p_xt", [P, RX, DM])
        ln = LayerNorm(m, "p", SUP)
        hn = m.sb("p_hn", [P, RH, DM])
        ht = m.sb("p_ht", [P, 2, C, WIDE])
        hi = m.sb("p_hi", [P, RS, WIDE], F32R)
        lo = m.sb("p_lo", [P, RS, WIDE], F32R)
        tp = [m.ps(f"p_tp{k}", [P, C, P]) for k in range(RT)]
        po = [m.ps(f"p_po{k}", [P, WIDE]) for k in range(RO)]

        weights_in = m.sem("weights_in")
        x_in = [m.sem(f"x_in{k}") for k in range(RX)]
        norm_done = m.sem("norm_done")
        h_done = m.sem("h_done")
        tp_done = m.sem("tp_done")
        ht_done = m.sem("ht_done")
        out_done = m.sem("out_done")
        hi_done = m.sem("hi_done")
        lo_done = m.sem("lo_done")
        v_done = m.sem("v_done")
        stage_out = [m.sem(f"stage_out{k}") for k in range(RS)]

        with nc.Block() as block:

            @block.sync
            def _(sp):
                sp.dma_start(idn[:], ident).then_inc(weights_in, 16)
                sp.dma_start(wq[:], wq_t.rearrange("(k p) n -> p k n", p=P)).then_inc(weights_in, 16)
                sp.dma_start(wk[:], wk_t.rearrange("(k p) n -> p k n", p=P)).then_inc(weights_in, 16)
                sp.dma_start(wv[:], wv_t.rearrange("(k p) n -> p k n", p=P)).then_inc(weights_in, 16)
                with sp.Fori(0, NT // BODY) as n:
                    for l in range(BODY):
                        sp.wait_ge(norm_done, n * BODY + l + 1)
                        sp.dma_start(xt[:, l % RX, :], x[bass.ds(n * (BODY * P) + l * P, P), :])\
                          .then_inc(x_in[l % RX], 16)

            @block.vector
            def _(dve):
                dve.sem_inc(norm_done, RX)
                dve.sem_inc(lo_done, PAIRS)

                def norm(n, l):
                    dve.wait_ge(tp_done, n * BODY + l + 1)
                    ln.centre(nc, hn[:, l % RH, :], xt[:, l % RX, :], l % SUP, row_of(rows_bc, n, CA)).then_inc(norm_done, 1)
                    dve.wait_ge(norm_done, RX + n * BODY + l + 1)
                    ln.shift(nc, hn[:, l % RH, :], l % SUP, row_of(rows_bc, n, SA)).then_inc(h_done, 1)

                def statistics(n, u):
                    for j in range(SUP):
                        l = u * SUP + j
                        dve.wait_ge(x_in[l % RX], (n + 1) * 16)
                        ln.statistics(nc, xt[:, l % RX, :], j)
                    ln.deviation(nc, dve, n * 2 + u)

                def split(n, u, item):
                    slot = (u * PAIRS + item) % RS
                    bank = (u * ITEMS + item) % RO
                    dve.wait_ge(hi_done, n * (2 * PAIRS) + u * PAIRS + item + 1)
                    nc.vector.scalar_tensor_tensor(out=lo[:, slot, :], in0=po[bank][:],
                                                   scalar=QSCALE if item < G else 1.0,
                                                   in1=hi[:, slot, :].bitcast(F32), op0=ALU.mult,
                                                   op1=ALU.subtract).then_inc(lo_done, 1)

                def body(n, more):
                    for u in range(2):
                        ahead = u == 0 or more
                        after = (n, 1) if u == 0 else (n + 1, 0)
                        if ahead:
                            statistics(*after)
                        for item in range(PAIRS):
                            if ahead and item < SUP:
                                norm(after[0], after[1] * SUP + item)
                            split(n, u, item)

                statistics(0, 0)
                for j in range(SUP):
                    norm(0, j)
                with dve.Fori(0, NT // BODY - 1) as n:
                    body(n, True)
                body(NT // BODY - 1, False)

            @block.scalar
            def _(act):
                act.sem_inc(ht_done, RT)
                act.sem_inc(v_done, 1)
                for slot in range(RS):
                    act.sem_inc(stage_out[slot], 32)

                def transposed(n, l):
                    k = n * BODY + l
                    u, j = divmod(l, SUP)
                    act.wait_ge(tp_done, RH + k + 1)
                    if j == 0:
                        act.wait_ge(out_done, (n * 2 + u + 1) * ITEMS)
                    nc.scalar.activation(ht[:, u, :, j * P:(j + 1) * P], tp[l % RT][:], ACT.Copy).then_inc(ht_done, 1)

                def high(n, u, item):
                    slot = (u * PAIRS + item) % RS
                    bank = (u * ITEMS + item) % RO
                    act.wait_ge(out_done, 2 * ITEMS + (n * 2 + u) * ITEMS + item + 1)
                    act.wait_ge(stage_out[slot], n * (PAIRS * 32) + ((u * PAIRS + item) // RS + 1) * 32)
                    nc.scalar.activation(hi[:, slot, :], po[bank][:], ACT.Copy,
                                         scale=QSCALE if item < G else 1.0).then_inc(hi_done, 1)
                    act.wait_ge(hi_done, n * (2 * PAIRS) + u * PAIRS + item + 1)
                    act.wait_ge(lo_done, PAIRS + n * (2 * PAIRS) + u * PAIRS + item + 1)
                    for half, src in ((0, hi), (1, lo)):
                        if item < G:
                            dst = q_dram[bass.ds(n // 2 * G + item, 1), half, :,
                                         bass.ds(n % 2 * (BODY * P) + u * WIDE, WIDE)]
                            act.dma_start(dst.rearrange("o p t -> (o p) t"), src[:, slot, :].bitcast(F32))\
                               .then_inc(stage_out[slot], 16)
                        else:
                            dst = k_dram[bass.ds(n // 2, 1), half, :,
                                         bass.ds(n % 2 * (BODY * P) + u * WIDE, WIDE)]
                            act.dma_start(dst.rearrange("o p t -> (o p) t"), src[:, slot, :].bitcast(F32))\
                               .then_inc(stage_out[slot], 16)

                def values(n, u):
                    bank = (u * ITEMS + G + 1) % RO
                    act.wait_ge(out_done, 2 * ITEMS + (n * 2 + u + 1) * ITEMS)
                    nc.scalar.activation(v_all[:, bass.ds(n * BODY + u * SUP, SUP), :],
                                         po[bank][:].rearrange("p (j c) -> p j c", c=P), ACT.Copy).then_inc(v_done, 1)

                def body(n, more):
                    for u in range(2):
                        ahead = u == 0 or more
                        after = (n, SUP) if u == 0 else (n + 1, 0)
                        if ahead:
                            ln.root(nc, act, n * 2 + u + 1)
                        for item in range(PAIRS):
                            high(n, u, item)
                            if ahead and item < SUP:
                                transposed(after[0], after[1] + item)
                        values(n, u)

                ln.root(nc, act, 0)
                for l in range(SUP):
                    transposed(0, l)
                with act.Fori(0, NT // BODY - 1) as n:
                    body(n, True)
                body(NT // BODY - 1, False)
                for slot in range(RS):
                    act.wait_ge(stage_out[slot], 32 + NT // BODY * PAIRS * 32)

            @block.tensor
            def _(pe):
                pe.sem_inc(tp_done, RH)
                pe.sem_inc(out_done, 2 * ITEMS)
                pe.wait_ge(weights_in, 4 * 16)

                def transposes(n, l):
                    pe.wait_ge(h_done, n * BODY + l + 1)
                    pe.wait_ge(ht_done, n * BODY + l + 1)
                    for c in range(C):
                        last = nc.tensor.transpose(tp[l % RT][:, c, :], hn[:, l % RH, c * P:(c + 1) * P], idn[:])
                    last.then_inc(tp_done, 1)

                def project(n, u, item):
                    s = n * 2 + u
                    bank = (u * ITEMS + item) % RO
                    if item < RO - 1:
                        pe.wait_ge(lo_done, s * PAIRS + item + 3)
                    elif item == RO - 1:
                        pe.wait_ge(v_done, s + 1)
                    else:
                        pe.wait_ge(lo_done, PAIRS + s * PAIRS + item - RO + 1)
                    if item <= G:
                        for c in range(C):
                            w = wq[:, c, item * P:(item + 1) * P] if item < G else wk[:, c, :]
                            last = nc.tensor.matmul(po[bank][:], w, ht[:, u, c, :], start=(c == 0), stop=(c == C - 1))
                    else:
                        for j in range(SUP):
                            for c in range(C):
                                last = nc.tensor.matmul(po[bank][:, j * P:(j + 1) * P],
                                                        ht[:, u, c, j * P:(j + 1) * P], wv[:, c, :],
                                                        start=(c == 0), stop=(c == C - 1))
                    last.then_inc(out_done, 1)

                def body(n, more):
                    for u in range(2):
                        ahead = u == 0 or more
                        after = (n, SUP) if u == 0 else (n + 1, 0)
                        pe.wait_ge(ht_done, RT + n * BODY + (u + 1) * SUP)
                        for item in range(ITEMS):
                            project(n, u, item)
                            if ahead and item < SUP:
                                transposes(after[0], after[1] + item)

                for l in range(SUP):
                    transposes(0, l)
                with pe.Fori(0, NT // BODY - 1) as n:
                    body(n, True)
                body(NT // BODY - 1, False)


class Task:

    def __init__(self, number):
        self.number = number
        self.pi, self.r = divmod(number, REP)
        self.u, self.pair = divmod(self.pi, PAIRS_U)
        self.big, self.small = NB - 1 - self.pair, self.pair
        self.split = self.big + 1

    def half(self, h):
        if h < 2:
            return self.big, h * HALF, min(self.split * P, (h + 1) * HALF), h * HALF
        return self.small, 0, (self.small + 1) * P, self.split * P

    def key_block(self, b):
        return (0, b) if b < self.split else (1, b - self.split)


HALF = 2 * WIDE
PAIRS_U = NB // 2
GROUP_BLOCKS = [range(0, 4), range(4, 7), range(7, 11), range(11, 14), range(14, 17)]
EXP_AFTER = (0, 2)
OWNER = "ADADA"


def attention(nc, q_dram, k_dram, o_dram, dist, slopes, ident, v_all, slot_dram):
    PIS = 2 * PAIRS_U
    tasks = [Task(t) for t in range(PIS * REP)]
    NG = len(GROUP_BLOCKS)
    HALVES, GROUPS = 3 * len(tasks), NG * len(tasks)
    UNIT_HALVES, UNIT_GROUPS = HALVES // 2, GROUPS // 2
    BODIES = UNITS // 2
    XR, TR, PR = 4, 3, 5
    LAG = 3
    QL = 2
    LOADS = PAIRS_U // QL
    ZERO = ROWS * DM // P // (4 * UNITS)
    banks = []
    for task in tasks:
        banks += [(task.number, j) for j in range(NG)]
        if task.r == 1 and task.pi:
            banks.append((task.pi - 1, "sums"))
    banks.append((PIS - 1, "sums"))
    assert len(banks) % TR == 0 and GROUPS % PR == 0
    COPIES = {k: OWNER.count(k) * len(tasks) for k in "AD"}

    with ExitStack() as ctx:
        m = Mem(nc, ctx)
        idn = m.sb("a_idn", [P, P])
        dst = m.sb("a_dist", [P, S])
        slope_all = m.sb("a_slope_all", [P, UNITS * REP])
        slope = m.sb("a_slope", [P, 2, REP])
        bias = m.sb("a_bias", [P, 2, REP, S])
        vcur = m.sb("a_vcur", [P, 2, NB, D])
        kp = m.sb("a_kp", [P, 2, S], F32R)
        qp = m.sb("a_qp", [P, 2, REP, 2, QL * P], F32R)
        xs = m.sb("a_xs", [P, XR, S + P])
        zeros = m.sb("a_zeros", [P, ZERO])
        pt = m.sb("a_pt", [P, PR, WIDE])
        mn = m.sb("a_mn", [P, XR, 3])
        sums = m.sb("a_sums", [P, 2, 2, REP])
        rec = m.sb("a_rec", [P, 2, 2, REP])
        recw = m.sb("a_recw", [P, 2, 2 * REP, D])
        rt = m.sb("a_rt", [P, 2, 2 * P])
        os = m.sb("a_os", [P, 2, 2 * P])
        sp_ps = [m.ps(f"a_s{k}", [P, HALF]) for k in range(2)]
        tp = [m.ps(f"a_t{k}", [P, WIDE]) for k in range(TR)]
        op = m.ps("a_o", [P, 2, P])

        const_in = m.sem("const_in")
        zeros_set = m.sem("zeros_set")
        zeros_out = m.sem("zeros_out")
        k_in = [m.sem(f"k_in{k}") for k in range(2)]
        q_in = [m.sem(f"q_in{k}") for k in range(2)]
        slope_done = m.sem("slope_done")
        bias_done = m.sem("bias_done")
        vcur_done = m.sem("vcur_done")
        qk_done = m.sem("qk_done")
        min_done = m.sem("min_done")
        exp_done = m.sem("exp_done")
        tr_done = m.sem("tr_done")
        copied = {k: m.sem("copied_" + k) for k in "AD"}
        pv_done = m.sem("pv_done")
        rec_done = m.sem("rec_done")
        recw_done = m.sem("recw_done")
        rtr_done = m.sem("rtr_done")
        rt_done = m.sem("rt_done")
        drained = m.sem("drained")
        o_done = m.sem("o_done")
        o_out = m.sem("o_out")
        stored = m.sem("stored")

        def at(i, count, event):
            return (i + 1) * count + event + 1

        def bank(*entry):
            return tp[banks.index(entry) % TR]

        slot_rows = slot_dram.rearrange("(p f) n -> p (f n)", p=P)

        with nc.Block() as block:

            @block.sync
            def _(sp):
                sp.dma_start(idn[:], ident).then_inc(const_in, 16)
                sp.dma_start(dst[:], dist).then_inc(const_in, 16)
                sp.dma_start(slope_all[:], slopes).then_inc(const_in, 16)

                def keys(i, u):
                    sp.wait_ge(qk_done, at(i, HALVES, (u + 1) * UNIT_HALVES - 1 - HALVES))
                    for s in range(4):
                        sp.dma_start(kp[s * D:(s + 1) * D, u, :].bitcast(F32),
                                     k_dram[bass.ds(i // 2, 1), s % 2, bass.ds(i % 2 * (2 * D) + u * D, D), :]
                                     .rearrange("o p t -> (o p) t")).then_inc(k_in[u], 16)

                def queries(i, u, l):
                    q = u * LOADS + l
                    sp.wait_ge(qk_done, at(i, HALVES, (q - 1) * QL * REP * 3 - 1))
                    for s in range(4):
                        for k, first in enumerate((NB - (l + 1) * QL, l * QL)):
                            sp.dma_start(qp[s * D:(s + 1) * D, q % 2, :, k, :].bitcast(F32),
                                         q_dram[bass.ds(i * 2 + u, 1), s // 2, :, first * P:(first + QL) * P]
                                         .rearrange("o (r d) t -> (o d) r t", d=D)).then_inc(q_in[q % 2], 16)

                with sp.Fori(0, BODIES) as i:
                    for u in range(2):
                        keys(i, u)
                        for l in range(LOADS):
                            queries(i, u, l)
                            if u == 0 and l == 1:
                                sp.wait_ge(zeros_set, 1)
                            if l % 2:
                                for z in range(2):
                                    sp.dma_start(slot_rows[:, bass.ds((i * 8 + u * 4 + l // 2 * 2 + z) * ZERO, ZERO)],
                                                 zeros[:]).then_inc(zeros_out, 16)
                sp.wait_ge(zeros_out, 4 * UNITS * 16)

            @block.gpsimd
            def _(pool):
                pool.sem_inc(recw_done, PIS)
                pool.sem_inc(stored, PIS)

                def tables(i, u, r):
                    unit = i * 2 + u
                    slot = u % 2
                    if r == 0:
                        pool.wait_ge(min_done, at(i, HALVES, (u + 1) * UNIT_HALVES - 1 - HALVES))
                        apart(pool, m.passed)
                        nc.gpsimd.tensor_copy(slope[:, slot, :], slope_all[:, bass.ds(unit * REP, REP)]).then_inc(slope_done, 1)
                        pool.wait_ge(slope_done, unit)
                        apart(pool, m.passed)
                    nc.gpsimd.tensor_scalar(bias[:, slot, r, :], dst[:], slope[:, slot, r:r + 1], None,
                                            ALU.mult).then_inc(bias_done, 1)

                def values(i, u):
                    pool.wait_ge(pv_done, at(i, GROUPS, (u + 1) * UNIT_GROUPS - 1 - GROUPS))
                    apart(pool, m.passed)
                    nc.gpsimd.tensor_copy(vcur[:, u, :, :],
                                          v_all[:, bass.ds(i // 2 * NB, NB), bass.ds(i % 2 * (2 * D) + u * D, D)])\
                      .then_inc(vcur_done, 1)

                def widen(i, pi):
                    pool.wait_ge(rec_done, at(i, PIS, pi))
                    pool.wait_ge(rtr_done, at(i, PIS, pi - 2))
                    apart(pool, m.passed)
                    nc.gpsimd.tensor_copy(recw[:, pi % 2, :, :],
                                          rec[:, pi % 2, :, :].rearrange("p s r -> p (s r)").unsqueeze(2)
                                          .broadcast_to([P, 2 * REP, D])).then_inc(recw_done, 1)

                def store(i, pi):
                    u, pair = divmod(pi, PAIRS_U)
                    pool.wait_ge(o_done, at(i, PIS, pi))
                    for k, qb in enumerate((NB - 1 - pair, pair)):
                        pool.dma_start(o_dram[bass.ds(i * 2 + u, 1), qb, :, :].rearrange("o p t -> (o p) t"),
                                       os[:, pi % 2, k * P:(k + 1) * P]).then_inc(o_out, 16)
                    pool.wait_ge(o_out, i * (PIS * 32) + (pi + 1) * 32)
                    pool.sem_inc(stored, 1)

                def body(i, more):
                    for pi in range(PIS):
                        u, pair = divmod(pi, PAIRS_U)
                        if pair in (1, 2, 4, 5) and (u == 0 or more):
                            tables(i, u + 1, pair * 2 // 3)
                        widen(i, pi)
                        if pi:
                            store(i, pi - 1)
                        if pair == PAIRS_U - 1 and u == 0:
                            values(i, 1)
                    store(i, PIS - 1)
                    if more:
                        values(i + 1, 0)

                pool.wait_ge(const_in, 3 * 16)
                values(0, 0)
                with pool.Fori(0, BODIES - 1) as i:
                    body(i, True)
                body(BODIES - 1, False)

            @block.vector
            def _(dve):
                dve.sem_inc(min_done, HALVES)
                dve.sem_inc(copied["D"], COPIES["D"])
                dve.sem_inc(rec_done, PIS)
                dve.sem_inc(drained, PIS)
                dve.sem_inc(o_done, PIS)

                def minimum(i, t, h):
                    task = tasks[t]
                    hs = t * 3 + h
                    qb, a, b, row = task.half(h)
                    x = t % XR
                    off = (NB - 1 - qb) * P
                    if task.pair == 0 and h == 0:
                        dve.wait_ge(bias_done, i * (2 * REP) + task.u * REP + task.r + 1)
                    dve.wait_ge(qk_done, at(i, HALVES, hs))
                    if h == 0:
                        dve.wait_ge(tr_done, at(i, GROUPS, (t - XR + 1) * NG - 1))
                    start = 3e38
                    if h == 1:
                        dve.wait_ge(min_done, at(i, HALVES, hs - 1))
                        start = mn[:, x, 0:1]
                    apart(dve, m.passed)
                    nc.vector.tensor_tensor_reduce(out=xs[:, x, row:row + b - a], in0=sp_ps[hs % 2][:, 0:b - a],
                                                   in1=bias[:, task.u, task.r, off + a:off + b], scale=1.0, scalar=start,
                                                   op0=ALU.add, op1=ALU.min, accum_out=mn[:, x, h:h + 1])\
                      .then_inc(min_done, 1)

                def copy(i, t, j):
                    g = t * NG + j
                    cols = len(GROUP_BLOCKS[j]) * P
                    dve.wait_ge(tr_done, at(i, GROUPS, g))
                    dve.wait_ge(pv_done, at(i, GROUPS, g - PR))
                    nc.vector.tensor_copy(pt[:, g % PR, 0:cols], bank(t, j)[:, 0:cols]).then_inc(copied["D"], 1)

                def reciprocal(i, pi):
                    k = pi % 2
                    dve.wait_ge(exp_done, i * (2 * len(tasks)) + (pi + 1) * REP * 2)
                    dve.wait_ge(recw_done, at(i, PIS, pi - 2))
                    nc.vector.reciprocal(rec[:, k, :, :], sums[:, k, :, :]).then_inc(rec_done, 1)

                def drain(i, pi):
                    dve.wait_ge(pv_done, at(i, GROUPS, (pi + 1) * REP * NG - 1))
                    dve.wait_ge(stored, at(i, PIS, pi - 2))
                    nc.vector.tensor_copy(os[:, pi % 2, :], op[:].rearrange("p s q -> p (s q)")).then_inc(drained, 1)

                def normalise(i, pi):
                    k = pi % 2
                    dve.wait_ge(rt_done, at(i, PIS, pi))
                    dve.wait_ge(drained, at(i, PIS, pi))
                    nc.vector.tensor_tensor(os[:, k, :], os[:, k, :], rt[:, k, :],
                                            ALU.mult).then_inc(o_done, 1)

                def body(i, more):
                    for t, task in enumerate(tasks):
                        for j in range(NG):
                            if OWNER[j] == "D":
                                copy(i, t, j)
                            if j % 2 == 0:
                                if t + 2 < len(tasks):
                                    minimum(i, t + 2, j // 2)
                                elif more:
                                    minimum(i + 1, t + 2 - len(tasks), j // 2)
                            if task.r == 0 and j == LAG - 1 and task.pi:
                                drain(i, task.pi - 1)
                        if task.r == REP - 1:
                            reciprocal(i, task.pi)
                        if task.r == 2 and task.pi:
                            normalise(i, task.pi - 1)
                    drain(i, PIS - 1)
                    normalise(i, PIS - 1)

                dve.wait_ge(const_in, 3 * 16)
                for r in range(REP):
                    nc.vector.tensor_scalar(bias[:, 0, r, :], dst[:], slope_all[:, r:r + 1], None,
                                            ALU.mult).then_inc(bias_done, 1)
                nc.vector.memset(zeros[:], 0.0).then_inc(zeros_set, 1)
                for t in range(2):
                    for h in range(3):
                        minimum(0, t, h)
                with dve.Fori(0, BODIES - 1) as i:
                    body(i, True)
                body(BODIES - 1, False)

            @block.scalar
            def _(act):
                act.sem_inc(copied["A"], COPIES["A"])
                act.sem_inc(rt_done, PIS)

                def exponentials(i, t, small):
                    task = tasks[t]
                    a, b = (task.split * P, S + P) if small else (0, task.split * P)
                    x = t % XR
                    act.wait_ge(min_done, at(i, HALVES, t * 3 + 1 + small))
                    if task.r == 0 and not small:
                        act.wait_ge(rec_done, at(i, PIS, task.pi - 2))
                    nc.scalar.activation(xs[:, x, a:b], xs[:, x, a:b], ACT.Exp, scale=-1.0,
                                         bias=mn[:, x, 1 + small:2 + small],
                                         accum_out=sums[:, task.pi % 2, small, task.r:task.r + 1]).then_inc(exp_done, 1)

                def copy(i, t, j):
                    g = t * NG + j
                    cols = len(GROUP_BLOCKS[j]) * P
                    act.wait_ge(tr_done, at(i, GROUPS, g))
                    act.wait_ge(pv_done, at(i, GROUPS, g - PR))
                    nc.scalar.activation(pt[:, g % PR, 0:cols], bank(t, j)[:, 0:cols], ACT.Copy).then_inc(copied["A"], 1)

                def reciprocals(i, pi):
                    act.wait_ge(rtr_done, at(i, PIS, pi))
                    act.wait_ge(o_done, at(i, PIS, pi - 2))
                    nc.scalar.activation(rt[:, pi % 2, :], bank(pi, "sums")[:, 0:2 * P], ACT.Copy).then_inc(rt_done, 1)

                def body(i, more):
                    for t, task in enumerate(tasks):
                        for j in range(NG):
                            if OWNER[j] == "A":
                                copy(i, t, j)
                            if j in EXP_AFTER:
                                if t + 1 < len(tasks):
                                    exponentials(i, t + 1, EXP_AFTER.index(j))
                                elif more:
                                    exponentials(i + 1, 0, EXP_AFTER.index(j))
                        if task.r == 1 and task.pi:
                            reciprocals(i, task.pi - 1)
                    reciprocals(i, PIS - 1)

                for small in range(2):
                    exponentials(0, 0, small)
                with act.Fori(0, BODIES - 1) as i:
                    body(i, True)
                body(BODIES - 1, False)

            @block.tensor
            def _(pe):
                pe.sem_inc(qk_done, HALVES)
                pe.sem_inc(tr_done, GROUPS)
                pe.sem_inc(pv_done, GROUPS)
                pe.sem_inc(rtr_done, PIS)
                pe.wait_ge(const_in, 3 * 16)

                def scores(i, t, h):
                    task = tasks[t]
                    hs = t * 3 + h
                    qb, a, b, _ = task.half(h)
                    q = task.pi // QL
                    if task.r == 0 and h == 0:
                        if task.pair == 0:
                            pe.wait_ge(k_in[task.u], (i + 1) * 64)
                        if task.pair % QL == 0:
                            pe.wait_ge(q_in[q % 2], i * (LOADS * 128) + (q // 2 + 1) * 128)
                    pe.wait_ge(min_done, at(i, HALVES, hs - 2))
                    for c in range(a, b, WIDE):
                        e = min(b, c + WIDE)
                        last = nc.tensor.matmul(sp_ps[hs % 2][:, c - a:e - a],
                                                qp[:, q % 2, task.r, h // 2, qb % QL * P:(qb % QL + 1) * P],
                                                kp[:, task.u, c:e], start=True, stop=True)
                    last.then_inc(qk_done, 1)

                def wait_bank(i, *entry):
                    at_entry = banks.index(entry) - TR
                    n, j = banks[at_entry]
                    if j == "sums":
                        pe.wait_ge(rt_done, at(i, PIS, n - (PIS if at_entry < 0 else 0)))
                    else:
                        wait_copy(i, n * NG + j - (GROUPS if at_entry < 0 else 0))

                def transposes(i, t, j):
                    blocks = GROUP_BLOCKS[j]
                    small, c = tasks[t].key_block(blocks[-1])
                    pe.wait_ge(exp_done, i * (2 * len(tasks)) + t * 2 + small + 1)
                    wait_bank(i, t, j)
                    for k, b in enumerate(blocks):
                        last = nc.tensor.transpose(bank(t, j)[:, k * P:(k + 1) * P],
                                                   xs[:, t % XR, b * P:(b + 1) * P], idn[:])
                    last.then_inc(tr_done, 1)

                def wait_copy(i, g):
                    t, j = divmod(g, NG)
                    who = OWNER[j]
                    pe.wait_ge(copied[who], at(i, COPIES[who], t * OWNER.count(who) + OWNER[:j].count(who)))

                def products(i, t, j):
                    task = tasks[t]
                    g = t * NG + j
                    wait_copy(i, g)
                    if j == 0 and task.r == 0:
                        pe.wait_ge(drained, at(i, PIS, task.pi - 1))
                        if task.pair == 0:
                            pe.wait_ge(vcur_done, i * 2 + task.u + 1)
                    for k, b in enumerate(GROUP_BLOCKS[j]):
                        small, c = task.key_block(b)
                        last = nc.tensor.matmul(op[task.r * D:(task.r + 1) * D, small, :],
                                                vcur[:, task.u, c, :], pt[:, g % PR, k * P:(k + 1) * P], start=(c == 0),
                                                stop=(c == (task.small if small else task.big)),
                                                tile_position=(0, task.r * D))
                    last.then_inc(pv_done, 1)

                def reciprocals(i, pi):
                    pe.wait_ge(recw_done, at(i, PIS, pi))
                    wait_bank(i, pi, "sums")
                    for k in range(2):
                        last = nc.tensor.transpose(bank(pi, "sums")[:, k * P:(k + 1) * P],
                                                   recw[:, pi % 2, k * REP:(k + 1) * REP, :].rearrange("p r d -> p (r d)"),
                                                   idn[:])
                    last.then_inc(rtr_done, 1)

                def body(i, more):
                    waiting = []
                    for t, task in enumerate(tasks):
                        for j, ahead in enumerate([None, (2, 1), None, (2, 2), (3, 0)]):
                            transposes(i, t, j)
                            waiting.append((t, j))
                            if len(waiting) > LAG and not (task.r == 0 and j == LAG and task.pi):
                                products(i, *waiting.pop(0))
                            if len(waiting) > LAG and task.r == 0 and j == LAG + 1:
                                products(i, *waiting.pop(0))
                            if ahead:
                                n, h = ahead
                                if t + n < len(tasks):
                                    scores(i, t + n, h)
                                elif more:
                                    scores(i + 1, t + n - len(tasks), h)
                        if task.r == 1 and task.pi:
                            reciprocals(i, task.pi - 1)
                    for w in waiting:
                        products(i, *w)
                    reciprocals(i, PIS - 1)

                for t in range(2):
                    for h in range(3):
                        scores(0, t, h)
                scores(0, 2, 0)
                with pe.Fori(0, BODIES - 1) as i:
                    body(i, True)
                body(BODIES - 1, False)


def mix_and_gate(nc, x, o_dram, wo_t, gate_w_t, gate_b, gate_bias, ident, rows_bc, top_v, top_i, x1_dram, h2_dram,
                 fetch):
    RX, RH, RT = 8, 4, 2
    BODY = 2 * SUP
    with ExitStack() as ctx:
        m = Mem(nc, ctx)
        idn = m.sb("g_idn", [P, P])
        wo = m.sb("g_wo", [P, B * G, DM])
        gw = m.sb("g_gw", [P, C, E])
        gb = m.sb("g_gb", [P, 2, E])
        gbs = m.sb("g_gbs", [P, E])
        ot = m.sb("g_ot", [P, SUP, G, P])
        xt = m.sb("g_xt", [P, RX, DM])
        hn = m.sb("g_hn", [P, RH, DM])
        ht = m.sb("g_ht", [P, RT, C, P])
        score = m.sb("g_score", [P, 2, E])
        best = m.sb("g_best", [P, 2, 8])
        index = m.sb("g_index", [P, 2, 8], U32)
        ln = LayerNorm(m, "g", SUP)
        pp = [m.ps(f"g_pp{k}", [P, DM]) for k in range(2)]
        tp = [m.ps(f"g_tp{k}", [P, C, P]) for k in range(RT)]
        pg = [m.ps(f"g_pg{k}", [P, DM]) for k in range(2)]

        wo_in = m.sem("wo_in")
        const_in = m.sem("g_const_in")
        wo_scaled = m.sem("wo_scaled")
        gbs_done = m.sem("gbs_done")
        o_in = [m.sem(f"o_in{k}") for k in range(SUP)]
        x_in = [m.sem(f"gx_in{k}") for k in range(RX)]
        proj_done = m.sem("proj_done")
        x1_done = m.sem("x1_done")
        x1_out = [m.sem(f"x1_out{k}") for k in range(RX)]
        norm_done = m.sem("g_norm_done")
        h_done = m.sem("g_h_done")
        h_out = [m.sem(f"h_out{k}") for k in range(RH)]
        tp_done = m.sem("g_tp_done")
        ht_done = m.sem("g_ht_done")
        gate_done = m.sem("gate_done")
        score_done = m.sem("score_done")
        best_done = m.sem("best_done")
        index_done = m.sem("index_done")
        kept_v = m.sem("kept_v")
        kept_i = m.sem("kept_i")

        with nc.Block() as block:

            @block.sync
            def _(sp):
                sp.dma_start(wo[:, 0:G, :], wo_t.rearrange("(g p) n -> p g n", p=P)).then_inc(wo_in, 16)
                sp.dma_start(wo[:, G:2 * G, :], wo_t.rearrange("(g p) n -> p g n", p=P)).then_inc(wo_in, 16)
                sp.dma_start(idn[:], ident).then_inc(const_in, 16)
                sp.dma_start(gw[:], gate_w_t.rearrange("(c p) e -> p c e", p=P)).then_inc(const_in, 16)
                sp.dma_start(gb[:, 0, :], gate_b.partition_broadcast(P)).then_inc(const_in, 16)
                sp.dma_start(gb[:, 1, :], gate_bias.partition_broadcast(P)).then_inc(const_in, 16)

                def load(n, l):
                    k = n * BODY + l
                    sp.wait_ge(proj_done, k + 1)
                    sp.dma_start(ot[:, l % SUP, :, :],
                                 o_dram[bass.ds(n // 2 * G, G), bass.ds(n % 2 * BODY + l, 1), :, :]
                                 .rearrange("g o p t -> p (g o) t")).then_inc(o_in[l % SUP], 16)
                    sp.wait_ge(x1_out[l % RX], (n + 1) * 16)
                    sp.wait_ge(norm_done, k + 1)
                    sp.dma_start(xt[:, l % RX, :], x[bass.ds(k * P, P), :]).then_inc(x_in[l % RX], 16)

                with sp.Fori(0, NT // BODY) as n:
                    for l in range(BODY):
                        load(n, l)
                    fetch(sp, n)

            @block.tensor
            def _(pe):
                pe.sem_inc(proj_done, SUP)
                pe.sem_inc(tp_done, RH)
                pe.sem_inc(gate_done, RT)
                pe.wait_ge(const_in, 4 * 16)
                pe.wait_ge(wo_scaled, B * G)

                def project(n, l):
                    k = n * BODY + l
                    pe.wait_ge(o_in[l % SUP], n * (BODY // SUP * 16) + (l // SUP + 1) * 16)
                    pe.wait_ge(x1_done, k + 1)
                    for g in range(G):
                        w = wo[:, bass.ds(n // 2 * G + g, 1), :].rearrange("p o n -> p (o n)")
                        last = nc.tensor.matmul(pp[l % 2][:], ot[:, l % SUP, g, :], w, start=(g == 0), stop=(g == G - 1))
                    last.then_inc(proj_done, 1)

                def transposes(n, l):
                    k = n * BODY + l
                    pe.wait_ge(h_done, k + 1)
                    pe.wait_ge(ht_done, k + 1)
                    for c in range(C):
                        last = nc.tensor.transpose(tp[l % RT][:, c, :], hn[:, l % RH, c * P:(c + 1) * P], idn[:])
                    last.then_inc(tp_done, 1)

                def gate(n, l):
                    k = n * BODY + l
                    pe.wait_ge(ht_done, RT + k + 1)
                    pe.wait_ge(score_done, k + 1)
                    for c in range(C):
                        last = nc.tensor.matmul(pg[l % 2][:, 0:E], ht[:, l % RT, c, :], gw[:, c, :],
                                                start=(c == 0), stop=(c == C - 1))
                    last.then_inc(gate_done, 1)

                def body(n, more):
                    for u in range(2):
                        ahead = u == 0 or more
                        after = (n, SUP) if u == 0 else (n + 1, 0)
                        for j in range(SUP):
                            transposes(n, u * SUP + j)
                            if ahead:
                                project(after[0], after[1] + j)
                            gate(n, u * SUP + j)

                for l in range(SUP):
                    project(0, l)
                with pe.Fori(0, NT // BODY - 1) as n:
                    body(n, True)
                body(NT // BODY - 1, False)

            @block.vector
            def _(dve):
                dve.sem_inc(x1_done, 2)
                dve.sem_inc(norm_done, RX)
                dve.sem_inc(score_done, 2)
                dve.wait_ge(wo_in, 2 * 16)
                for b in range(B):
                    for g in range(G):
                        nc.vector.tensor_tensor(wo[:, b * G + g, :], wo[:, b * G + g, :], rows_bc[:, b, GA, :],
                                                ALU.mult).then_inc(wo_scaled, 1)
                dve.wait_ge(const_in, 4 * 16)
                nc.vector.tensor_tensor(gbs[:], gb[:, 0, :], gb[:, 1, :], ALU.add).then_inc(gbs_done, 1)
                dve.wait_ge(gbs_done, 1)

                def residual(n, l):
                    k = n * BODY + l
                    dve.wait_ge(x_in[l % RX], (n + 1) * 16)
                    dve.wait_ge(proj_done, SUP + k + 1)
                    nc.vector.tensor_tensor(xt[:, l % RX, :], pp[l % 2][:], xt[:, l % RX, :], ALU.add).then_inc(x1_done, 1)
                    dve.wait_ge(x1_done, 2 + k + 1)
                    ln.statistics(nc, xt[:, l % RX, :], l % SUP)

                def norm(n, l):
                    k = n * BODY + l
                    dve.wait_ge(tp_done, k + 1)
                    dve.wait_ge(h_out[l % RH], n * (BODY // RH * 16) + (l // RH + 1) * 16)
                    ln.centre(nc, hn[:, l % RH, :], xt[:, l % RX, :], l % SUP, row_of(rows_bc, n, CB)).then_inc(norm_done, 1)
                    dve.wait_ge(norm_done, RX + k + 1)
                    ln.shift(nc, hn[:, l % RH, :], l % SUP, row_of(rows_bc, n, SB)).then_inc(h_done, 1)

                def choose(n, l):
                    k = n * BODY + l
                    s = l % 2
                    dve.wait_ge(gate_done, RT + k + 1)
                    nc.vector.tensor_tensor(score[:, s, :], pg[s][:, 0:E], gbs[:], ALU.add).then_inc(score_done, 1)
                    dve.wait_ge(score_done, 2 + k + 1)
                    apart(dve, m.passed)
                    nc.vector.max(best[:, s, :], score[:, s, :]).then_inc(best_done, 1)
                    dve.wait_ge(best_done, k + 1)
                    apart(dve, m.passed)
                    nc.vector.max_index(index[:, s, :], best[:, s, :], score[:, s, :]).then_inc(index_done, 1)
                    dve.wait_ge(index_done, k + 1)
                    nc.vector.tensor_copy(top_v[:, bass.ds(k, 1), :], best[:, s:s + 1, 0:2]).then_inc(kept_v, 1)
                    nc.vector.tensor_copy(top_i[:, bass.ds(k, 1), :], index[:, s:s + 1, 0:2]).then_inc(kept_i, 1)

                def body(n, more):
                    for u in range(2):
                        ahead = u == 0 or more
                        after = (n, SUP) if u == 0 else (n + 1, 0)
                        for j in range(SUP):
                            if ahead:
                                residual(after[0], after[1] + j)
                            choose(n, u * SUP + j)
                        if ahead:
                            ln.deviation(nc, dve, n * 2 + u + 1)
                            for j in range(SUP):
                                norm(after[0], after[1] + j)

                for l in range(SUP):
                    residual(0, l)
                ln.deviation(nc, dve, 0)
                for l in range(SUP):
                    norm(0, l)
                with dve.Fori(0, NT // BODY - 1) as n:
                    body(n, True)
                body(NT // BODY - 1, False)
                dve.wait_ge(kept_v, NT)
                dve.wait_ge(kept_i, NT)

            @block.scalar
            def _(act):
                act.sem_inc(ht_done, RT)
                for out in x1_out + h_out:
                    act.sem_inc(out, 16)

                def transposed(n, l):
                    k = n * BODY + l
                    act.wait_ge(tp_done, RH + k + 1)
                    act.wait_ge(gate_done, k + 1)
                    nc.scalar.activation(ht[:, l % RT, :, :], tp[l % RT][:], ACT.Copy).then_inc(ht_done, 1)
                    act.wait_ge(x1_done, 2 + k + 1)
                    act.dma_start(x1_dram[bass.ds(k * P, P), :], xt[:, l % RX, :]).then_inc(x1_out[l % RX], 16)
                    act.wait_ge(h_done, k + 1)
                    act.dma_start(h2_dram[bass.ds(k * P, P), :], hn[:, l % RH, :]).then_inc(h_out[l % RH], 16)

                def body(n, more):
                    for u in range(2):
                        for j in range(SUP):
                            transposed(n, u * SUP + j)
                        if u == 0 or more:
                            ln.root(nc, act, n * 2 + u + 1)

                ln.root(nc, act, 0)
                with act.Fori(0, NT // BODY - 1) as n:
                    body(n, True)
                body(NT // BODY - 1, False)
                for k in range(RX):
                    act.wait_ge(x1_out[k], 16 + NT // RX * 16)
                for k in range(RH):
                    act.wait_ge(h_out[k], 16 + NT // RH * 16)


def route(nc, top_v, top_i, before, experts, tile_start, gates, slots, tile_expert, h2_dram, slot_dram):
    RL = 4
    N = NT * E
    with ExitStack() as ctx:
        m = Mem(nc, ctx)
        tri = m.sb("r_tri", [P, P])
        ones = m.sb("r_ones", [P, P])
        iota = m.sb("r_iota", [P, NT, E])
        starts = m.sb("r_starts", [P, ST])
        mask = [m.sb(f"r_mask{k}", [P, NT, E]) for k in range(2)]
        both = m.sb("r_both", [P, NT, E])
        count = m.sb("r_count", [P, NT, E])
        upto = m.sb("r_upto", [P, NT, E])
        place = m.sb("r_place", [P, NT, E])
        hit = m.sb("r_hit", [P, NT, E])
        padded = m.sb("r_padded", [P, E])
        padded_i = m.sb("r_padded_i", [P, E], I32)
        ends = m.sb("r_ends", [P, E])
        begins = m.sb("r_begins", [P, E])
        slot_f = m.sb("r_slot_f", [P, NT])
        expert_f = m.sb("r_expert_f", [P, ST])
        diff = m.sb("r_diff", [P, NT])
        ratio = m.sb("r_ratio", [P, NT])
        one_more = m.sb("r_one_more", [P, NT])
        rows = m.sb("r_rows", [P, RL, DM])
        where = m.sb("r_where", [P, RL, 2], U32)
        rank_ps = m.ps("r_rank", [P, NT, E])
        total_ps = m.ps("r_total", [P, NT, E])

        const_in = m.sem("r_const_in")
        ones_set = m.sem("ones_set")
        step = m.sem("route_step")
        both_done = m.sem("both_done")
        ranked = m.sem("ranked")
        totalled = m.sem("totalled")
        diff_done = m.sem("diff_done")
        ratio_done = m.sem("ratio_done")
        slots_done = m.sem("slots_done")
        rows_in = [m.sem(f"rows_in{k}") for k in range(RL)]
        where_done = m.sem("where_done")
        scattered = [m.sem(f"scattered{k}") for k in range(RL)]

        with nc.Block() as block:

            @block.sync
            def _(sp):
                sp.dma_start(tri[:], before).then_inc(const_in, 16)
                sp.dma_start(iota[:], experts).then_inc(const_in, 16)
                sp.dma_start(starts[:], tile_start).then_inc(const_in, 16)

                def load(n, l):
                    sp.dma_start(rows[:, l, :], h2_dram[bass.ds(n * (RL * P) + l * P, P), :]).then_inc(rows_in[l], 16)

                for l in range(RL):
                    load(0, l)
                with sp.Fori(1, NT // RL) as n:
                    for l in range(RL):
                        sp.wait_ge(scattered[l], n * 32)
                        load(n, l)

            @block.tensor
            def _(pe):
                pe.wait_ge(const_in, 3 * 16)
                pe.wait_ge(ones_set, 1)
                pe.wait_ge(both_done, 1)
                flat = both[:].rearrange("p t e -> p (t e)")
                nc.tensor.matmul(rank_ps[:].rearrange("p t e -> p (t e)"), tri[:], flat, start=True, stop=True).then_inc(ranked, 1)
                nc.tensor.matmul(total_ps[:].rearrange("p t e -> p (t e)"), ones[:], flat, start=True, stop=True).then_inc(totalled, 1)

            @block.scalar
            def _(act):
                act.wait_ge(diff_done, 1)
                nc.scalar.activation(ratio[:], diff[:], ACT.Exp).then_inc(ratio_done, 1)

            @block.vector
            def _(dve):
                done = [0]

                def then(ins):
                    done[0] += 1
                    ins.then_inc(step, 1)
                    dve.wait_ge(step, done[0])

                nc.vector.memset(ones[:], 1.0).then_inc(ones_set, 1)
                nc.vector.tensor_tensor(diff[:], top_v[:, :, 1], top_v[:, :, 0], ALU.subtract).then_inc(diff_done, 1)
                dve.wait_ge(const_in, 3 * 16)
                for k in range(2):
                    then(nc.vector.tensor_tensor(mask[k][:], iota[:], top_i[:, :, k].unsqueeze(2).broadcast_to([P, NT, E]),
                                                 ALU.is_equal))
                nc.vector.tensor_tensor(both[:], mask[0][:], mask[1][:], ALU.add).then_inc(both_done, 1)
                dve.wait_ge(ones_set, 1)
                dve.wait_ge(totalled, 1)
                then(nc.vector.tensor_copy(count[:], total_ps[:]))
                for e in range(E):
                    last = nc.vector.tensor_tensor_scan(out=upto[:, :, e], data0=ones[:, 0:NT], data1=count[:, :, e],
                                                        initial=0.0, op0=ALU.mult, op1=ALU.add)
                    then(last)
                then(nc.vector.tensor_scalar(padded_i[:], upto[:, NT - 1, :], float(P - 1), None, ALU.add))
                then(nc.vector.tensor_scalar(padded_i[:], padded_i[:], 7, 7, ALU.arith_shift_right, ALU.arith_shift_left))
                then(nc.vector.tensor_copy(padded[:], padded_i[:]))
                then(nc.vector.tensor_tensor_scan(out=ends[:], data0=ones[:, 0:E], data1=padded[:], initial=0.0,
                                                  op0=ALU.mult, op1=ALU.add))
                then(nc.vector.tensor_tensor(begins[:], ends[:], padded[:], ALU.subtract))
                then(nc.vector.tensor_tensor(place[:], upto[:], count[:], ALU.subtract))
                then(nc.vector.tensor_tensor(place[:], place[:], begins[:].unsqueeze(1).broadcast_to([P, NT, E]), ALU.add))
                dve.wait_ge(ranked, 1)
                then(nc.vector.tensor_tensor(place[:], rank_ps[:], place[:], ALU.add))
                for k in range(2):
                    then(nc.vector.tensor_tensor(hit[:], mask[k][:], place[:], ALU.mult))
                    then(nc.vector.tensor_reduce(slot_f[:], hit[:], AX.X, ALU.add))
                    nc.vector.tensor_copy(slots[:, :, k], slot_f[:]).then_inc(slots_done, 1)
                    dve.wait_ge(slots_done, k + 1)
                then(nc.vector.tensor_scalar(expert_f[:], starts[:], ends[:, 0:1], None, ALU.is_ge))
                for e in range(1, E - 1):
                    then(nc.vector.scalar_tensor_tensor(out=expert_f[:], in0=starts[:], scalar=ends[:, e:e + 1],
                                                        in1=expert_f[:], op0=ALU.is_ge, op1=ALU.add))
                then(nc.vector.tensor_copy(tile_expert[:], expert_f[:]))
                dve.wait_ge(ratio_done, 1)
                then(nc.vector.tensor_scalar(one_more[:], ratio[:], 1.0, None, ALU.add))
                then(nc.vector.reciprocal(gates[:, 0, :], one_more[:]))
                then(nc.vector.tensor_tensor(gates[:, 1, :], ratio[:], gates[:, 0, :], ALU.mult))

            @block.gpsimd
            def _(pool):
                pool.wait_ge(slots_done, 2)

                def scatter(n, l):
                    nc.gpsimd.tensor_copy(where[:, l:l + 1, :], slots[:, bass.ds(n * RL + l, 1), :]).then_inc(where_done, 1)
                    pool.wait_ge(where_done, n * RL + l + 1)
                    pool.wait_ge(rows_in[l], (n + 1) * 16)
                    apart(pool, m.passed)
                    for k in range(2):
                        pool.indirect_dma_start(slot_dram, bass.IndirectOffsetOnAxis(ap=where[:, l, k:k + 1], axis=0),
                                                rows[:, l, :], None, bounds_check=ROWS - 1,
                                                oob_is_err=False).then_inc(scattered[l], 16)

                for l in range(RL):
                    scatter(0, l)
                with pool.Fori(1, NT // RL) as n:
                    for l in range(RL):
                        pool.wait_ge(scattered[l], n * 32)
                        apart(pool, m.passed)
                        scatter(n, l)
                for l in range(RL):
                    pool.wait_ge(scattered[l], NT // RL * 32)


def run_experts(nc, ident, w1, w2, b1, b2, weights_in, tile_expert, slot_dram, y_dram):
    RX, RY = 4, 4
    PADH = len(HC) * P
    with ExitStack() as ctx:
        m = Mem(nc, ctx)
        idn = m.sb("e_idn", [P, P])
        xt = m.sb("e_xt", [P, RX, DM])
        xtt = m.sb("e_xtt", [P, 2, C, P])
        z = m.sb("e_z", [P, 2, HF])
        th = m.sb("e_th", [P, 2, HF])
        hz = m.sb("e_hz", [P, 2, PADH])
        hzt = m.sb("e_hzt", [P, 2, PADH])
        ys = m.sb("e_ys", [P, RY, DM])
        tx = [m.ps(f"e_tx{k}", [P, C, P]) for k in range(2)]
        thp = [m.ps(f"e_th{k}", [P, PADH]) for k in range(2)]
        pz = [m.ps(f"e_pz{k}", [P, DM]) for k in range(2)]
        py = [m.ps(f"e_py{k}", [P, DM]) for k in range(2)]

        idn_in = m.sem("e_idn_in")
        x_in = [m.sem(f"ex_in{k}") for k in range(RX)]
        tx_done = m.sem("tx_done")
        xtt_done = m.sem("xtt_done")
        up_done = m.sem("up_done")
        z_done = m.sem("z_done")
        tanh_done = m.sem("e_tanh_done")
        pad_set = m.sem("pad_set")
        hz_done = m.sem("hz_done")
        th_done = m.sem("th_done")
        hzt_done = m.sem("hzt_done")
        down_done = m.sem("down_done")
        y_done = m.sem("y_done")
        y_out = m.sem("y_out")
        stored = m.sem("y_stored")

        with nc.Block() as block:

            @block.sync
            def _(sp):
                sp.dma_start(idn[:], ident).then_inc(idn_in, 16)
                with sp.Fori(0, ST // RX) as n:
                    for l in range(RX):
                        sp.wait_ge(tx_done, n * RX + l + 1)
                        sp.dma_start(xt[:, l, :], slot_dram[bass.ds(n * (RX * P) + l * P, P), :]).then_inc(x_in[l], 16)

            @block.tensor
            def _(pe):
                pe.sem_inc(tx_done, RX)
                pe.sem_inc(up_done, 2)
                pe.sem_inc(th_done, 2)
                pe.sem_inc(down_done, 2)
                pe.wait_ge(idn_in, 16)
                for s in weights_in:
                    pe.wait_ge(*s)

                def transposes(n, l):
                    k = n * RX + l
                    pe.wait_ge(x_in[l], (n + 1) * 16)
                    pe.wait_ge(xtt_done, k + 1)
                    for c in range(C):
                        last = nc.tensor.transpose(tx[l % 2][:, c, :], xt[:, l, c * P:(c + 1) * P], idn[:])
                    last.then_inc(tx_done, 1)

                def up(n, l):
                    k = n * RX + l
                    e = nc.tensor.value_load(tile_expert[0:1, bass.ds(k, 1)], min_val=0, max_val=E - 1)
                    pe.wait_ge(xtt_done, 2 + k + 1)
                    pe.wait_ge(z_done, k + 1)
                    for c in range(C):
                        last = nc.tensor.matmul(pz[l % 2][:, 0:HF], xtt[:, l % 2, c, :], w1[:, c, bass.ds(e * HF, HF)],
                                                start=(c == 0), stop=(c == C - 1))
                    last.then_inc(up_done, 1)

                def turn(n, l):
                    k = n * RX + l
                    pe.wait_ge(hz_done, 2 + k + 1)
                    pe.wait_ge(hzt_done, k + 1)
                    for c in range(len(HC)):
                        last = nc.tensor.transpose(thp[l % 2][:, c * P:(c + 1) * P], hz[:, l % 2, c * P:(c + 1) * P], idn[:])
                    last.then_inc(th_done, 1)

                def down(n, l):
                    k = n * RX + l
                    e = nc.tensor.value_load(tile_expert[0:1, bass.ds(k, 1)], min_val=0, max_val=E - 1)
                    pe.wait_ge(hzt_done, 2 + k + 1)
                    pe.wait_ge(y_done, k + 1)
                    for c in range(len(HC)):
                        last = nc.tensor.matmul(py[l % 2][:], hzt[:, l % 2, c * P:(c + 1) * P], w2[:, c, bass.ds(e * DM, DM)],
                                                start=(c == 0), stop=(c == len(HC) - 1))
                    last.then_inc(down_done, 1)

                def body(n, more):
                    for l in range(RX):
                        ahead = l < RX - 1 or more
                        after = (n, l + 1) if l < RX - 1 else (n + 1, 0)
                        if ahead:
                            transposes(*after)
                        turn(n, l)
                        if ahead:
                            up(*after)
                        down(n, l)

                transposes(0, 0)
                up(0, 0)
                with pe.Fori(0, ST // RX - 1) as n:
                    body(n, True)
                body(ST // RX - 1, False)

            @block.scalar
            def _(act):
                act.sem_inc(xtt_done, 2)
                act.sem_inc(hzt_done, 2)

                def input_copy(n, l):
                    k = n * RX + l
                    act.wait_ge(tx_done, RX + k + 1)
                    act.wait_ge(up_done, k + 1)
                    nc.scalar.activation(xtt[:, l % 2, :, :], tx[l % 2][:], ACT.Copy).then_inc(xtt_done, 1)

                def hidden_copy(n, l):
                    k = n * RX + l
                    act.wait_ge(th_done, 2 + k + 1)
                    act.wait_ge(down_done, k + 1)
                    nc.scalar.activation(hzt[:, l % 2, :], thp[l % 2][:], ACT.Copy).then_inc(hzt_done, 1)

                def tanh(n, l):
                    k = n * RX + l
                    act.wait_ge(z_done, 2 + k + 1)
                    act.wait_ge(hz_done, k + 1)
                    nc.scalar.activation(th[:, l % 2, :], z[:, l % 2, :], ACT.Tanh, scale=0.5).then_inc(tanh_done, 1)

                def body(n, more):
                    for l in range(RX):
                        ahead = l < RX - 1 or more
                        after = (n, l + 1) if l < RX - 1 else (n + 1, 0)
                        if ahead:
                            input_copy(*after)
                        hidden_copy(n, l)
                        if ahead:
                            tanh(*after)

                input_copy(0, 0)
                tanh(0, 0)
                with act.Fori(0, ST // RX - 1) as n:
                    body(n, True)
                body(ST // RX - 1, False)

            @block.vector
            def _(dve):
                dve.sem_inc(z_done, 2)
                dve.sem_inc(y_done, 2)
                dve.sem_inc(hz_done, 2)
                nc.vector.memset(hz[:, :, HF:PADH], 0.0).then_inc(pad_set, 1)
                dve.wait_ge(pad_set, 1)
                for s in weights_in:
                    dve.wait_ge(*s)

                def hidden(n, l):
                    k = n * RX + l
                    e = nc.vector.value_load(tile_expert[0:1, bass.ds(k, 1)], min_val=0, max_val=E - 1)
                    dve.wait_ge(up_done, 2 + k + 1)
                    nc.vector.tensor_tensor(z[:, l % 2, :], pz[l % 2][:, 0:HF], b1[:, bass.ds(e * HF, HF)],
                                            ALU.add).then_inc(z_done, 1)
                    dve.wait_ge(tanh_done, k + 1)
                    dve.wait_ge(th_done, k + 1)
                    nc.vector.scalar_tensor_tensor(out=hz[:, l % 2, 0:HF], in0=th[:, l % 2, :], scalar=1.0,
                                                   in1=z[:, l % 2, :], op0=ALU.add, op1=ALU.mult).then_inc(hz_done, 1)

                def output(n, l):
                    k = n * RX + l
                    e = nc.vector.value_load(tile_expert[0:1, bass.ds(k, 1)], min_val=0, max_val=E - 1)
                    dve.wait_ge(down_done, 2 + k + 1)
                    dve.wait_ge(stored, k + 1)
                    nc.vector.scalar_tensor_tensor(out=ys[:, l % RY, :], in0=py[l % 2][:], scalar=0.5,
                                                   in1=b2[:, bass.ds(e * DM, DM)], op0=ALU.mult,
                                                   op1=ALU.add).then_inc(y_done, 1)

                def body(n, more):
                    for l in range(RX):
                        if l < RX - 1:
                            hidden(n, l + 1)
                        elif more:
                            hidden(n + 1, 0)
                        output(n, l)

                hidden(0, 0)
                with dve.Fori(0, ST // RX - 1) as n:
                    body(n, True)
                body(ST // RX - 1, False)

            @block.gpsimd
            def _(pool):
                pool.sem_inc(stored, RY)
                with pool.Fori(0, ST // RY) as n:
                    for l in range(RY):
                        k = n * RY + l
                        pool.wait_ge(y_done, 2 + k + 1)
                        pool.dma_start(y_dram[bass.ds(n * (RY * P) + l * P, P), :], ys[:, l, :]).then_inc(y_out, 16)
                        pool.wait_ge(y_out, (k + 1) * 16)
                        pool.sem_inc(stored, 1)


def combine(nc, rows_bc, gates, slots, x1_dram, y_dram, out):
    R = 4
    with ExitStack() as ctx:
        m = Mem(nc, ctx)
        xt = m.sb("c_xt", [P, R, DM])
        y = m.sb("c_y", [P, R, 2, DM])
        acc = m.sb("c_acc", [P, R, DM])
        where = m.sb("c_where", [P, R, 2], U32)
        weight = m.sb("c_weight", [P, R, 2])
        x_in = [m.sem(f"cx_in{k}") for k in range(R)]
        y_in = [m.sem(f"cy_in{k}") for k in range(R)]
        where_done = m.sem("c_where_done")
        weight_done = m.sem("weight_done")
        first_done = m.sem("first_done")
        both_done = m.sem("c_both_done")
        scaled = m.sem("scaled")
        sum_done = m.sem("sum_done")
        out_done = [m.sem(f"c_out{k}") for k in range(R)]

        with nc.Block() as block:

            @block.sync
            def _(sp):
                with sp.Fori(0, NT // R) as n:
                    for l in range(R):
                        sp.wait_ge(sum_done, n * R + l + 1)
                        sp.dma_start(xt[:, l, :], x1_dram[bass.ds(n * (R * P) + l * P, P), :]).then_inc(x_in[l], 16)

            @block.gpsimd
            def _(pool):
                with pool.Fori(0, NT // R) as n:
                    for l in range(R):
                        k = n * R + l
                        pool.wait_ge(both_done, k + 1)
                        apart(pool, m.passed)
                        nc.gpsimd.tensor_copy(where[:, l:l + 1, :], slots[:, bass.ds(k, 1), :]).then_inc(where_done, 1)
                        nc.gpsimd.tensor_copy(weight[:, l, :].unsqueeze(2), gates[:, :, bass.ds(k, 1)]).then_inc(weight_done, 1)
                        pool.wait_ge(where_done, k + 1)
                        apart(pool, m.passed)
                        for j in range(2):
                            pool.indirect_dma_start(y[:, l, j, :], None, y_dram,
                                                    bass.IndirectOffsetOnAxis(ap=where[:, l, j:j + 1], axis=0),
                                                    bounds_check=ROWS - 1, oob_is_err=False).then_inc(y_in[l], 16)

            @block.vector
            def _(dve):
                dve.sem_inc(both_done, R)
                dve.sem_inc(sum_done, R)
                for b in range(B):
                    with dve.Fori(b * (NB // R), (b + 1) * (NB // R)) as n:
                        for l in range(R):
                            k = n * R + l
                            dve.wait_ge(y_in[l], (n + 1) * 32)
                            dve.wait_ge(weight_done, k + 1)
                            dve.wait_ge(out_done[l], (n + 1) * 16)
                            nc.vector.tensor_scalar(acc[:, l, :], y[:, l, 0, :], weight[:, l, 0:1], None,
                                                    ALU.mult).then_inc(first_done, 1)
                            dve.wait_ge(first_done, k + 1)
                            nc.vector.scalar_tensor_tensor(out=acc[:, l, :], in0=y[:, l, 1, :], scalar=weight[:, l, 1:2],
                                                           in1=acc[:, l, :], op0=ALU.mult, op1=ALU.add).then_inc(both_done, 1)
                            dve.wait_ge(both_done, R + k + 1)
                            nc.vector.tensor_tensor(acc[:, l, :], acc[:, l, :], rows_bc[:, b, GB, :],
                                                    ALU.mult).then_inc(scaled, 1)
                            dve.wait_ge(scaled, k + 1)
                            dve.wait_ge(x_in[l], (n + 1) * 16)
                            nc.vector.tensor_tensor(acc[:, l, :], acc[:, l, :], xt[:, l, :], ALU.add).then_inc(sum_done, 1)

            @block.scalar
            def _(act):
                for l in range(R):
                    act.sem_inc(out_done[l], 16)
                with act.Fori(0, NT // R) as n:
                    for l in range(R):
                        act.wait_ge(sum_done, R + n * R + l + 1)
                        act.dma_start(out[bass.ds(n * (R * P) + l * P, P), :], acc[:, l, :]).then_inc(out_done[l], 16)
                for l in range(R):
                    act.wait_ge(out_done[l], 16 + NT // R * 16)


def build(nc, x, wq_t, wk_t, wv_t, wo_t, gate_w_t, gate_b, gate_bias, w1_t, b1, w2_t, b2, c_t, wmod,
          ident, before, experts, tile_start, dist, slopes, out):
    def scratch(name, shape):
        return nc.dram_tensor(name, shape, F32, kind="Internal").ap()

    mod_dram = scratch("mod_dram", (6, B, DM))
    q_dram = scratch("q_dram", (UNITS, 2, P, S))
    k_dram = scratch("k_dram", (B, 2, P, S))
    o_dram = scratch("o_dram", (UNITS, NB, P, P))
    x1_dram = scratch("x1_dram", (NT * P, DM))
    h2_dram = scratch("h2_dram", (NT * P, DM))
    slot_dram = scratch("slot_dram", (ROWS, DM))
    y_dram = scratch("y_dram", (ROWS, DM))

    with ExitStack() as ctx:
        m = Mem(nc, ctx)
        rows_bc = m.sb("rows_bc", [P, B, 6, DM])
        modulation(nc, c_t, wmod, mod_dram, rows_bc)
        with nc.sbuf_tensor("v_all", [P, NT, P], F32) as v_all:
            projections(nc, x, wq_t, wk_t, wv_t, ident, rows_bc, v_all, q_dram, k_dram)
            attention(nc, q_dram, k_dram, o_dram, dist, slopes, ident, v_all, slot_dram)
        top_v = m.sb("top_v", [P, NT, 2])
        top_i = m.sb("top_i", [P, NT, 2])
        gates = m.sb("gates", [P, 2, NT])
        slots = m.sb("slots", [P, NT, 2], U32)
        tile_expert = m.sb("tile_expert", [P, ST], I32)
        with ExitStack() as inner:
            w = Mem(nc, inner)
            w1 = w.sb("w1", [P, C, E * HF])
            w2 = w.sb("w2", [P, len(HC), E * DM])
            b1_bc = w.sb("b1_bc", [P, E * HF])
            b2_bc = w.sb("b2_bc", [P, E * DM])
            w_in = w.sem("experts_in")
            zero_set = w.sem("zero_set")

            def fetch(sp, n):
                sp.dma_start(w1[:, bass.ds(n, 1), :], w1_t[bass.ds(n * P, P), :].unsqueeze(1)).then_inc(w_in, 16)
                part = E * DM // C
                for c, (a, size) in enumerate(HC):
                    sp.dma_start(w2[0:size, c, bass.ds(n * part, part)],
                                 w2_t[a:a + size, bass.ds(n * part, part)]).then_inc(w_in, 16)
                sp.dma_start(b1_bc[:, bass.ds(n * (E * HF // C), E * HF // C)],
                             b1[bass.ds(n * (E * HF // C), E * HF // C)].partition_broadcast(P)).then_inc(w_in, 16)
                sp.dma_start(b2_bc[:, bass.ds(n * part, part)],
                             b2[bass.ds(n * part, part)].partition_broadcast(P)).then_inc(w_in, 16)

            weights_in = [(w_in, C * (len(HC) + 3) * 16), (zero_set, 1)]
            with nc.Block() as block:

                @block.vector
                def _(dve):
                    nc.vector.memset(w2[HC[-1][1]:P, len(HC) - 1, :], 0.0).then_inc(zero_set, 1)

            mix_and_gate(nc, x, o_dram, wo_t, gate_w_t, gate_b, gate_bias, ident, rows_bc, top_v, top_i,
                         x1_dram, h2_dram, fetch)
            route(nc, top_v, top_i, before, experts, tile_start, gates, slots, tile_expert, h2_dram, slot_dram)
            run_experts(nc, ident, w1, w2, b1_bc, b2_bc, weights_in, tile_expert, slot_dram, y_dram)
        combine(nc, rows_bc, gates, slots, x1_dram, y_dram, out)


def kernel(L0_attn_x, L0_attn_Wq, L0_attn_Wk, L0_attn_Wv, L0_attn_Wo, L0_ffn_gate_w, L0_ffn_gate_b, L0_ffn_bias,
           L0_ffn_w1, L0_ffn_b1, L0_ffn_w2, L0_ffn_b2, L0_c, L0_wmod):
    import concourse.bacc as bacc
    from concourse.bass_utils import run_bass_kernel_spmd

    def t(a):
        return np.ascontiguousarray(np.asarray(a).T)

    p = np.arange(P)[:, None]
    y = np.arange(S)[None, :]
    d = p + (NB - 1) * P - y
    dist = np.where(d >= 0, np.sqrt(np.maximum(d, 0).astype(np.float32)), np.float32(1e32)).astype(np.float32)
    slope = ((2.0 ** (-8.0 / H)) ** np.arange(1, H + 1)).astype(np.float32)
    slopes = np.broadcast_to(np.tile(slope, B), (P, UNITS * REP)).copy()
    ins = {
        "x": np.asarray(L0_attn_x).reshape(NT * P, DM),
        "wq_t": t(L0_attn_Wq), "wk_t": t(L0_attn_Wk), "wv_t": t(L0_attn_Wv), "wo_t": t(L0_attn_Wo),
        "gate_w_t": t(L0_ffn_gate_w), "gate_b": np.asarray(L0_ffn_gate_b), "gate_bias": np.asarray(L0_ffn_bias),
        "w1_t": t(np.asarray(L0_ffn_w1).reshape(E * HF, DM)),
        "b1": np.asarray(L0_ffn_b1).reshape(E * HF),
        "w2_t": np.ascontiguousarray(np.asarray(L0_ffn_w2).transpose(2, 0, 1)).reshape(HF, E * DM),
        "b2": np.asarray(L0_ffn_b2).reshape(E * DM),
        "c_t": t(L0_c), "wmod": np.asarray(L0_wmod),
        "ident": np.eye(P, dtype=np.float32),
        "before": np.triu(np.ones((P, P), np.float32), 1),
        "experts": np.broadcast_to(np.arange(E, dtype=np.float32), (P, NT, E)).copy(),
        "tile_start": np.broadcast_to(np.arange(ST, dtype=np.float32) * P, (P, ST)).copy(),
        "dist": dist, "slopes": slopes,
    }
    nc = bacc.Bacc("TRN2", target_bir_lowering=False, num_devices=1)
    args = {n: nc.dram_tensor(n, a.shape, mybir.dt.from_np(a.dtype), kind="ExternalInput").ap() for n, a in ins.items()}
    out = nc.dram_tensor("out", (NT * P, DM), F32, kind="ExternalOutput").ap()
    build(nc, out=out, **args)
    r = run_bass_kernel_spmd(nc, [ins], core_ids=[0])
    return r.results[0]["out"].reshape(B, S, DM)
```

```python
from contextlib import ExitStack

import numpy as np

import concourse.bass as bass
from concourse import mybir

F32 = mybir.dt.float32
F32R = mybir.dt.float32r
I32 = mybir.dt.int32
U32 = mybir.dt.uint32
F16 = mybir.dt.float16
ALU = mybir.AluOpType
ACT = mybir.ActivationFunctionType
AX = mybir.AxisListType

P = 128
B, S, DM = 2, 2048, 512
H, G, D = 16, 4, 32
REP = H // G
C = DM // P
NB = S // P
NT = B * NB
SUP = 4
WIDE = SUP * P
UNITS = B * G
EPS = 1e-5
QSCALE = -1.0 / float(np.sqrt(D))
SA, CA, GA, SB, CB, GB = range(6)

E, HF = 8, 352
HC = [(0, 128), (128, 128), (256, 96)]
ROUTES = 2 * NT * P
ST = ROUTES // P + E
ROWS = ST * P


def apart(engine, sem):
    engine.sem_inc(sem, 1)


class Mem:

    def __init__(self, nc, ctx):
        self.nc, self.ctx, self.sems = nc, ctx, []
        ctx.callback(self.close)
        self.passed = self.sem(f"passed{nc.next_id()}")

    def sb(self, name, shape, dt=F32):
        return self.ctx.enter_context(self.nc.sbuf_tensor(name, shape, dt))

    def ps(self, name, shape):
        return self.ctx.enter_context(self.nc.psum_tensor(name, shape, F32))

    def sem(self, name):
        self.sems.append(self.nc.alloc_semaphore(name))
        return self.sems[-1]

    def close(self):
        self.nc.clear_and_free_semaphores(self.sems)
        self.nc.all_engine_barrier()


class LayerNorm:

    def __init__(self, m, name, size):
        self.size = size
        self.stats = m.sb(name + "_stats", [P, size, 6])
        self.mean = m.sb(name + "_mean", [P, size, 2])
        self.var = m.sb(name + "_var", [P, size])
        self.std = m.sb(name + "_std", [P, size])
        self.rstd = m.sb(name + "_rstd", [P, size])
        self.inv = m.sb(name + "_inv", [P, size])
        self.new = m.sb(name + "_new", [P, size])
        self.passed = m.passed
        self.bn_done = m.sem(name + "_bn_done")
        self.mean_done = m.sem(name + "_mean_done")
        self.var_done = m.sem(name + "_var_done")
        self.root_done = m.sem(name + "_root_done")
        self.newton = m.sem(name + "_newton")

    def statistics(self, nc, src, j):
        nc.vector.bn_stats(self.stats[:, j, :], src).then_inc(self.bn_done, 1)

    def deviation(self, nc, dve, t):
        size = self.size
        dve.wait_ge(self.bn_done, (t + 1) * size)
        apart(dve, self.passed)
        for j in range(size):
            nc.vector.bn_aggr(self.mean[:, j, :], self.stats[:, j, :]).then_inc(self.mean_done, 1)
        dve.wait_ge(self.mean_done, (t + 1) * size)
        nc.vector.tensor_scalar(self.var[:], self.mean[:, :, 1], EPS, None, ALU.add).then_inc(self.var_done, 1)
        dve.wait_ge(self.root_done, t + 1)
        steps = [
            lambda: nc.vector.reciprocal(self.inv[:], self.std[:]),
            lambda: nc.vector.tensor_tensor(self.new[:], self.inv[:], self.inv[:], ALU.mult),
            lambda: nc.vector.tensor_tensor(self.new[:], self.new[:], self.var[:], ALU.mult),
            lambda: nc.vector.tensor_scalar(self.new[:], self.new[:], -0.5, 1.5, ALU.mult, ALU.add),
            lambda: nc.vector.tensor_tensor(self.rstd[:, :], self.new[:], self.inv[:], ALU.mult),
        ]
        for k, step in enumerate(steps):
            step().then_inc(self.newton, 1)
            dve.wait_ge(self.newton, t * len(steps) + k + 1)

    def root(self, nc, act, t):
        act.wait_ge(self.var_done, t + 1)
        nc.scalar.activation(self.std[:], self.var[:], ACT.Sqrt).then_inc(self.root_done, 1)

    def centre(self, nc, out, src, j, factor):
        return nc.vector.scalar_tensor_tensor(out=out, in0=src, scalar=self.mean[:, j, 0:1], in1=factor,
                                              op0=ALU.subtract, op1=ALU.mult)

    def shift(self, nc, out, j, term):
        return nc.vector.scalar_tensor_tensor(out=out, in0=out, scalar=self.rstd[:, j:j + 1], in1=term,
                                              op0=ALU.mult, op1=ALU.add)


def row_of(rows_bc, n, v):
    return rows_bc[:, bass.ds(n // 2, 1), v, :].rearrange("p o n -> p (o n)")


def modulation(nc, c_t, wmod, mod_dram, rows_bc, fetch, rest_in):
    with ExitStack() as ctx:
        m = Mem(nc, ctx)
        ct = m.sb("m_ct", [P, C, B])
        th = m.sb("m_th", [P, C, B])
        act_c = m.sb("m_act", [P, C, B])
        w = m.sb("m_w", [P, C, 6 * DM])
        row = m.sb("m_row", [P, 6, DM])
        mag = m.sb("m_mag", [P, 2, DM])
        sgn = m.sb("m_sgn", [P, 2, DM])
        pm = m.ps("m_pm", [P, 6, DM])
        c_in = m.sem("c_in")
        w_in = [m.sem(f"w_in{k}") for k in range(C)]
        tanh_done = m.sem("tanh_done")
        silu_step = m.sem("silu_step")
        mod_done = m.sem("mod_done")
        row_step = m.sem("row_step")
        rows_done = m.sem("rows_done")
        mod_out = m.sem("mod_out")
        bc_in = m.sem("bc_in")

        with nc.Block() as block:

            @block.sync
            def _(sp):
                sp.dma_start(ct[:], c_t.rearrange("(k p) b -> p k b", p=P)).then_inc(c_in, 16)
                for k in range(C):
                    sp.dma_start(w[:, k, :], wmod[k * P:(k + 1) * P, :]).then_inc(w_in[k], 16)
                fetch(sp)

                def spread(rows, arrived):
                    sp.wait_ge(rows_done, rows[-1] + 1)
                    for v in rows:
                        q = 32 * (v % 4)
                        sp.dma_start(mod_dram[v], row[q:q + B, v, :]).then_inc(mod_out, 16)
                    sp.wait_ge(mod_out, (rows[-1] + 1) * 16)
                    for v in rows:
                        for b in range(B):
                            sp.dma_start(rows_bc[:, b, v, :], mod_dram[v, b, :].partition_broadcast(P)).then_inc(arrived, 16)

                spread((SA, CA), bc_in)
                spread((GA, SB, CB, GB), rest_in)
                sp.wait_ge(bc_in, 2 * B * 16)

            @block.scalar
            def _(act):
                act.wait_ge(c_in, 16)
                nc.scalar.activation(th[:], ct[:], ACT.Tanh, scale=0.5).then_inc(tanh_done, 1)

            @block.vector
            def _(dve):
                dve.wait_ge(tanh_done, 1)
                nc.vector.scalar_tensor_tensor(out=act_c[:], in0=th[:], scalar=1.0, in1=ct[:],
                                               op0=ALU.add, op1=ALU.mult).then_inc(silu_step, 1)
                dve.wait_ge(silu_step, 1)
                nc.vector.tensor_scalar(act_c[:], act_c[:], 0.5, None, ALU.mult).then_inc(silu_step, 1)
                for v in range(6):
                    q = slice(32 * (v % 4), 32 * (v % 4) + B)
                    dve.wait_ge(mod_done, v + 1)
                    if v in (SA, SB):
                        nc.vector.tensor_copy(row[q, v, :], pm[q, v, :]).then_inc(rows_done, 1)
                    elif v in (CA, CB):
                        nc.vector.tensor_scalar(row[q, v, :], pm[q, v, :], 1.0, None, ALU.add).then_inc(rows_done, 1)
                    else:
                        k = v // 3
                        nc.vector.tensor_scalar(sgn[q, k, :], pm[q, v, :], 0.0, 2.0,
                                                ALU.is_ge, ALU.mult).then_inc(row_step, 1)
                        dve.wait_ge(row_step, 3 * k + 1)
                        nc.vector.scalar_tensor_tensor(out=mag[q, k, :], in0=sgn[q, k, :], scalar=-1.0,
                                                       in1=pm[q, v, :], op0=ALU.add, op1=ALU.mult).then_inc(row_step, 1)
                        dve.wait_ge(row_step, 3 * k + 2)
                        nc.vector.tensor_scalar(mag[q, k, :], mag[q, k, :], 0.25, None, ALU.max).then_inc(row_step, 1)
                        dve.wait_ge(row_step, 3 * k + 3)
                        nc.vector.scalar_tensor_tensor(out=row[q, v, :], in0=sgn[q, k, :], scalar=-1.0,
                                                       in1=mag[q, k, :], op0=ALU.add, op1=ALU.mult).then_inc(rows_done, 1)

            @block.tensor
            def _(pe):
                pe.wait_ge(silu_step, 2)
                for k in range(C):
                    pe.wait_ge(w_in[k], 16)
                    for v in range(6):
                        q = 32 * (v % 4)
                        last = nc.tensor.matmul(pm[q:q + B, v, :], act_c[:, k, :], w[:, k, v * DM:(v + 1) * DM],
                                                start=(k == 0), stop=(k == C - 1), tile_position=(0, q))
                        if k == C - 1:
                            last.then_inc(mod_done, 1)


RX_P = 8


def projections(nc, x, xt, x_in, wq, wk, wv, idn, weights_in, rest_in, rows_bc, v_all, q_dram, k_dram):
    RX, RH, RT, RO, RS = RX_P, 4, 2, 4, 2
    BODY = 2 * SUP
    ITEMS = G + 2
    PAIRS = G + 1
    with ExitStack() as ctx:
        m = Mem(nc, ctx)
        ln = LayerNorm(m, "p", SUP)
        hn = m.sb("p_hn", [P, RH, DM])
        ht = m.sb("p_ht", [P, 2, C, WIDE])
        hi = m.sb("p_hi", [P, RS, WIDE], F32R)
        lo = m.sb("p_lo", [P, RS, WIDE], F32R)
        tp = [m.ps(f"p_tp{k}", [P, C, P]) for k in range(RT)]
        po = [m.ps(f"p_po{k}", [P, WIDE]) for k in range(RO)]

        norm_done = m.sem("norm_done")
        h_done = m.sem("h_done")
        tp_done = m.sem("tp_done")
        ht_done = m.sem("ht_done")
        out_done = m.sem("out_done")
        hi_done = m.sem("hi_done")
        lo_done = m.sem("lo_done")
        v_done = m.sem("v_done")
        stage_out = [m.sem(f"stage_out{k}") for k in range(RS)]

        with nc.Block() as block:

            @block.sync
            def _(sp):
                sp.wait_ge(rest_in, 4 * B * 16)
                with sp.Fori(1, NT // BODY) as n:
                    for l in range(BODY):
                        sp.wait_ge(norm_done, n * BODY + l + 1)
                        sp.dma_start(xt[:, l % RX, :], x[bass.ds(n * (BODY * P) + l * P, P), :])\
                          .then_inc(x_in[l % RX], 16)

            @block.vector
            def _(dve):
                dve.sem_inc(norm_done, RX)
                dve.sem_inc(lo_done, PAIRS)

                def norm(n, l):
                    dve.wait_ge(tp_done, n * BODY + l + 1)
                    ln.centre(nc, hn[:, l % RH, :], xt[:, l % RX, :], l % SUP, row_of(rows_bc, n, CA)).then_inc(norm_done, 1)
                    dve.wait_ge(norm_done, RX + n * BODY + l + 1)
                    ln.shift(nc, hn[:, l % RH, :], l % SUP, row_of(rows_bc, n, SA)).then_inc(h_done, 1)

                def statistics(n, u):
                    for j in range(SUP):
                        l = u * SUP + j
                        dve.wait_ge(x_in[l % RX], (n + 1) * 16)
                        ln.statistics(nc, xt[:, l % RX, :], j)
                    ln.deviation(nc, dve, n * 2 + u)

                def split(n, u, item):
                    slot = (u * PAIRS + item) % RS
                    bank = (u * ITEMS + item) % RO
                    dve.wait_ge(hi_done, n * (2 * PAIRS) + u * PAIRS + item + 1)
                    nc.vector.scalar_tensor_tensor(out=lo[:, slot, :], in0=po[bank][:],
                                                   scalar=QSCALE if item < G else 1.0,
                                                   in1=hi[:, slot, :].bitcast(F32), op0=ALU.mult,
                                                   op1=ALU.subtract).then_inc(lo_done, 1)

                def body(n, more):
                    for u in range(2):
                        ahead = u == 0 or more
                        after = (n, 1) if u == 0 else (n + 1, 0)
                        if ahead:
                            statistics(*after)
                        for item in range(PAIRS):
                            if ahead and item < SUP:
                                norm(after[0], after[1] * SUP + item)
                            split(n, u, item)

                statistics(0, 0)
                for j in range(SUP):
                    norm(0, j)
                with dve.Fori(0, NT // BODY - 1) as n:
                    body(n, True)
                body(NT // BODY - 1, False)

            @block.scalar
            def _(act):
                act.sem_inc(ht_done, RT)
                act.sem_inc(v_done, 1)
                for slot in range(RS):
                    act.sem_inc(stage_out[slot], 32)

                def transposed(n, l):
                    k = n * BODY + l
                    u, j = divmod(l, SUP)
                    act.wait_ge(tp_done, RH + k + 1)
                    if j == 0:
                        act.wait_ge(out_done, (n * 2 + u + 1) * ITEMS)
                    nc.scalar.activation(ht[:, u, :, j * P:(j + 1) * P], tp[l % RT][:], ACT.Copy).then_inc(ht_done, 1)

                def high(n, u, item):
                    slot = (u * PAIRS + item) % RS
                    bank = (u * ITEMS + item) % RO
                    act.wait_ge(out_done, 2 * ITEMS + (n * 2 + u) * ITEMS + item + 1)
                    act.wait_ge(stage_out[slot], n * (PAIRS * 32) + ((u * PAIRS + item) // RS + 1) * 32)
                    nc.scalar.activation(hi[:, slot, :], po[bank][:], ACT.Copy,
                                         scale=QSCALE if item < G else 1.0).then_inc(hi_done, 1)
                    act.wait_ge(hi_done, n * (2 * PAIRS) + u * PAIRS + item + 1)
                    act.wait_ge(lo_done, PAIRS + n * (2 * PAIRS) + u * PAIRS + item + 1)
                    for half, src in ((0, hi), (1, lo)):
                        if item < G:
                            dst = q_dram[bass.ds(n // 2 * G + item, 1), half, :,
                                         bass.ds(n % 2 * (BODY * P) + u * WIDE, WIDE)]
                            act.dma_start(dst.rearrange("o p t -> (o p) t"), src[:, slot, :].bitcast(F32))\
                               .then_inc(stage_out[slot], 16)
                        else:
                            dst = k_dram[bass.ds(n // 2, 1), half, :,
                                         bass.ds(n % 2 * (BODY * P) + u * WIDE, WIDE)]
                            act.dma_start(dst.rearrange("o p t -> (o p) t"), src[:, slot, :].bitcast(F32))\
                               .then_inc(stage_out[slot], 16)

                def values(n, u):
                    bank = (u * ITEMS + G + 1) % RO
                    act.wait_ge(out_done, 2 * ITEMS + (n * 2 + u + 1) * ITEMS)
                    nc.scalar.activation(v_all[:, bass.ds(n * BODY + u * SUP, SUP), :],
                                         po[bank][:].rearrange("p (j c) -> p j c", c=P), ACT.Copy).then_inc(v_done, 1)

                def body(n, more):
                    for u in range(2):
                        ahead = u == 0 or more
                        after = (n, SUP) if u == 0 else (n + 1, 0)
                        if ahead:
                            ln.root(nc, act, n * 2 + u + 1)
                        for item in range(PAIRS):
                            high(n, u, item)
                            if ahead and item < SUP:
                                transposed(after[0], after[1] + item)
                        values(n, u)

                ln.root(nc, act, 0)
                for l in range(SUP):
                    transposed(0, l)
                with act.Fori(0, NT // BODY - 1) as n:
                    body(n, True)
                body(NT // BODY - 1, False)
                for slot in range(RS):
                    act.wait_ge(stage_out[slot], 32 + NT // BODY * PAIRS * 32)

            @block.tensor
            def _(pe):
                pe.sem_inc(tp_done, RH)
                pe.sem_inc(out_done, 2 * ITEMS)
                pe.wait_ge(weights_in, 4 * 16)

                def transposes(n, l):
                    pe.wait_ge(h_done, n * BODY + l + 1)
                    pe.wait_ge(ht_done, n * BODY + l + 1)
                    for c in range(C):
                        last = nc.tensor.transpose(tp[l % RT][:, c, :], hn[:, l % RH, c * P:(c + 1) * P], idn[:])
                    last.then_inc(tp_done, 1)

                def project(n, u, item):
                    s = n * 2 + u
                    bank = (u * ITEMS + item) % RO
                    if item < RO - 1:
                        pe.wait_ge(lo_done, s * PAIRS + item + 3)
                    elif item == RO - 1:
                        pe.wait_ge(v_done, s + 1)
                    else:
                        pe.wait_ge(lo_done, PAIRS + s * PAIRS + item - RO + 1)
                    if item <= G:
                        for c in range(C):
                            w = wq[:, c, item * P:(item + 1) * P] if item < G else wk[:, c, :]
                            last = nc.tensor.matmul(po[bank][:], w, ht[:, u, c, :], start=(c == 0), stop=(c == C - 1))
                    else:
                        for j in range(SUP):
                            for c in range(C):
                                last = nc.tensor.matmul(po[bank][:, j * P:(j + 1) * P],
                                                        ht[:, u, c, j * P:(j + 1) * P], wv[:, c, :],
                                                        start=(c == 0), stop=(c == C - 1))
                    last.then_inc(out_done, 1)

                def body(n, more):
                    for u in range(2):
                        ahead = u == 0 or more
                        after = (n, SUP) if u == 0 else (n + 1, 0)
                        pe.wait_ge(ht_done, RT + n * BODY + (u + 1) * SUP)
                        for item in range(ITEMS):
                            project(n, u, item)
                            if ahead and item < SUP:
                                transposes(after[0], after[1] + item)

                for l in range(SUP):
                    transposes(0, l)
                with pe.Fori(0, NT // BODY - 1) as n:
                    body(n, True)
                body(NT // BODY - 1, False)


class Task:

    def __init__(self, number):
        self.number = number
        self.pi, self.r = divmod(number, REP)
        self.u, self.pair = divmod(self.pi, PAIRS_U)
        self.big, self.small = NB - 1 - self.pair, self.pair
        self.split = self.big + 1

    def half(self, h):
        if h < 2:
            return self.big, h * HALF, min(self.split * P, (h + 1) * HALF), h * HALF
        return self.small, 0, (self.small + 1) * P, self.split * P

    def key_block(self, b):
        return (0, b) if b < self.split else (1, b - self.split)


HALF = 2 * WIDE
PAIRS_U = NB // 2
GROUP_BLOCKS = [range(0, 4), range(4, 7), range(7, 11), range(11, 14), range(14, 17)]
EXP_AFTER = (0, 2)
OWNER = "ADADA"


def attention(nc, q_dram, k_dram, o_dram, dist, slopes, ident, v_all):
    PIS = 2 * PAIRS_U
    tasks = [Task(t) for t in range(PIS * REP)]
    NG = len(GROUP_BLOCKS)
    HALVES, GROUPS = 3 * len(tasks), NG * len(tasks)
    UNIT_HALVES, UNIT_GROUPS = HALVES // 2, GROUPS // 2
    BODIES = UNITS // 2
    XR, TR, PR = 4, 3, 5
    LAG = 3
    QL = 2
    LOADS = PAIRS_U // QL
    banks = []
    for task in tasks:
        banks += [(task.number, j) for j in range(NG)]
        if task.r == 1 and task.pi:
            banks.append((task.pi - 1, "sums"))
    banks.append((PIS - 1, "sums"))
    assert len(banks) % TR == 0 and GROUPS % PR == 0
    COPIES = {k: OWNER.count(k) * len(tasks) for k in "AD"}

    with ExitStack() as ctx:
        m = Mem(nc, ctx)
        idn = m.sb("a_idn", [P, P])
        dst = m.sb("a_dist", [P, S])
        slope_all = m.sb("a_slope_all", [P, UNITS * REP])
        slope = m.sb("a_slope", [P, 2, REP])
        bias = m.sb("a_bias", [P, 2, REP, S])
        vcur = m.sb("a_vcur", [P, 2, NB, D])
        kp = m.sb("a_kp", [P, 2, S], F32R)
        qp = m.sb("a_qp", [P, 2, REP, 2, QL * P], F32R)
        xs = m.sb("a_xs", [P, XR, S + P])
        pt = m.sb("a_pt", [P, PR, WIDE])
        mn = m.sb("a_mn", [P, XR, 3])
        sums = m.sb("a_sums", [P, 2, 2, REP])
        rec = m.sb("a_rec", [P, 2, 2, REP])
        recw = m.sb("a_recw", [P, 2, 2 * REP, D])
        rt = m.sb("a_rt", [P, 2, 2 * P])
        os = m.sb("a_os", [P, 2, 2 * P])
        sp_ps = [m.ps(f"a_s{k}", [P, HALF]) for k in range(2)]
        tp = [m.ps(f"a_t{k}", [P, WIDE]) for k in range(TR)]
        op = m.ps("a_o", [P, 2, P])

        const_in = m.sem("const_in")
        k_in = [m.sem(f"k_in{k}") for k in range(2)]
        q_in = [m.sem(f"q_in{k}") for k in range(2)]
        slope_done = m.sem("slope_done")
        bias_done = m.sem("bias_done")
        vcur_done = m.sem("vcur_done")
        qk_done = m.sem("qk_done")
        min_done = m.sem("min_done")
        exp_done = m.sem("exp_done")
        tr_done = m.sem("tr_done")
        copied = {k: m.sem("copied_" + k) for k in "AD"}
        pv_done = m.sem("pv_done")
        rec_done = m.sem("rec_done")
        recw_done = m.sem("recw_done")
        rtr_done = m.sem("rtr_done")
        rt_done = m.sem("rt_done")
        drained = m.sem("drained")
        o_done = m.sem("o_done")
        o_out = m.sem("o_out")
        stored = m.sem("stored")

        def at(i, count, event):
            return (i + 1) * count + event + 1

        def bank(*entry):
            return tp[banks.index(entry) % TR]

        with nc.Block() as block:

            @block.sync
            def _(sp):
                sp.dma_start(idn[:], ident).then_inc(const_in, 16)
                sp.dma_start(dst[:], dist).then_inc(const_in, 16)
                sp.dma_start(slope_all[:], slopes).then_inc(const_in, 16)

                def keys(i, u):
                    sp.wait_ge(qk_done, at(i, HALVES, (u + 1) * UNIT_HALVES - 1 - HALVES))
                    for s in range(4):
                        sp.dma_start(kp[s * D:(s + 1) * D, u, :].bitcast(F32),
                                     k_dram[bass.ds(i // 2, 1), s % 2, bass.ds(i % 2 * (2 * D) + u * D, D), :]
                                     .rearrange("o p t -> (o p) t")).then_inc(k_in[u], 16)

                def queries(i, u, l):
                    q = u * LOADS + l
                    sp.wait_ge(qk_done, at(i, HALVES, (q - 1) * QL * REP * 3 - 1))
                    for s in range(4):
                        for k, first in enumerate((NB - (l + 1) * QL, l * QL)):
                            sp.dma_start(qp[s * D:(s + 1) * D, q % 2, :, k, :].bitcast(F32),
                                         q_dram[bass.ds(i * 2 + u, 1), s // 2, :, first * P:(first + QL) * P]
                                         .rearrange("o (r d) t -> (o d) r t", d=D)).then_inc(q_in[q % 2], 16)

                with sp.Fori(0, BODIES) as i:
                    for u in range(2):
                        keys(i, u)
                        for l in range(LOADS):
                            queries(i, u, l)

            @block.gpsimd
            def _(pool):
                pool.sem_inc(recw_done, PIS)
                pool.sem_inc(stored, PIS)

                def tables(i, u, r):
                    unit = i * 2 + u
                    slot = u % 2
                    if r == 0:
                        pool.wait_ge(min_done, at(i, HALVES, (u + 1) * UNIT_HALVES - 1 - HALVES))
                        apart(pool, m.passed)
                        nc.gpsimd.tensor_copy(slope[:, slot, :], slope_all[:, bass.ds(unit * REP, REP)]).then_inc(slope_done, 1)
                        pool.wait_ge(slope_done, unit)
                        apart(pool, m.passed)
                    nc.gpsimd.tensor_scalar(bias[:, slot, r, :], dst[:], slope[:, slot, r:r + 1], None,
                                            ALU.mult).then_inc(bias_done, 1)

                def values(i, u):
                    pool.wait_ge(pv_done, at(i, GROUPS, (u + 1) * UNIT_GROUPS - 1 - GROUPS))
                    apart(pool, m.passed)
                    nc.gpsimd.tensor_copy(vcur[:, u, :, :],
                                          v_all[:, bass.ds(i // 2 * NB, NB), bass.ds(i % 2 * (2 * D) + u * D, D)])\
                      .then_inc(vcur_done, 1)

                def widen(i, pi):
                    pool.wait_ge(rec_done, at(i, PIS, pi))
                    pool.wait_ge(rtr_done, at(i, PIS, pi - 2))
                    apart(pool, m.passed)
                    nc.gpsimd.tensor_copy(recw[:, pi % 2, :, :],
                                          rec[:, pi % 2, :, :].rearrange("p s r -> p (s r)").unsqueeze(2)
                                          .broadcast_to([P, 2 * REP, D])).then_inc(recw_done, 1)

                def store(i, pi):
                    u, pair = divmod(pi, PAIRS_U)
                    pool.wait_ge(o_done, at(i, PIS, pi))
                    for k, qb in enumerate((NB - 1 - pair, pair)):
                        pool.dma_start(o_dram[bass.ds(i * 2 + u, 1), qb, :, :].rearrange("o p t -> (o p) t"),
                                       os[:, pi % 2, k * P:(k + 1) * P]).then_inc(o_out, 16)
                    pool.wait_ge(o_out, i * (PIS * 32) + (pi + 1) * 32)
                    pool.sem_inc(stored, 1)

                def body(i, more):
                    for pi in range(PIS):
                        u, pair = divmod(pi, PAIRS_U)
                        if pair in (1, 2, 4, 5) and (u == 0 or more):
                            tables(i, u + 1, pair * 2 // 3)
                        widen(i, pi)
                        if pi:
                            store(i, pi - 1)
                        if pair == PAIRS_U - 1 and u == 0:
                            values(i, 1)
                    store(i, PIS - 1)
                    if more:
                        values(i + 1, 0)

                pool.wait_ge(const_in, 3 * 16)
                values(0, 0)
                with pool.Fori(0, BODIES - 1) as i:
                    body(i, True)
                body(BODIES - 1, False)

            @block.vector
            def _(dve):
                dve.sem_inc(min_done, HALVES)
                dve.sem_inc(copied["D"], COPIES["D"])
                dve.sem_inc(rec_done, PIS)
                dve.sem_inc(drained, PIS)
                dve.sem_inc(o_done, PIS)

                def minimum(i, t, h):
                    task = tasks[t]
                    hs = t * 3 + h
                    qb, a, b, row = task.half(h)
                    x = t % XR
                    off = (NB - 1 - qb) * P
                    if task.pair == 0 and h == 0:
                        dve.wait_ge(bias_done, i * (2 * REP) + task.u * REP + task.r + 1)
                    dve.wait_ge(qk_done, at(i, HALVES, hs))
                    if h == 0:
                        dve.wait_ge(tr_done, at(i, GROUPS, (t - XR + 1) * NG - 1))
                    start = 3e38
                    if h == 1:
                        dve.wait_ge(min_done, at(i, HALVES, hs - 1))
                        start = mn[:, x, 0:1]
                    apart(dve, m.passed)
                    nc.vector.tensor_tensor_reduce(out=xs[:, x, row:row + b - a], in0=sp_ps[hs % 2][:, 0:b - a],
                                                   in1=bias[:, task.u, task.r, off + a:off + b], scale=1.0, scalar=start,
                                                   op0=ALU.add, op1=ALU.min, accum_out=mn[:, x, h:h + 1])\
                      .then_inc(min_done, 1)

                def copy(i, t, j):
                    g = t * NG + j
                    cols = len(GROUP_BLOCKS[j]) * P
                    dve.wait_ge(tr_done, at(i, GROUPS, g))
                    dve.wait_ge(pv_done, at(i, GROUPS, g - PR))
                    nc.vector.tensor_copy(pt[:, g % PR, 0:cols], bank(t, j)[:, 0:cols]).then_inc(copied["D"], 1)

                def reciprocal(i, pi):
                    k = pi % 2
                    dve.wait_ge(exp_done, i * (2 * len(tasks)) + (pi + 1) * REP * 2)
                    dve.wait_ge(recw_done, at(i, PIS, pi - 2))
                    nc.vector.reciprocal(rec[:, k, :, :], sums[:, k, :, :]).then_inc(rec_done, 1)

                def drain(i, pi):
                    dve.wait_ge(pv_done, at(i, GROUPS, (pi + 1) * REP * NG - 1))
                    dve.wait_ge(stored, at(i, PIS, pi - 2))
                    nc.vector.tensor_copy(os[:, pi % 2, :], op[:].rearrange("p s q -> p (s q)")).then_inc(drained, 1)

                def normalise(i, pi):
                    k = pi % 2
                    dve.wait_ge(rt_done, at(i, PIS, pi))
                    dve.wait_ge(drained, at(i, PIS, pi))
                    nc.vector.tensor_tensor(os[:, k, :], os[:, k, :], rt[:, k, :],
                                            ALU.mult).then_inc(o_done, 1)

                def body(i, more):
                    for t, task in enumerate(tasks):
                        for j in range(NG):
                            if OWNER[j] == "D":
                                copy(i, t, j)
                            if j % 2 == 0:
                                if t + 2 < len(tasks):
                                    minimum(i, t + 2, j // 2)
                                elif more:
                                    minimum(i + 1, t + 2 - len(tasks), j // 2)
                            if task.r == 0 and j == LAG - 1 and task.pi:
                                drain(i, task.pi - 1)
                        if task.r == REP - 1:
                            reciprocal(i, task.pi)
                        if task.r == 2 and task.pi:
                            normalise(i, task.pi - 1)
                    drain(i, PIS - 1)
                    normalise(i, PIS - 1)

                dve.wait_ge(const_in, 3 * 16)
                for r in range(REP):
                    nc.vector.tensor_scalar(bias[:, 0, r, :], dst[:], slope_all[:, r:r + 1], None,
                                            ALU.mult).then_inc(bias_done, 1)
                for t in range(2):
                    for h in range(3):
                        minimum(0, t, h)
                with dve.Fori(0, BODIES - 1) as i:
                    body(i, True)
                body(BODIES - 1, False)

            @block.scalar
            def _(act):
                act.sem_inc(copied["A"], COPIES["A"])
                act.sem_inc(rt_done, PIS)

                def exponentials(i, t, small):
                    task = tasks[t]
                    a, b = (task.split * P, S + P) if small else (0, task.split * P)
                    x = t % XR
                    act.wait_ge(min_done, at(i, HALVES, t * 3 + 1 + small))
                    if task.r == 0 and not small:
                        act.wait_ge(rec_done, at(i, PIS, task.pi - 2))
                    nc.scalar.activation(xs[:, x, a:b], xs[:, x, a:b], ACT.Exp, scale=-1.0,
                                         bias=mn[:, x, 1 + small:2 + small],
                                         accum_out=sums[:, task.pi % 2, small, task.r:task.r + 1]).then_inc(exp_done, 1)

                def copy(i, t, j):
                    g = t * NG + j
                    cols = len(GROUP_BLOCKS[j]) * P
                    act.wait_ge(tr_done, at(i, GROUPS, g))
                    act.wait_ge(pv_done, at(i, GROUPS, g - PR))
                    nc.scalar.activation(pt[:, g % PR, 0:cols], bank(t, j)[:, 0:cols], ACT.Copy).then_inc(copied["A"], 1)

                def reciprocals(i, pi):
                    act.wait_ge(rtr_done, at(i, PIS, pi))
                    act.wait_ge(o_done, at(i, PIS, pi - 2))
                    nc.scalar.activation(rt[:, pi % 2, :], bank(pi, "sums")[:, 0:2 * P], ACT.Copy).then_inc(rt_done, 1)

                def body(i, more):
                    for t, task in enumerate(tasks):
                        for j in range(NG):
                            if OWNER[j] == "A":
                                copy(i, t, j)
                            if j in EXP_AFTER:
                                if t + 1 < len(tasks):
                                    exponentials(i, t + 1, EXP_AFTER.index(j))
                                elif more:
                                    exponentials(i + 1, 0, EXP_AFTER.index(j))
                        if task.r == 1 and task.pi:
                            reciprocals(i, task.pi - 1)
                    reciprocals(i, PIS - 1)

                for small in range(2):
                    exponentials(0, 0, small)
                with act.Fori(0, BODIES - 1) as i:
                    body(i, True)
                body(BODIES - 1, False)

            @block.tensor
            def _(pe):
                pe.sem_inc(qk_done, HALVES)
                pe.sem_inc(tr_done, GROUPS)
                pe.sem_inc(pv_done, GROUPS)
                pe.sem_inc(rtr_done, PIS)
                pe.wait_ge(const_in, 3 * 16)

                def scores(i, t, h):
                    task = tasks[t]
                    hs = t * 3 + h
                    qb, a, b, _ = task.half(h)
                    q = task.pi // QL
                    if task.r == 0 and h == 0:
                        if task.pair == 0:
                            pe.wait_ge(k_in[task.u], (i + 1) * 64)
                        if task.pair % QL == 0:
                            pe.wait_ge(q_in[q % 2], i * (LOADS * 128) + (q // 2 + 1) * 128)
                    pe.wait_ge(min_done, at(i, HALVES, hs - 2))
                    for c in range(a, b, WIDE):
                        e = min(b, c + WIDE)
                        last = nc.tensor.matmul(sp_ps[hs % 2][:, c - a:e - a],
                                                qp[:, q % 2, task.r, h // 2, qb % QL * P:(qb % QL + 1) * P],
                                                kp[:, task.u, c:e], start=True, stop=True)
                    last.then_inc(qk_done, 1)

                def wait_bank(i, *entry):
                    at_entry = banks.index(entry) - TR
                    n, j = banks[at_entry]
                    if j == "sums":
                        pe.wait_ge(rt_done, at(i, PIS, n - (PIS if at_entry < 0 else 0)))
                    else:
                        wait_copy(i, n * NG + j - (GROUPS if at_entry < 0 else 0))

                def transposes(i, t, j):
                    blocks = GROUP_BLOCKS[j]
                    small, c = tasks[t].key_block(blocks[-1])
                    pe.wait_ge(exp_done, i * (2 * len(tasks)) + t * 2 + small + 1)
                    wait_bank(i, t, j)
                    for k, b in enumerate(blocks):
                        last = nc.tensor.transpose(bank(t, j)[:, k * P:(k + 1) * P],
                                                   xs[:, t % XR, b * P:(b + 1) * P], idn[:])
                    last.then_inc(tr_done, 1)

                def wait_copy(i, g):
                    t, j = divmod(g, NG)
                    who = OWNER[j]
                    pe.wait_ge(copied[who], at(i, COPIES[who], t * OWNER.count(who) + OWNER[:j].count(who)))

                def products(i, t, j):
                    task = tasks[t]
                    g = t * NG + j
                    wait_copy(i, g)
                    if j == 0 and task.r == 0:
                        pe.wait_ge(drained, at(i, PIS, task.pi - 1))
                        if task.pair == 0:
                            pe.wait_ge(vcur_done, i * 2 + task.u + 1)
                    for k, b in enumerate(GROUP_BLOCKS[j]):
                        small, c = task.key_block(b)
                        last = nc.tensor.matmul(op[task.r * D:(task.r + 1) * D, small, :],
                                                vcur[:, task.u, c, :], pt[:, g % PR, k * P:(k + 1) * P], start=(c == 0),
                                                stop=(c == (task.small if small else task.big)),
                                                tile_position=(0, task.r * D))
                    last.then_inc(pv_done, 1)

                def reciprocals(i, pi):
                    pe.wait_ge(recw_done, at(i, PIS, pi))
                    wait_bank(i, pi, "sums")
                    for k in range(2):
                        last = nc.tensor.transpose(bank(pi, "sums")[:, k * P:(k + 1) * P],
                                                   recw[:, pi % 2, k * REP:(k + 1) * REP, :].rearrange("p r d -> p (r d)"),
                                                   idn[:])
                    last.then_inc(rtr_done, 1)

                def body(i, more):
                    waiting = []
                    for t, task in enumerate(tasks):
                        for j, ahead in enumerate([None, (2, 1), None, (2, 2), (3, 0)]):
                            transposes(i, t, j)
                            waiting.append((t, j))
                            if len(waiting) > LAG and not (task.r == 0 and j == LAG and task.pi):
                                products(i, *waiting.pop(0))
                            if len(waiting) > LAG and task.r == 0 and j == LAG + 1:
                                products(i, *waiting.pop(0))
                            if ahead:
                                n, h = ahead
                                if t + n < len(tasks):
                                    scores(i, t + n, h)
                                elif more:
                                    scores(i + 1, t + n - len(tasks), h)
                        if task.r == 1 and task.pi:
                            reciprocals(i, task.pi - 1)
                    for w in waiting:
                        products(i, *w)
                    reciprocals(i, PIS - 1)

                for t in range(2):
                    for h in range(3):
                        scores(0, t, h)
                scores(0, 2, 0)
                with pe.Fori(0, BODIES - 1) as i:
                    body(i, True)
                body(BODIES - 1, False)


def mix_and_gate(nc, x, o_dram, wo_t, gate_w_t, gate_b, gate_bias, ident, rows_bc, top_v, top_i, x1_dram, h2_dram,
                 fetch):
    RX, RH, RT, RO, RP = 8, 4, 2, 8, 4
    LEAD = SUP + RP - 1
    BODY = 2 * SUP
    with ExitStack() as ctx:
        m = Mem(nc, ctx)
        idn = m.sb("g_idn", [P, P])
        wo = m.sb("g_wo", [P, B * G, DM])
        gw = m.sb("g_gw", [P, C, E])
        gb = m.sb("g_gb", [P, 2, E])
        gbs = m.sb("g_gbs", [P, E])
        ot = m.sb("g_ot", [P, RO, G, P])
        xt = m.sb("g_xt", [P, RX, DM])
        hn = m.sb("g_hn", [P, RH, DM])
        ht = m.sb("g_ht", [P, RT, C, P])
        score = m.sb("g_score", [P, 2, E])
        best = m.sb("g_best", [P, 2, 8])
        index = m.sb("g_index", [P, 2, 8], U32)
        ln = LayerNorm(m, "g", SUP)
        pp = [m.ps(f"g_pp{k}", [P, DM]) for k in range(RP)]
        tp = [m.ps(f"g_tp{k}", [P, C, P]) for k in range(RT)]
        pg = [m.ps(f"g_pg{k}", [P, DM]) for k in range(2)]

        wo_in = m.sem("wo_in")
        const_in = m.sem("g_const_in")
        wo_scaled = m.sem("wo_scaled")
        gbs_done = m.sem("gbs_done")
        o_in = [m.sem(f"o_in{k}") for k in range(RO)]
        x_in = [m.sem(f"gx_in{k}") for k in range(RX)]
        proj_done = m.sem("proj_done")
        x1_done = m.sem("x1_done")
        x1_out = [m.sem(f"x1_out{k}") for k in range(RX)]
        norm_done = m.sem("g_norm_done")
        h_done = m.sem("g_h_done")
        h_out = [m.sem(f"h_out{k}") for k in range(RH)]
        tp_done = m.sem("g_tp_done")
        ht_done = m.sem("g_ht_done")
        gate_done = m.sem("gate_done")
        score_done = m.sem("score_done")
        best_done = m.sem("best_done")
        index_done = m.sem("index_done")
        kept_v = m.sem("kept_v")
        kept_i = m.sem("kept_i")

        with nc.Block() as block:

            @block.sync
            def _(sp):
                sp.dma_start(wo[:, 0:G, :], wo_t.rearrange("(g p) n -> p g n", p=P)).then_inc(wo_in, 16)
                sp.dma_start(wo[:, G:2 * G, :], wo_t.rearrange("(g p) n -> p g n", p=P)).then_inc(wo_in, 16)
                sp.dma_start(idn[:], ident).then_inc(const_in, 16)
                sp.dma_start(gw[:], gate_w_t.rearrange("(c p) e -> p c e", p=P)).then_inc(const_in, 16)
                sp.dma_start(gb[:, 0, :], gate_b.partition_broadcast(P)).then_inc(const_in, 16)
                sp.dma_start(gb[:, 1, :], gate_bias.partition_broadcast(P)).then_inc(const_in, 16)

                def load(n, l):
                    k = n * BODY + l
                    sp.wait_ge(proj_done, k + 1)
                    sp.dma_start(ot[:, l % RO, :, :],
                                 o_dram[bass.ds(n // 2 * G, G), bass.ds(n % 2 * BODY + l, 1), :, :]
                                 .rearrange("g o p t -> p (g o) t")).then_inc(o_in[l % RO], 16)
                    sp.wait_ge(x1_out[l % RX], (n + 1) * 16)
                    sp.wait_ge(norm_done, k + 1)
                    sp.dma_start(xt[:, l % RX, :], x[bass.ds(k * P, P), :]).then_inc(x_in[l % RX], 16)

                with sp.Fori(0, NT // BODY) as n:
                    for l in range(BODY):
                        load(n, l)
                    fetch(sp, n)

            @block.tensor
            def _(pe):
                pe.sem_inc(proj_done, RO)
                pe.sem_inc(tp_done, RH)
                pe.sem_inc(gate_done, RT)
                pe.wait_ge(const_in, 4 * 16)
                pe.wait_ge(wo_scaled, B * G)

                def project(n, l):
                    k = n * BODY + l
                    pe.wait_ge(o_in[l % RO], (n + 1) * 16)
                    pe.wait_ge(x1_done, k + 1)
                    for g in range(G):
                        w = wo[:, bass.ds(n // 2 * G + g, 1), :].rearrange("p o n -> p (o n)")
                        last = nc.tensor.matmul(pp[l % RP][:], ot[:, l % RO, g, :], w, start=(g == 0), stop=(g == G - 1))
                    last.then_inc(proj_done, 1)

                def transposes(n, l):
                    k = n * BODY + l
                    pe.wait_ge(h_done, k + 1)
                    pe.wait_ge(ht_done, k + 1)
                    for c in range(C):
                        last = nc.tensor.transpose(tp[l % RT][:, c, :], hn[:, l % RH, c * P:(c + 1) * P], idn[:])
                    last.then_inc(tp_done, 1)

                def gate(n, l):
                    k = n * BODY + l
                    pe.wait_ge(ht_done, RT + k + 1)
                    pe.wait_ge(score_done, k + 1)
                    for c in range(C):
                        last = nc.tensor.matmul(pg[l % 2][:, 0:E], ht[:, l % RT, c, :], gw[:, c, :],
                                                start=(c == 0), stop=(c == C - 1))
                    last.then_inc(gate_done, 1)

                def body(n, more):
                    for l in range(BODY):
                        transposes(n, l)
                        if l + LEAD < BODY:
                            project(n, l + LEAD)
                        elif more:
                            project(n + 1, l + LEAD - BODY)
                        gate(n, l)

                for l in range(LEAD):
                    project(0, l)
                with pe.Fori(0, NT // BODY - 1) as n:
                    body(n, True)
                body(NT // BODY - 1, False)

            @block.vector
            def _(dve):
                dve.sem_inc(x1_done, RP)
                dve.sem_inc(norm_done, RX)
                dve.sem_inc(score_done, 2)
                dve.wait_ge(wo_in, 2 * 16)
                for b in range(B):
                    for g in range(G):
                        nc.vector.tensor_tensor(wo[:, b * G + g, :], wo[:, b * G + g, :], rows_bc[:, b, GA, :],
                                                ALU.mult).then_inc(wo_scaled, 1)
                dve.wait_ge(const_in, 4 * 16)
                nc.vector.tensor_tensor(gbs[:], gb[:, 0, :], gb[:, 1, :], ALU.add).then_inc(gbs_done, 1)
                dve.wait_ge(gbs_done, 1)

                def residual(n, l):
                    k = n * BODY + l
                    dve.wait_ge(x_in[l % RX], (n + 1) * 16)
                    dve.wait_ge(proj_done, RO + k + 1)
                    nc.vector.tensor_tensor(xt[:, l % RX, :], pp[l % RP][:], xt[:, l % RX, :], ALU.add).then_inc(x1_done, 1)
                    dve.wait_ge(x1_done, RP + k + 1)
                    ln.statistics(nc, xt[:, l % RX, :], l % SUP)

                def norm(n, l):
                    k = n * BODY + l
                    dve.wait_ge(tp_done, k + 1)
                    dve.wait_ge(h_out[l % RH], n * (BODY // RH * 16) + (l // RH + 1) * 16)
                    ln.centre(nc, hn[:, l % RH, :], xt[:, l % RX, :], l % SUP, row_of(rows_bc, n, CB)).then_inc(norm_done, 1)
                    dve.wait_ge(norm_done, RX + k + 1)
                    ln.shift(nc, hn[:, l % RH, :], l % SUP, row_of(rows_bc, n, SB)).then_inc(h_done, 1)

                def choose(n, l):
                    k = n * BODY + l
                    s = l % 2
                    dve.wait_ge(gate_done, RT + k + 1)
                    nc.vector.tensor_tensor(score[:, s, :], pg[s][:, 0:E], gbs[:], ALU.add).then_inc(score_done, 1)
                    dve.wait_ge(score_done, 2 + k + 1)
                    apart(dve, m.passed)
                    nc.vector.max(best[:, s, :], score[:, s, :]).then_inc(best_done, 1)
                    dve.wait_ge(best_done, k + 1)
                    apart(dve, m.passed)
                    nc.vector.max_index(index[:, s, :], best[:, s, :], score[:, s, :]).then_inc(index_done, 1)
                    dve.wait_ge(index_done, k + 1)
                    nc.vector.tensor_copy(top_v[:, bass.ds(k, 1), :], best[:, s:s + 1, 0:2]).then_inc(kept_v, 1)
                    nc.vector.tensor_copy(top_i[:, bass.ds(k, 1), :], index[:, s:s + 1, 0:2]).then_inc(kept_i, 1)

                def body(n, more):
                    for u in range(2):
                        ahead = u == 0 or more
                        after = (n, SUP) if u == 0 else (n + 1, 0)
                        if ahead:
                            for j in range(SUP):
                                residual(after[0], after[1] + j)
                            ln.deviation(nc, dve, n * 2 + u + 1)
                        for j in range(SUP):
                            if ahead:
                                norm(after[0], after[1] + j)
                            choose(n, u * SUP + j)

                for l in range(SUP):
                    residual(0, l)
                ln.deviation(nc, dve, 0)
                for l in range(SUP):
                    norm(0, l)
                with dve.Fori(0, NT // BODY - 1) as n:
                    body(n, True)
                body(NT // BODY - 1, False)
                dve.wait_ge(kept_v, NT)
                dve.wait_ge(kept_i, NT)

            @block.scalar
            def _(act):
                act.sem_inc(ht_done, RT)
                for out in x1_out + h_out:
                    act.sem_inc(out, 16)

                def transposed(n, l):
                    k = n * BODY + l
                    act.wait_ge(tp_done, RH + k + 1)
                    act.wait_ge(gate_done, k + 1)
                    nc.scalar.activation(ht[:, l % RT, :, :], tp[l % RT][:], ACT.Copy).then_inc(ht_done, 1)
                    act.wait_ge(x1_done, RP + k + 1)
                    act.dma_start(x1_dram[bass.ds(k * P, P), :], xt[:, l % RX, :]).then_inc(x1_out[l % RX], 16)
                    act.wait_ge(h_done, k + 1)
                    act.dma_start(h2_dram[bass.ds(k * P, P), :], hn[:, l % RH, :]).then_inc(h_out[l % RH], 16)

                def body(n, more):
                    for u in range(2):
                        for j in range(SUP):
                            transposed(n, u * SUP + j)
                            if j == 0 and (u == 0 or more):
                                ln.root(nc, act, n * 2 + u + 1)

                ln.root(nc, act, 0)
                with act.Fori(0, NT // BODY - 1) as n:
                    body(n, True)
                body(NT // BODY - 1, False)
                for k in range(RX):
                    act.wait_ge(x1_out[k], 16 + NT // RX * 16)
                for k in range(RH):
                    act.wait_ge(h_out[k], 16 + NT // RH * 16)


def route(nc, top_v, top_i, before, experts, tile_start, slot_number, row_step, positions, ident, gates, slots,
          tile_expert, slot_token, fetch):
    TILES = 3
    LOTS = ST // TILES
    RUNS = NT * E // P
    RL, LEAD = 4, 3
    N = NT * E
    with ExitStack() as ctx:
        m = Mem(nc, ctx)
        tri = m.sb("r_tri", [P, P])
        ones = m.sb("r_ones", [P, P])
        iota = m.sb("r_iota", [P, NT, E])
        starts = m.sb("r_starts", [P, ST])
        mask = [m.sb(f"r_mask{k}", [P, NT, E]) for k in range(2)]
        both = m.sb("r_both", [P, NT, E])
        count = m.sb("r_count", [P, NT, E])
        upto = m.sb("r_upto", [P, NT, E])
        place = m.sb("r_place", [P, NT, E])
        hit = m.sb("r_hit", [P, NT, E])
        padded = m.sb("r_padded", [P, E])
        padded_i = m.sb("r_padded_i", [P, E], I32)
        ends = m.sb("r_ends", [P, E])
        begins = m.sb("r_begins", [P, E])
        slot_f = m.sb("r_slot_f", [P, NT])
        expert_f = m.sb("r_expert_f", [P, ST])
        diff = m.sb("r_diff", [P, NT])
        ratio = m.sb("r_ratio", [P, NT])
        one_more = m.sb("r_one_more", [P, NT])
        idn = m.sb("r_idn", [P, P])
        number = m.sb("r_number", [P, ST])
        between = m.sb("r_between", [P, ST])
        pos = m.sb("r_pos", [P, TILES * P])
        first = m.sb("r_first", [P, E, NT])
        upto_token = m.sb("r_upto_token", [P, E, NT])
        step_row = m.sb("r_step_row", [P, N])
        runs = m.sb("r_runs", [P, RUNS, P + 1], F16)
        first_step = m.sb("r_first_step", [P, RUNS])
        starts_at = m.sb("r_starts_at", [P, RUNS])
        run_start = m.sb("r_run_start", [P, RUNS, LOTS])
        begun = m.sb("r_begun", [P, RL, RUNS, TILES * P], F16)
        signs = m.sb("r_signs", [P, RL, TILES, P])
        balance = m.sb("r_balance", [P, RL, TILES])
        token = m.sb("r_token", [P, RL, TILES])
        turned = m.ps("r_turned", [P, 2 * RUNS, P])
        picked = [m.ps(f"r_picked{k}", [P, WIDE]) for k in range(RL)]
        rank_ps = m.ps("r_rank", [P, NT, E])
        total_ps = m.ps("r_total", [P, NT, E])

        const_in = m.sem("r_const_in")
        ones_set = m.sem("ones_set")
        step = m.sem("route_step")
        both_done = m.sem("both_done")
        ranked = m.sem("ranked")
        totalled = m.sem("totalled")
        diff_done = m.sem("diff_done")
        ratio_done = m.sem("ratio_done")
        slots_done = m.sem("slots_done")
        steps_ready = m.sem("steps_ready")
        turn_done = m.sem("turn_done")
        begun_done = m.sem("begun_done")
        pick_done = m.sem("pick_done")
        between_done = m.sem("between_done")
        count_done = m.sem("count_done")
        token_done = m.sem("token_done")
        kept = m.sem("r_kept")

        with nc.Block() as block:

            @block.sync
            def _(sp):
                sp.dma_start(tri[:], before).then_inc(const_in, 16)
                sp.dma_start(iota[:], experts).then_inc(const_in, 16)
                sp.dma_start(starts[:], tile_start).then_inc(const_in, 16)
                sp.dma_start(number[:], slot_number).then_inc(const_in, 16)
                sp.dma_start(pos[:], positions).then_inc(const_in, 16)
                sp.dma_start(idn[:], ident).then_inc(const_in, 16)
                sp.dma_start(first_step[:], row_step).then_inc(const_in, 16)
                fetch(sp)

            @block.tensor
            def _(pe):
                pe.sem_inc(pick_done, RL)
                pe.wait_ge(const_in, 7 * 16)
                pe.wait_ge(ones_set, 1)
                pe.wait_ge(both_done, 1)
                flat = both[:].rearrange("p t e -> p (t e)")
                nc.tensor.matmul(rank_ps[:].rearrange("p t e -> p (t e)"), tri[:], flat, start=True, stop=True).then_inc(ranked, 1)
                nc.tensor.matmul(total_ps[:].rearrange("p t e -> p (t e)"), ones[:], flat, start=True, stop=True).then_inc(totalled, 1)
                pe.wait_ge(steps_ready, 1)
                for c in range(RUNS):
                    nc.tensor.transpose(turned[:, c, :], step_row[:, c * P:(c + 1) * P], idn[:])
                    last = nc.tensor.transpose(turned[:, RUNS + c, :],
                                               first[:].rearrange("p e t -> p (e t)")[:, c * P:(c + 1) * P], idn[:])
                last.then_inc(turn_done, 1)

                def pick(n, l):
                    k = n * RL + l
                    pe.wait_ge(begun_done, (k + 1) * RUNS)
                    pe.wait_ge(token_done, k + 1)
                    for t in range(TILES):
                        for c in range(RUNS):
                            last = nc.tensor.matmul(picked[l][:, t * (P + 1):(t + 1) * (P + 1)],
                                                    begun[:, l, c, t * P:(t + 1) * P], runs[:, c, :],
                                                    start=(c == 0), stop=(c == RUNS - 1))
                    last.then_inc(pick_done, 1)

                with pe.Fori(0, LOTS // RL) as n:
                    for l in range(RL):
                        pick(n, l)

            @block.scalar
            def _(act):
                act.wait_ge(diff_done, 1)
                nc.scalar.activation(ratio[:], diff[:], ACT.Exp).then_inc(ratio_done, 1)
                act.wait_ge(between_done, 1)
                with act.Fori(0, LOTS // RL) as n:
                    for l in range(RL):
                        k = n * RL + l
                        act.wait_ge(pick_done, RL + k + 1)
                        for t in range(TILES):
                            nc.scalar.activation(signs[:, l, t, :], picked[l][:, t * (P + 1):t * (P + 1) + P], ACT.Sign,
                                                 scale=-1.0, bias=between[:, bass.ds(k * TILES + t, 1)],
                                                 accum_out=balance[:, l, t:t + 1]).then_inc(count_done, 1)

            @block.vector
            def _(dve):
                dve.sem_inc(token_done, RL)
                done = [0]

                def then(ins):
                    done[0] += 1
                    ins.then_inc(step, 1)
                    dve.wait_ge(step, done[0])

                nc.vector.memset(ones[:], 1.0).then_inc(ones_set, 1)
                nc.vector.tensor_tensor(diff[:], top_v[:, :, 1], top_v[:, :, 0], ALU.subtract).then_inc(diff_done, 1)
                dve.wait_ge(const_in, 7 * 16)
                nc.vector.tensor_scalar(between[:], number[:], 0.5, None, ALU.add).then_inc(between_done, 1)
                for k in range(2):
                    then(nc.vector.tensor_tensor(mask[k][:], iota[:], top_i[:, :, k].unsqueeze(2).broadcast_to([P, NT, E]),
                                                 ALU.is_equal))
                nc.vector.tensor_tensor(both[:], mask[0][:], mask[1][:], ALU.add).then_inc(both_done, 1)
                dve.wait_ge(ones_set, 1)
                dve.wait_ge(totalled, 1)
                then(nc.vector.tensor_copy(count[:], total_ps[:]))
                for e in range(E):
                    last = nc.vector.tensor_tensor_scan(out=upto[:, :, e], data0=ones[:, 0:NT], data1=count[:, :, e],
                                                        initial=0.0, op0=ALU.mult, op1=ALU.add)
                    then(last)
                then(nc.vector.tensor_scalar(padded_i[:], upto[:, NT - 1, :], float(P - 1), None, ALU.add))
                then(nc.vector.tensor_scalar(padded_i[:], padded_i[:], 7, 7, ALU.arith_shift_right, ALU.arith_shift_left))
                then(nc.vector.tensor_copy(padded[:], padded_i[:]))
                then(nc.vector.tensor_tensor_scan(out=ends[:], data0=ones[:, 0:E], data1=padded[:], initial=0.0,
                                                  op0=ALU.mult, op1=ALU.add))
                then(nc.vector.tensor_tensor(begins[:], ends[:], padded[:], ALU.subtract))
                then(nc.vector.tensor_tensor(place[:], upto[:], count[:], ALU.subtract))
                then(nc.vector.tensor_tensor(place[:], place[:], begins[:].unsqueeze(1).broadcast_to([P, NT, E]), ALU.add))
                by_run = first[:].rearrange("p e t -> p t e")
                then(nc.vector.tensor_copy(by_run, place[:]))
                dve.wait_ge(ranked, 1)
                then(nc.vector.tensor_tensor(place[:], rank_ps[:], place[:], ALU.add))
                then(nc.vector.tensor_tensor(upto_token[:].rearrange("p e t -> p t e"), place[:], both[:], ALU.add))
                flat = upto_token[:].rearrange("p e t -> p (e t)")
                then(nc.vector.tensor_tensor(step_row[:, 1:N], flat[:, 1:N], flat[:, 0:N - 1], ALU.subtract))
                nc.vector.tensor_copy(step_row[:, 0:1], flat[:, 0:1]).then_inc(steps_ready, 1)
                for k in range(2):
                    then(nc.vector.tensor_tensor(hit[:], mask[k][:], place[:], ALU.mult))
                    then(nc.vector.tensor_reduce(slot_f[:], hit[:], AX.X, ALU.add))
                    nc.vector.tensor_copy(slots[:, :, k], slot_f[:]).then_inc(slots_done, 1)
                    dve.wait_ge(slots_done, k + 1)
                then(nc.vector.tensor_scalar(expert_f[:], starts[:], ends[:, 0:1], None, ALU.is_ge))
                for e in range(1, E - 1):
                    then(nc.vector.scalar_tensor_tensor(out=expert_f[:], in0=starts[:], scalar=ends[:, e:e + 1],
                                                        in1=expert_f[:], op0=ALU.is_ge, op1=ALU.add))
                then(nc.vector.tensor_copy(tile_expert[:], expert_f[:]))
                dve.wait_ge(ratio_done, 1)
                then(nc.vector.tensor_scalar(one_more[:], ratio[:], 1.0, None, ALU.add))
                then(nc.vector.reciprocal(gates[:, 0, :], one_more[:]))
                then(nc.vector.tensor_tensor(gates[:, 1, :], ratio[:], gates[:, 0, :], ALU.mult))

                dve.wait_ge(turn_done, 1)
                then(nc.vector.tensor_copy(runs[:, :, 0:P], turned[:, 0:RUNS, :]))
                then(nc.vector.tensor_copy(runs[:, :, P], first_step[:]))
                then(nc.vector.tensor_copy(starts_at[:], turned[:, RUNS:2 * RUNS, 0]))
                lot_start = starts[:].rearrange("p (l t) -> p l t", t=TILES)[:, :, 0]
                then(nc.vector.tensor_tensor(run_start[:], starts_at[:].unsqueeze(2).broadcast_to([P, RUNS, LOTS]),
                                             lot_start.unsqueeze(1).broadcast_to([P, RUNS, LOTS]), ALU.subtract))

                def begin(n, l):
                    k = n * RL + l
                    dve.wait_ge(pick_done, k + 1)
                    for c in range(RUNS):
                        nc.vector.tensor_scalar(begun[:, l, c, :], pos[:], run_start[:, c, bass.ds(k, 1)], None,
                                                ALU.is_ge).then_inc(begun_done, 1)

                def find(n, l):
                    k = n * RL + l
                    run = picked[l][:, 0:TILES * (P + 1)].rearrange("p (t c) -> p t c", c=P + 1)
                    dve.wait_ge(count_done, (k + 1) * TILES)
                    nc.vector.scalar_tensor_tensor(out=token[:, l, :], in0=balance[:, l, :], scalar=0.5,
                                                   in1=run[:, :, P], op0=ALU.mult, op1=ALU.add).then_inc(token_done, 1)
                    dve.wait_ge(token_done, RL + k + 1)
                    nc.vector.tensor_scalar(slot_token[:, bass.ds(k * TILES, TILES)], token[:, l, :],
                                            float(P // 2), float(NT * P - 1), ALU.add, ALU.min).then_inc(kept, 1)

                def body(n, more):
                    for l in range(RL):
                        if l + LEAD < RL:
                            begin(n, l + LEAD)
                        elif more:
                            begin(n + 1, l + LEAD - RL)
                        find(n, l)

                for l in range(LEAD):
                    begin(0, l)
                with dve.Fori(0, LOTS // RL - 1) as n:
                    body(n, True)
                body(LOTS // RL - 1, False)
                dve.wait_ge(kept, LOTS)


def run_experts(nc, ident, w1, w2, b1, b2, weights_in, tile_expert, slot_token, h2_dram, y_dram, fetch):
    RX, RY = 4, 2
    PADH = len(HC) * P
    with ExitStack() as ctx:
        m = Mem(nc, ctx)
        idn = m.sb("e_idn", [P, P])
        xt = m.sb("e_xt", [P, RX, DM])
        xtt = m.sb("e_xtt", [P, 2, C, P])
        z = m.sb("e_z", [P, 2, HF])
        th = m.sb("e_th", [P, 2, HF])
        hz = m.sb("e_hz", [P, 2, PADH])
        hzt = m.sb("e_hzt", [P, 2, PADH])
        where = m.sb("e_where", [P, RX], U32)
        ys = m.sb("e_ys", [P, RY, DM])
        tx = [m.ps(f"e_tx{k}", [P, C, P]) for k in range(2)]
        thp = [m.ps(f"e_th{k}", [P, PADH]) for k in range(2)]
        pz = [m.ps(f"e_pz{k}", [P, DM]) for k in range(2)]
        py = [m.ps(f"e_py{k}", [P, DM]) for k in range(2)]

        idn_in = m.sem("e_idn_in")
        x_in = [m.sem(f"ex_in{k}") for k in range(RX)]
        tx_done = m.sem("tx_done")
        xtt_done = m.sem("xtt_done")
        up_done = m.sem("up_done")
        z_done = m.sem("z_done")
        tanh_done = m.sem("e_tanh_done")
        pad_set = m.sem("pad_set")
        hz_done = m.sem("hz_done")
        th_done = m.sem("th_done")
        hzt_done = m.sem("hzt_done")
        down_done = m.sem("down_done")
        y_done = m.sem("y_done")
        where_done = m.sem("e_where_done")
        y_out = [m.sem(f"y_out{k}") for k in range(RY)]

        with nc.Block() as block:

            @block.sync
            def _(sp):
                sp.dma_start(idn[:], ident).then_inc(idn_in, 16)
                fetch(sp)
                for l in range(RY):
                    sp.sem_inc(y_out[l], 16)
                with sp.Fori(0, ST // RX) as n:
                    for l in range(RX):
                        sp.wait_ge(y_done, 2 + n * RX + l + 1)
                        sp.dma_start(y_dram[bass.ds(n * (RX * P) + l * P, P), :], ys[:, l % RY, :])\
                          .then_inc(y_out[l % RY], 16)
                for l in range(RY):
                    sp.wait_ge(y_out[l], 16 + ST // RY * 16)

            @block.tensor
            def _(pe):
                pe.sem_inc(tx_done, RX)
                pe.sem_inc(up_done, 2)
                pe.sem_inc(th_done, 2)
                pe.sem_inc(down_done, 2)
                pe.wait_ge(idn_in, 16)
                for s in weights_in:
                    pe.wait_ge(*s)

                def transposes(n, l):
                    k = n * RX + l
                    pe.wait_ge(x_in[l], (n + 1) * 16)
                    pe.wait_ge(xtt_done, k + 1)
                    for c in range(C):
                        last = nc.tensor.transpose(tx[l % 2][:, c, :], xt[:, l, c * P:(c + 1) * P], idn[:])
                    last.then_inc(tx_done, 1)

                def up(n, l):
                    k = n * RX + l
                    e = nc.tensor.value_load(tile_expert[0:1, bass.ds(k, 1)], min_val=0, max_val=E - 1)
                    pe.wait_ge(xtt_done, 2 + k + 1)
                    pe.wait_ge(z_done, k + 1)
                    for c in range(C):
                        last = nc.tensor.matmul(pz[l % 2][:, 0:HF], xtt[:, l % 2, c, :], w1[:, c, bass.ds(e * HF, HF)],
                                                start=(c == 0), stop=(c == C - 1))
                    last.then_inc(up_done, 1)

                def turn(n, l):
                    k = n * RX + l
                    pe.wait_ge(hz_done, 2 + k + 1)
                    pe.wait_ge(hzt_done, k + 1)
                    for c in range(len(HC)):
                        last = nc.tensor.transpose(thp[l % 2][:, c * P:(c + 1) * P], hz[:, l % 2, c * P:(c + 1) * P], idn[:])
                    last.then_inc(th_done, 1)

                def down(n, l):
                    k = n * RX + l
                    e = nc.tensor.value_load(tile_expert[0:1, bass.ds(k, 1)], min_val=0, max_val=E - 1)
                    pe.wait_ge(hzt_done, 2 + k + 1)
                    pe.wait_ge(y_done, k + 1)
                    for c in range(len(HC)):
                        last = nc.tensor.matmul(py[l % 2][:], hzt[:, l % 2, c * P:(c + 1) * P], w2[:, c, bass.ds(e * DM, DM)],
                                                start=(c == 0), stop=(c == len(HC) - 1))
                    last.then_inc(down_done, 1)

                def body(n, more):
                    for l in range(RX):
                        ahead = l < RX - 1 or more
                        after = (n, l + 1) if l < RX - 1 else (n + 1, 0)
                        if ahead:
                            transposes(*after)
                        turn(n, l)
                        if ahead:
                            up(*after)
                        down(n, l)

                transposes(0, 0)
                up(0, 0)
                with pe.Fori(0, ST // RX - 1) as n:
                    body(n, True)
                body(ST // RX - 1, False)

            @block.scalar
            def _(act):
                act.sem_inc(xtt_done, 2)
                act.sem_inc(hzt_done, 2)

                def input_copy(n, l):
                    k = n * RX + l
                    act.wait_ge(tx_done, RX + k + 1)
                    act.wait_ge(up_done, k + 1)
                    nc.scalar.activation(xtt[:, l % 2, :, :], tx[l % 2][:], ACT.Copy).then_inc(xtt_done, 1)

                def hidden_copy(n, l):
                    k = n * RX + l
                    act.wait_ge(th_done, 2 + k + 1)
                    act.wait_ge(down_done, k + 1)
                    nc.scalar.activation(hzt[:, l % 2, :], thp[l % 2][:], ACT.Copy).then_inc(hzt_done, 1)

                def tanh(n, l):
                    k = n * RX + l
                    act.wait_ge(z_done, 2 + k + 1)
                    act.wait_ge(hz_done, k + 1)
                    nc.scalar.activation(th[:, l % 2, :], z[:, l % 2, :], ACT.Tanh, scale=0.5).then_inc(tanh_done, 1)

                def body(n, more):
                    for l in range(RX):
                        ahead = l < RX - 1 or more
                        after = (n, l + 1) if l < RX - 1 else (n + 1, 0)
                        if ahead:
                            input_copy(*after)
                        hidden_copy(n, l)
                        if ahead:
                            tanh(*after)

                input_copy(0, 0)
                tanh(0, 0)
                with act.Fori(0, ST // RX - 1) as n:
                    body(n, True)
                body(ST // RX - 1, False)

            @block.vector
            def _(dve):
                dve.sem_inc(z_done, 2)
                dve.sem_inc(y_done, 2)
                dve.sem_inc(hz_done, 2)
                nc.vector.memset(hz[:, :, HF:PADH], 0.0).then_inc(pad_set, 1)
                dve.wait_ge(pad_set, 1)
                for s in weights_in:
                    dve.wait_ge(*s)

                def hidden(n, l):
                    k = n * RX + l
                    e = nc.vector.value_load(tile_expert[0:1, bass.ds(k, 1)], min_val=0, max_val=E - 1)
                    dve.wait_ge(up_done, 2 + k + 1)
                    nc.vector.tensor_tensor(z[:, l % 2, :], pz[l % 2][:, 0:HF], b1[:, bass.ds(e * HF, HF)],
                                            ALU.add).then_inc(z_done, 1)
                    dve.wait_ge(tanh_done, k + 1)
                    dve.wait_ge(th_done, k + 1)
                    nc.vector.scalar_tensor_tensor(out=hz[:, l % 2, 0:HF], in0=th[:, l % 2, :], scalar=1.0,
                                                   in1=z[:, l % 2, :], op0=ALU.add, op1=ALU.mult).then_inc(hz_done, 1)

                def output(n, l):
                    k = n * RX + l
                    e = nc.vector.value_load(tile_expert[0:1, bass.ds(k, 1)], min_val=0, max_val=E - 1)
                    dve.wait_ge(down_done, 2 + k + 1)
                    dve.wait_ge(y_out[l % RY], n * (RX // RY * 16) + (l // RY + 1) * 16)
                    nc.vector.scalar_tensor_tensor(out=ys[:, l % RY, :], in0=py[l % 2][:], scalar=0.5,
                                                   in1=b2[:, bass.ds(e * DM, DM)], op0=ALU.mult,
                                                   op1=ALU.add).then_inc(y_done, 1)

                def body(n, more):
                    for l in range(RX):
                        if l < RX - 1:
                            hidden(n, l + 1)
                        elif more:
                            hidden(n + 1, 0)
                        output(n, l)

                hidden(0, 0)
                with dve.Fori(0, ST // RX - 1) as n:
                    body(n, True)
                body(ST // RX - 1, False)

            @block.gpsimd
            def _(pool):
                with pool.Fori(0, ST // RX) as n:
                    for l in range(RX):
                        k = n * RX + l
                        pool.wait_ge(tx_done, k + 1)
                        apart(pool, m.passed)
                        nc.gpsimd.tensor_copy(where[:, l:l + 1], slot_token[:, bass.ds(k, 1)]).then_inc(where_done, 1)
                        pool.wait_ge(where_done, k + 1)
                        apart(pool, m.passed)
                        pool.indirect_dma_start(xt[:, l, :], None, h2_dram,
                                                bass.IndirectOffsetOnAxis(ap=where[:, l:l + 1], axis=0),
                                                bounds_check=NT * P - 1, oob_is_err=False).then_inc(x_in[l], 16)


def combine(nc, rows_bc, gates, slots, x1_first, first_in, room, x1_dram, y_dram, out):
    R = 4
    with ExitStack() as ctx:
        m = Mem(nc, ctx)
        xt = m.sb("c_xt", [P, R, DM])
        y = m.sb("c_y", [P, R, 2, DM])
        acc = room[:, 0:R * DM].rearrange("p (r n) -> p r n", r=R)
        where = m.sb("c_where", [P, R, 2], U32)
        weight = m.sb("c_weight", [P, R, 2])
        x_in = [m.sem(f"cx_in{k}") for k in range(R)]
        y_in = [m.sem(f"cy_in{k}") for k in range(R)]
        where_done = m.sem("c_where_done")
        weight_done = m.sem("weight_done")
        first_done = m.sem("first_done")
        both_done = m.sem("c_both_done")
        scaled = m.sem("scaled")
        sum_done = m.sem("sum_done")
        out_done = [m.sem(f"c_out{k}") for k in range(R)]

        with nc.Block() as block:

            @block.sync
            def _(sp):

                def load(n, l):
                    sp.dma_start(xt[:, l, :], x1_dram[bass.ds(n * (R * P) + l * P, P), :]).then_inc(x_in[l], 16)

                for l in range(R):
                    load(NB // R, l)
                with sp.Fori(NB // R + 1, NT // R) as n:
                    for l in range(R):
                        sp.wait_ge(sum_done, n * R + l + 1)
                        load(n, l)

            @block.gpsimd
            def _(pool):
                with pool.Fori(0, NT // R) as n:
                    for l in range(R):
                        k = n * R + l
                        pool.wait_ge(both_done, k + 1)
                        apart(pool, m.passed)
                        nc.gpsimd.tensor_copy(where[:, l:l + 1, :], slots[:, bass.ds(k, 1), :]).then_inc(where_done, 1)
                        nc.gpsimd.tensor_copy(weight[:, l, :].unsqueeze(2), gates[:, :, bass.ds(k, 1)]).then_inc(weight_done, 1)
                        pool.wait_ge(where_done, k + 1)
                        apart(pool, m.passed)
                        for j in range(2):
                            pool.indirect_dma_start(y[:, l, j, :], None, y_dram,
                                                    bass.IndirectOffsetOnAxis(ap=where[:, l, j:j + 1], axis=0),
                                                    bounds_check=ROWS - 1, oob_is_err=False).then_inc(y_in[l], 16)

            @block.vector
            def _(dve):
                dve.sem_inc(both_done, R)
                dve.sem_inc(sum_done, R)
                dve.wait_ge(first_in, NB * 16)
                for b in range(B):
                    with dve.Fori(b * (NB // R), (b + 1) * (NB // R)) as n:
                        for l in range(R):
                            k = n * R + l
                            dve.wait_ge(first_done, k + 1)
                            nc.vector.scalar_tensor_tensor(out=acc[:, l, :], in0=y[:, l, 1, :], scalar=weight[:, l, 1:2],
                                                           in1=acc[:, l, :], op0=ALU.mult, op1=ALU.add).then_inc(both_done, 1)
                            dve.wait_ge(both_done, R + k + 1)
                            nc.vector.tensor_tensor(acc[:, l, :], acc[:, l, :], rows_bc[:, b, GB, :],
                                                    ALU.mult).then_inc(scaled, 1)
                            dve.wait_ge(scaled, k + 1)
                            if b == 0:
                                rest = x1_first[:, bass.ds(k, 1), :].rearrange("p o n -> p (o n)")
                            else:
                                rest = xt[:, l, :]
                                dve.wait_ge(x_in[l], (n - NB // R + 1) * 16)
                            nc.vector.tensor_tensor(acc[:, l, :], acc[:, l, :], rest, ALU.add).then_inc(sum_done, 1)

            @block.scalar
            def _(act):
                for l in range(R):
                    act.sem_inc(out_done[l], 16)

                def weigh(n, l):
                    act.wait_ge(y_in[l], (n + 1) * 32)
                    act.wait_ge(weight_done, n * R + l + 1)
                    act.wait_ge(out_done[l], (n + 1) * 16)
                    nc.scalar.activation(acc[:, l, :], y[:, l, 0, :], ACT.Copy, scale=weight[:, l, 0:1])\
                      .then_inc(first_done, 1)

                def store(n, l):
                    act.wait_ge(sum_done, R + n * R + l + 1)
                    act.dma_start(out[bass.ds(n * (R * P) + l * P, P), :], acc[:, l, :]).then_inc(out_done[l], 16)

                def body(n, more):
                    for l in range(R):
                        if l + 2 < R:
                            weigh(n, l + 2)
                        elif more:
                            weigh(n + 1, l + 2 - R)
                        store(n, l)

                for l in range(2):
                    weigh(0, l)
                with act.Fori(0, NT // R - 1) as n:
                    body(n, True)
                body(NT // R - 1, False)
                for l in range(R):
                    act.wait_ge(out_done[l], 16 + NT // R * 16)


def build(nc, x, wq_t, wk_t, wv_t, wo_t, gate_w_t, gate_b, gate_bias, w1_t, b1, w2_t, b2, c_t, wmod,
          ident, before, experts, tile_start, slot_number, row_step, positions, dist, slopes, out):
    def scratch(name, shape):
        return nc.dram_tensor(name, shape, F32, kind="Internal").ap()

    mod_dram = scratch("mod_dram", (6, B, DM))
    q_dram = scratch("q_dram", (UNITS, 2, P, S))
    k_dram = scratch("k_dram", (B, 2, P, S))
    o_dram = scratch("o_dram", (UNITS, NB, P, P))
    x1_dram = scratch("x1_dram", (NT * P, DM))
    h2_dram = scratch("h2_dram", (NT * P, DM))
    y_dram = scratch("y_dram", (ROWS, DM))

    with ExitStack() as ctx:
        m = Mem(nc, ctx)
        rows_bc = m.sb("rows_bc", [P, B, 6, DM])
        with nc.sbuf_tensor("v_all", [P, NT, P], F32) as v_all:
            with ExitStack() as inner:
                w = Mem(nc, inner)
                wq = w.sb("p_wq", [P, C, DM])
                wk = w.sb("p_wk", [P, C, P])
                wv = w.sb("p_wv", [P, C, P])
                idn = w.sb("p_idn", [P, P])
                xt = w.sb("p_xt", [P, RX_P, DM])
                weights_in = w.sem("weights_in")
                rest_in = w.sem("rest_in")
                x_in = [w.sem(f"x_in{k}") for k in range(RX_P)]

                def fetch(sp):
                    for k in range(SUP):
                        sp.dma_start(xt[:, k, :], x[k * P:(k + 1) * P, :]).then_inc(x_in[k], 16)
                    sp.dma_start(idn[:], ident).then_inc(weights_in, 16)
                    for weight, src in ((wq, wq_t), (wk, wk_t), (wv, wv_t)):
                        sp.dma_start(weight[:], src.rearrange("(k p) n -> p k n", p=P)).then_inc(weights_in, 16)
                    for k in range(SUP, RX_P):
                        sp.dma_start(xt[:, k, :], x[k * P:(k + 1) * P, :]).then_inc(x_in[k], 16)

                modulation(nc, c_t, wmod, mod_dram, rows_bc, fetch, rest_in)
                projections(nc, x, xt, x_in, wq, wk, wv, idn, weights_in, rest_in, rows_bc, v_all, q_dram, k_dram)
            attention(nc, q_dram, k_dram, o_dram, dist, slopes, ident, v_all)
        top_v = m.sb("top_v", [P, NT, 2])
        top_i = m.sb("top_i", [P, NT, 2])
        gates = m.sb("gates", [P, 2, NT])
        slots = m.sb("slots", [P, NT, 2], U32)
        tile_expert = m.sb("tile_expert", [P, ST], I32)
        slot_token = m.sb("slot_token", [P, ST], U32)
        with ExitStack() as inner:
            w = Mem(nc, inner)
            w1 = w.sb("w1", [P, C, E * HF])
            w2 = w.sb("w2", [P, len(HC), E * DM])
            b1_bc = w.sb("b1_bc", [P, E * HF])
            b2_bc = w.sb("b2_bc", [P, E * DM])
            w_in = w.sem("experts_in")
            zero_set = w.sem("zero_set")

            def fetch_up(sp, n):
                sp.dma_start(w1[:, bass.ds(n, 1), :], w1_t[bass.ds(n * P, P), :].unsqueeze(1)).then_inc(w_in, 16)

            def fetch_down(sp):
                sp.dma_start(b1_bc[:], b1.partition_broadcast(P)).then_inc(w_in, 16)
                for c, (a, size) in enumerate(HC):
                    sp.dma_start(w2[0:size, c, :], w2_t[a:a + size, :]).then_inc(w_in, 16)
                sp.dma_start(b2_bc[:], b2.partition_broadcast(P)).then_inc(w_in, 16)

            weights_in = [(w_in, (C + len(HC) + 2) * 16), (zero_set, 1)]
            with nc.Block() as block:

                @block.vector
                def _(dve):
                    nc.vector.memset(w2[HC[-1][1]:P, len(HC) - 1, :], 0.0).then_inc(zero_set, 1)

            mix_and_gate(nc, x, o_dram, wo_t, gate_w_t, gate_b, gate_bias, ident, rows_bc, top_v, top_i,
                         x1_dram, h2_dram, fetch_up)
            route(nc, top_v, top_i, before, experts, tile_start, slot_number, row_step, positions, ident, gates,
                  slots, tile_expert, slot_token, fetch_down)
            x1_first = w.sb("x1_first", [P, NB, DM])
            first_in = w.sem("x1_first_in")

            def fetch_residual(sp):
                for k in range(NB):
                    sp.dma_start(x1_first[:, k, :], x1_dram[k * P:(k + 1) * P, :]).then_inc(first_in, 16)

            run_experts(nc, ident, w1, w2, b1_bc, b2_bc, weights_in, tile_expert, slot_token, h2_dram, y_dram,
                        fetch_residual)
            combine(nc, rows_bc, gates, slots, x1_first, first_in, b2_bc, x1_dram, y_dram, out)


def kernel(L0_attn_x, L0_attn_Wq, L0_attn_Wk, L0_attn_Wv, L0_attn_Wo, L0_ffn_gate_w, L0_ffn_gate_b, L0_ffn_bias,
           L0_ffn_w1, L0_ffn_b1, L0_ffn_w2, L0_ffn_b2, L0_c, L0_wmod):
    import concourse.bacc as bacc
    from concourse.bass_utils import run_bass_kernel_spmd

    def t(a):
        return np.ascontiguousarray(np.asarray(a).T)

    p = np.arange(P)[:, None]
    y = np.arange(S)[None, :]
    d = p + (NB - 1) * P - y
    dist = np.where(d >= 0, np.sqrt(np.maximum(d, 0).astype(np.float32)), np.float32(1e32)).astype(np.float32)
    slope = ((2.0 ** (-8.0 / H)) ** np.arange(1, H + 1)).astype(np.float32)
    slopes = np.broadcast_to(np.tile(slope, B), (P, UNITS * REP)).copy()
    first = np.tile(np.arange(NT) * P, E)
    step = np.diff(first, prepend=0).astype(np.float32)
    ins = {
        "x": np.asarray(L0_attn_x).reshape(NT * P, DM),
        "wq_t": t(L0_attn_Wq), "wk_t": t(L0_attn_Wk), "wv_t": t(L0_attn_Wv), "wo_t": t(L0_attn_Wo),
        "gate_w_t": t(L0_ffn_gate_w), "gate_b": np.asarray(L0_ffn_gate_b), "gate_bias": np.asarray(L0_ffn_bias),
        "w1_t": t(np.asarray(L0_ffn_w1).reshape(E * HF, DM)),
        "b1": np.asarray(L0_ffn_b1).reshape(E * HF),
        "w2_t": np.ascontiguousarray(np.asarray(L0_ffn_w2).transpose(2, 0, 1)).reshape(HF, E * DM),
        "b2": np.asarray(L0_ffn_b2).reshape(E * DM),
        "c_t": t(L0_c), "wmod": np.asarray(L0_wmod),
        "ident": np.eye(P, dtype=np.float32),
        "before": np.triu(np.ones((P, P), np.float32), 1),
        "experts": np.broadcast_to(np.arange(E, dtype=np.float32), (P, NT, E)).copy(),
        "tile_start": np.broadcast_to(np.arange(ST, dtype=np.float32) * P, (P, ST)).copy(),
        "slot_number": (p + np.arange(ST)[None, :] * P).astype(np.float32),
        "row_step": np.ascontiguousarray(step.reshape(-1, P).T),
        "positions": np.broadcast_to(np.arange(3 * P, dtype=np.float32), (P, 3 * P)).copy(),
        "dist": dist, "slopes": slopes,
    }
    nc = bacc.Bacc("TRN2", target_bir_lowering=False, num_devices=1)
    args = {n: nc.dram_tensor(n, a.shape, mybir.dt.from_np(a.dtype), kind="ExternalInput").ap() for n, a in ins.items()}
    out = nc.dram_tensor("out", (NT * P, DM), F32, kind="ExternalOutput").ap()
    build(nc, out=out, **args)
    r = run_bass_kernel_spmd(nc, [ins], core_ids=[0])
    return r.results[0]["out"].reshape(B, S, DM)
```
